# Optimizing a Trainium2 kernel written in Bass

```python
import numpy as np
import jax
import jax.numpy as jnp

def _softmax(x, axis=-1):
    return jax.nn.softmax(x, axis=axis)

def _gelu(x):
    return jax.nn.gelu(x, approximate=True)

def _silu(x):
    return jax.nn.silu(x)

def _sigmoid(x):
    return jax.nn.sigmoid(x)

def _layernorm(x, axis=-1, eps=1e-05):
    m = jnp.mean(x, axis=axis, keepdims=True)
    v = jnp.var(x, axis=axis, keepdims=True)
    return (x - m) / jnp.sqrt(v + eps)

def _scatter_add(tgt, idx, src, axis=0):
    return tgt.at[idx].add(src)

def _segment_sum(src, seg, n):
    return jax.ops.segment_sum(src, seg, n)
kernel_name = 'mk_seq_preln_d2_jaxref_r8_466292'

def setup_inputs(seed: int=0):
    np.random.seed(seed)
    _w = jnp.asarray

    def _L0_attn_setup():
        import jax, jax.numpy as jnp
        import numpy as np
        import math
        H = 16
        DN = 128
        DR = 64
        DV = 128
        Q_LORA = 192
        KV_LORA = 64
        EPS = 1e-06
        ROPE_BASE = 10000.0
        YARN_FACTOR = 16.0
        ORIG_MAX = 1024

        def rmsnorm(x, w):
            return x * jax.lax.rsqrt(jnp.mean(x * x, axis=-1, keepdims=True) + EPS) * w

        def rotate_half(x):
            h = x.shape[-1] // 2
            return jnp.concatenate([-x[..., h:], x[..., :h]], axis=-1)

        def yarn_cos_sin(L, dtype):
            pos2 = jnp.arange(0, DR, 2, dtype=jnp.float32)
            inv_freq = 1.0 / ROPE_BASE ** (pos2 / DR)
            wavelen = 2.0 * jnp.pi / inv_freq
            ramp = jnp.clip((ORIG_MAX / wavelen - 1.0) / (4.0 - 1.0), 0.0, 1.0)
            inv_freq = inv_freq * (1.0 - ramp) + inv_freq / YARN_FACTOR * ramp
            t = jnp.arange(L, dtype=jnp.float32)
            freqs = jnp.outer(t, inv_freq)
            emb = jnp.concatenate([freqs, freqs], axis=-1)
            attn_factor = 0.1 * math.log(YARN_FACTOR) + 1.0
            cos = (jnp.cos(emb) * attn_factor)[None, :, None, :].astype(dtype)
            sin = (jnp.sin(emb) * attn_factor)[None, :, None, :].astype(dtype)
            return (cos, sin)
        key = jax.random.key(seed)
        ks = jax.random.split(key, 8)
        s = 0.02
        hid = 256
        return {'x': jax.random.normal(ks[0], (2, 256, hid), jnp.float32), 'w_qa': jax.random.normal(ks[1], (hid, Q_LORA), jnp.float32) * s, 'q_norm_w': jnp.ones((Q_LORA,), jnp.float32), 'w_qb': jax.random.normal(ks[2], (Q_LORA, H * (DN + DR)), jnp.float32) * s, 'w_kva': jax.random.normal(ks[3], (hid, KV_LORA + DR), jnp.float32) * s, 'kv_norm_w': jnp.ones((KV_LORA,), jnp.float32), 'w_kvb': jax.random.normal(ks[4], (KV_LORA, H * (DN + DV)), jnp.float32) * s, 'w_o': jax.random.normal(ks[5], (H * DV, hid), jnp.float32) * s}
    _L0_attn_in = _L0_attn_setup()

    def _L0_ffn_setup():
        import jax, jax.numpy as jnp
        import numpy as np
        B, S, H = (2, 64, 256)
        E, I, K = (64, 176, 6)
        NS = 2
        SH_I = I * NS
        key = jax.random.key(seed)
        ks = jax.random.split(key, 6)
        s = 0.02
        return {'hidden_states': jax.random.normal(ks[0], (B, S, H), jnp.float32), 'gate_w': jax.random.normal(ks[1], (E, H), jnp.float32) * s, 'experts_w1': jax.random.normal(ks[2], (E, I, H), jnp.float32) * s, 'experts_w2': jax.random.normal(ks[3], (E, H, I), jnp.float32) * s, 'shared_gate_up': jax.random.normal(ks[4], (2 * SH_I, H), jnp.float32) * s, 'shared_down': jax.random.normal(ks[5], (H, SH_I), jnp.float32) * s}
    _L0_ffn_in = _L0_ffn_setup()

    def _L1_attn_setup():
        import jax, jax.numpy as jnp
        import numpy as np
        import math
        DIM = 256
        D_STATE = 64
        EXPAND = 2
        CHUNK = 64
        HEADDIM = 64
        D_CONV = 4
        D_INNER = EXPAND * DIM
        NHEADS = D_INNER // HEADDIM

        def _segsum(x):
            T = x.shape[-1]
            keep = jnp.tril(jnp.ones((T, T), bool), -1)
            seg = jnp.cumsum(jnp.where(keep, x[..., None], 0.0), axis=-2)
            valid = jnp.tril(jnp.ones((T, T), bool))
            return jnp.where(valid, seg, -jnp.inf)

        def _ssd(X, A, B, C, block):
            b, L, h, p = X.shape
            n = B.shape[-1]
            c = L // block
            X = X.reshape(b, c, block, h, p)
            A = A.reshape(b, c, block, h)
            B = B.reshape(b, c, block, h, n)
            C = C.reshape(b, c, block, h, n)
            A = jnp.transpose(A, (0, 3, 1, 2))
            A_cum = jnp.cumsum(A, axis=-1)
            L_intra = jnp.exp(_segsum(A))
            Y_diag = jnp.einsum('bclhn,bcshn,bhcls,bcshp->bclhp', C, B, L_intra, X)
            decay_states = jnp.exp(A_cum[..., -1:] - A_cum)
            states = jnp.einsum('bclhn,bhcl,bclhp->bchpn', B, decay_states, X)
            states = jnp.concatenate([jnp.zeros_like(states[:, :1]), states], axis=1)
            chunk_end = jnp.pad(A_cum[..., -1], ((0, 0), (0, 0), (1, 0)))
            decay_chunk = jnp.exp(_segsum(chunk_end))
            new_states = jnp.einsum('bhzc,bchpn->bzhpn', decay_chunk, states)
            states_per_chunk = new_states[:, :-1]
            state_decay_out = jnp.exp(A_cum)
            Y_off = jnp.einsum('bclhn,bchpn,bhcl->bclhp', C, states_per_chunk, state_decay_out)
            return (Y_diag + Y_off).reshape(b, L, h, p)
        key = jax.random.key(seed)
        ks = jax.random.split(key, 6)
        b, l = (2, 256)
        x = jax.random.normal(ks[0], (b, l, DIM), jnp.float32)
        proj_out = 2 * D_INNER + 2 * D_STATE + NHEADS
        in_proj_w = jax.random.normal(ks[1], (proj_out, DIM), jnp.float32) / math.sqrt(DIM)
        conv_w = jax.random.normal(ks[2], (D_INNER, 1, D_CONV), jnp.float32) / math.sqrt(D_CONV)
        conv_b = jnp.zeros((D_INNER,), jnp.float32)
        out_proj_w = jax.random.normal(ks[3], (DIM, D_INNER), jnp.float32) / math.sqrt(D_INNER)
        A_log = jnp.zeros((NHEADS,), jnp.float32)
        D_skip = jnp.ones((D_INNER,), jnp.float32)
        u = jax.random.uniform(ks[4], (NHEADS,), jnp.float32)
        dt = jnp.clip(jnp.exp(u * (math.log(0.1) - math.log(0.001)) + math.log(0.001)), 0.0001, None)
        dt_bias = dt + jnp.log(-jnp.expm1(-dt))
        return dict(x=x, in_proj_w=in_proj_w, conv_w=conv_w, conv_b=conv_b, out_proj_w=out_proj_w, A_log=A_log, D_skip=D_skip, dt_bias=dt_bias)
    _L1_attn_in = _L1_attn_setup()

    def _L1_ffn_setup():
        import jax, jax.numpy as jnp
        import numpy as np
        HIDDEN = 256
        INTER = 704
        B, S = (2, 256)

        def _ternary(key, shape):
            return jax.random.randint(key, shape, -1, 2).astype(jnp.float32)
        key = jax.random.key(seed)
        ks = jax.random.split(key, 7)
        x = jax.random.normal(ks[0], (B, S, HIDDEN), dtype=jnp.float32)
        gate_w = _ternary(ks[1], (INTER, HIDDEN))
        up_w = _ternary(ks[2], (INTER, HIDDEN))
        down_w = _ternary(ks[3], (HIDDEN, INTER))
        gate_s = jax.random.uniform(ks[4], (INTER,), minval=0.01, maxval=0.1, dtype=jnp.float32)
        up_s = jax.random.uniform(ks[5], (INTER,), minval=0.01, maxval=0.1, dtype=jnp.float32)
        down_s = jax.random.uniform(ks[6], (HIDDEN,), minval=0.01, maxval=0.1, dtype=jnp.float32)
        return {'x': x, 'gate_w': gate_w, 'up_w': up_w, 'down_w': down_w, 'gate_s': gate_s, 'up_s': up_s, 'down_s': down_s}
    _L1_ffn_in = _L1_ffn_setup()
    _d = {'L0_attn_x': _L0_attn_in['x'], 'L0_attn_w_qa': _L0_attn_in['w_qa'], 'L0_attn_q_norm_w': _L0_attn_in['q_norm_w'], 'L0_attn_w_qb': _L0_attn_in['w_qb'], 'L0_attn_w_kva': _L0_attn_in['w_kva'], 'L0_attn_kv_norm_w': _L0_attn_in['kv_norm_w'], 'L0_attn_w_kvb': _L0_attn_in['w_kvb'], 'L0_attn_w_o': _L0_attn_in['w_o'], 'L0_ffn_gate_w': _L0_ffn_in['gate_w'], 'L0_ffn_experts_w1': _L0_ffn_in['experts_w1'], 'L0_ffn_experts_w2': _L0_ffn_in['experts_w2'], 'L0_ffn_shared_gate_up': _L0_ffn_in['shared_gate_up'], 'L0_ffn_shared_down': _L0_ffn_in['shared_down'], 'L1_attn_in_proj_w': _L1_attn_in['in_proj_w'], 'L1_attn_conv_w': _L1_attn_in['conv_w'], 'L1_attn_conv_b': _L1_attn_in['conv_b'], 'L1_attn_out_proj_w': _L1_attn_in['out_proj_w'], 'L1_attn_A_log': _L1_attn_in['A_log'], 'L1_attn_D_skip': _L1_attn_in['D_skip'], 'L1_attn_dt_bias': _L1_attn_in['dt_bias'], 'L1_ffn_gate_w': _L1_ffn_in['gate_w'], 'L1_ffn_up_w': _L1_ffn_in['up_w'], 'L1_ffn_down_w': _L1_ffn_in['down_w'], 'L1_ffn_gate_s': _L1_ffn_in['gate_s'], 'L1_ffn_up_s': _L1_ffn_in['up_s'], 'L1_ffn_down_s': _L1_ffn_in['down_s']}
    _x0 = _d['L0_attn_x']
    _d['L0_attn_x'] = jax.random.normal(jax.random.fold_in(jax.random.key(seed), 1), (4, 512, 256), dtype=_x0.dtype)
    del _x0
    return _d

def reference(L0_attn_x, L0_attn_w_qa, L0_attn_q_norm_w, L0_attn_w_qb, L0_attn_w_kva, L0_attn_kv_norm_w, L0_attn_w_kvb, L0_attn_w_o, L0_ffn_gate_w, L0_ffn_experts_w1, L0_ffn_experts_w2, L0_ffn_shared_gate_up, L0_ffn_shared_down, L1_attn_in_proj_w, L1_attn_conv_w, L1_attn_conv_b, L1_attn_out_proj_w, L1_attn_A_log, L1_attn_D_skip, L1_attn_dt_bias, L1_ffn_gate_w, L1_ffn_up_w, L1_ffn_down_w, L1_ffn_gate_s, L1_ffn_up_s, L1_ffn_down_s):

    def _L0_attn_ref(x, w_qa, q_norm_w, w_qb, w_kva, kv_norm_w, w_kvb, w_o):
        import jax, jax.numpy as jnp
        import numpy as np
        import math
        H = 16
        DN = 128
        DR = 64
        DV = 128
        Q_LORA = 192
        KV_LORA = 64
        EPS = 1e-06
        ROPE_BASE = 10000.0
        YARN_FACTOR = 16.0
        ORIG_MAX = 1024

        def rmsnorm(x, w):
            return x * jax.lax.rsqrt(jnp.mean(x * x, axis=-1, keepdims=True) + EPS) * w

        def rotate_half(x):
            h = x.shape[-1] // 2
            return jnp.concatenate([-x[..., h:], x[..., :h]], axis=-1)

        def yarn_cos_sin(L, dtype):
            pos2 = jnp.arange(0, DR, 2, dtype=jnp.float32)
            inv_freq = 1.0 / ROPE_BASE ** (pos2 / DR)
            wavelen = 2.0 * jnp.pi / inv_freq
            ramp = jnp.clip((ORIG_MAX / wavelen - 1.0) / (4.0 - 1.0), 0.0, 1.0)
            inv_freq = inv_freq * (1.0 - ramp) + inv_freq / YARN_FACTOR * ramp
            t = jnp.arange(L, dtype=jnp.float32)
            freqs = jnp.outer(t, inv_freq)
            emb = jnp.concatenate([freqs, freqs], axis=-1)
            attn_factor = 0.1 * math.log(YARN_FACTOR) + 1.0
            cos = (jnp.cos(emb) * attn_factor)[None, :, None, :].astype(dtype)
            sin = (jnp.sin(emb) * attn_factor)[None, :, None, :].astype(dtype)
            return (cos, sin)
        B, L, _ = x.shape
        q = rmsnorm(x @ w_qa, q_norm_w) @ w_qb
        q = q.reshape(B, L, H, DN + DR)
        q_nope, q_rope = (q[..., :DN], q[..., DN:])
        kv = x @ w_kva
        kv_c, k_rope = (kv[..., :KV_LORA], kv[..., KV_LORA:])
        kv = rmsnorm(kv_c, kv_norm_w) @ w_kvb
        kv = kv.reshape(B, L, H, DN + DV)
        k_nope, v = (kv[..., :DN], kv[..., DN:])
        k_rope = jnp.broadcast_to(k_rope[:, :, None, :], (B, L, H, DR))
        cos, sin = yarn_cos_sin(L, x.dtype)
        q_rope = q_rope * cos + rotate_half(q_rope) * sin
        k_rope = k_rope * cos + rotate_half(k_rope) * sin
        q = jnp.concatenate([q_nope, q_rope], axis=-1)
        k = jnp.concatenate([k_nope, k_rope], axis=-1)
        scale = 1.0 / math.sqrt(DN + DR)
        scores = jnp.einsum('blhd,bmhd->bhlm', q, k) * scale
        mask = jnp.tril(jnp.ones((L, L), bool))
        scores = jnp.where(mask[None, None], scores, jnp.array(-1e+30, scores.dtype))
        attn = jax.nn.softmax(scores, axis=-1)
        out = jnp.einsum('bhlm,bmhd->blhd', attn, v)
        return out.reshape(B, L, H * DV) @ w_o

    def _L0_ffn_ref(hidden_states, gate_w, experts_w1, experts_w2, shared_gate_up, shared_down):
        import jax, jax.numpy as jnp
        import numpy as np
        B, S, H = (2, 64, 256)
        E, I, K = (64, 176, 6)
        NS = 2
        SH_I = I * NS
        orig_shape = hidden_states.shape
        x = hidden_states.reshape(-1, orig_shape[-1])
        router_logits = x @ gate_w.T
        probs = jax.nn.softmax(router_logits, axis=-1)
        topk_w, topk_idx = jax.lax.top_k(probs, K)
        topk_w = topk_w / jnp.sum(topk_w, axis=-1, keepdims=True)
        combine = jnp.sum(jax.nn.one_hot(topk_idx, E, dtype=x.dtype) * topk_w[..., None], axis=1)
        h = jax.nn.silu(jnp.einsum('th,eih->tei', x, experts_w1))
        y = jnp.einsum('tei,ehi->teh', h, experts_w2)
        routed_out = jnp.einsum('teh,te->th', y, combine)
        gu = x @ shared_gate_up.T
        g, u = jnp.split(gu, 2, axis=-1)
        shared_out = jax.nn.silu(g) * u @ shared_down.T
        return (routed_out + shared_out).reshape(orig_shape)

    def _L1_attn_ref(x, in_proj_w, conv_w, conv_b, out_proj_w, A_log, D_skip, dt_bias):
        import jax, jax.numpy as jnp
        import numpy as np
        import math
        DIM = 256
        D_STATE = 64
        EXPAND = 2
        CHUNK = 64
        HEADDIM = 64
        D_CONV = 4
        D_INNER = EXPAND * DIM
        NHEADS = D_INNER // HEADDIM

        def _segsum(x):
            T = x.shape[-1]
            keep = jnp.tril(jnp.ones((T, T), bool), -1)
            seg = jnp.cumsum(jnp.where(keep, x[..., None], 0.0), axis=-2)
            valid = jnp.tril(jnp.ones((T, T), bool))
            return jnp.where(valid, seg, -jnp.inf)

        def _ssd(X, A, B, C, block):
            b, L, h, p = X.shape
            n = B.shape[-1]
            c = L // block
            X = X.reshape(b, c, block, h, p)
            A = A.reshape(b, c, block, h)
            B = B.reshape(b, c, block, h, n)
            C = C.reshape(b, c, block, h, n)
            A = jnp.transpose(A, (0, 3, 1, 2))
            A_cum = jnp.cumsum(A, axis=-1)
            L_intra = jnp.exp(_segsum(A))
            Y_diag = jnp.einsum('bclhn,bcshn,bhcls,bcshp->bclhp', C, B, L_intra, X)
            decay_states = jnp.exp(A_cum[..., -1:] - A_cum)
            states = jnp.einsum('bclhn,bhcl,bclhp->bchpn', B, decay_states, X)
            states = jnp.concatenate([jnp.zeros_like(states[:, :1]), states], axis=1)
            chunk_end = jnp.pad(A_cum[..., -1], ((0, 0), (0, 0), (1, 0)))
            decay_chunk = jnp.exp(_segsum(chunk_end))
            new_states = jnp.einsum('bhzc,bchpn->bzhpn', decay_chunk, states)
            states_per_chunk = new_states[:, :-1]
            state_decay_out = jnp.exp(A_cum)
            Y_off = jnp.einsum('bclhn,bchpn,bhcl->bclhp', C, states_per_chunk, state_decay_out)
            return (Y_diag + Y_off).reshape(b, L, h, p)
        b, l, _ = x.shape
        proj = x @ in_proj_w.T
        splits = [D_INNER, 2 * D_INNER, 2 * D_INNER + D_STATE, 2 * D_INNER + 2 * D_STATE]
        x_branch, z, B_in, C_in, dt = jnp.split(proj, splits, axis=-1)
        xc = jnp.transpose(x_branch, (0, 2, 1))
        xc = jax.lax.conv_general_dilated(xc, conv_w, (1,), [(D_CONV - 1, 0)], dimension_numbers=('NCH', 'OIH', 'NCH'), feature_group_count=D_INNER)
        xc = xc + conv_b[None, :, None]
        x_act = jax.nn.silu(jnp.transpose(xc, (0, 2, 1)))
        x_h = x_act.reshape(b, l, NHEADS, HEADDIM)
        dt_f = jax.nn.softplus(dt + dt_bias)
        A_f = -jnp.exp(A_log)
        X_disc = x_h * dt_f[..., None]
        A_disc = A_f[None, None, :] * dt_f
        B_b = jnp.broadcast_to(B_in[:, :, None, :], (b, l, NHEADS, D_STATE))
        C_b = jnp.broadcast_to(C_in[:, :, None, :], (b, l, NHEADS, D_STATE))
        Y = _ssd(X_disc, A_disc, B_b, C_b, CHUNK)
        y = Y.reshape(b, l, D_INNER) + D_skip * x_act
        y = y * jax.nn.silu(z)
        return y @ out_proj_w.T

    def _L1_ffn_ref(x, gate_w, up_w, down_w, gate_s, up_s, down_s):
        import jax, jax.numpy as jnp
        import numpy as np
        HIDDEN = 256
        INTER = 704
        B, S = (2, 256)

        def _ternary(key, shape):
            return jax.random.randint(key, shape, -1, 2).astype(jnp.float32)
        b, s, h = x.shape
        xf = x.reshape(b * s, h)
        g = jnp.einsum('th,ih->ti', xf, gate_w) * gate_s
        u = jnp.einsum('th,ih->ti', xf, up_w) * up_s
        hdn = jax.nn.silu(g) * u
        out = jnp.einsum('ti,hi->th', hdn, down_w) * down_s
        return out.reshape(b, s, -1)
    x = L0_attn_x
    x = x + _L0_attn_ref(_layernorm(x, axis=-1), L0_attn_w_qa, L0_attn_q_norm_w, L0_attn_w_qb, L0_attn_w_kva, L0_attn_kv_norm_w, L0_attn_w_kvb, L0_attn_w_o)
    x = x + _L0_ffn_ref(_layernorm(x, axis=-1), L0_ffn_gate_w, L0_ffn_experts_w1, L0_ffn_experts_w2, L0_ffn_shared_gate_up, L0_ffn_shared_down)
    x = x + _L1_attn_ref(_layernorm(x, axis=-1), L1_attn_in_proj_w, L1_attn_conv_w, L1_attn_conv_b, L1_attn_out_proj_w, L1_attn_A_log, L1_attn_D_skip, L1_attn_dt_bias)
    x = x + _L1_ffn_ref(_layernorm(x, axis=-1), L1_ffn_gate_w, L1_ffn_up_w, L1_ffn_down_w, L1_ffn_gate_s, L1_ffn_up_s, L1_ffn_down_s)
    return x

_drawn_inputs = setup_inputs


def setup_inputs(seed=0):
    import zlib

    import numpy as np

    out = dict(_drawn_inputs(seed))
    spreads = {'L0_attn_q_norm_w': (1.0, 0.6),
     'L0_attn_kv_norm_w': (1.0, 0.6),
     'L1_attn_conv_b': (0.0, 0.1),
     'L1_attn_A_log': (0.0, 0.1),
     'L1_attn_D_skip': (1.0, 0.6)}
    factors = {'L0_attn_w_qa': 8.0, 'L0_attn_w_qb': 8.0}
    for name, (base, spread) in spreads.items():
        noise = np.random.default_rng([zlib.crc32(name.encode()), seed]).standard_normal(out[name].shape)
        drawn = base * np.exp(spread * noise) if base else spread * noise
        out[name] = jnp.asarray(drawn.astype(out[name].dtype))
    for name, factor in factors.items():
        out[name] = (out[name] * factor).astype(out[name].dtype)
    return out
```

```python
import math
from contextlib import ExitStack

import numpy as np

import concourse.bass as bass
from concourse import mybir

F32 = mybir.dt.float32
BF16 = mybir.dt.bfloat16
ALU = mybir.AluOpType
ACT = mybir.ActivationFunctionType
AX = mybir.AxisListType

P = 128
BATCH, SEQ, DIM = 4, 512, 256
TOKENS = BATCH * SEQ
TILES = TOKENS // P
TB = SEQ // P
KC = DIM // P
HEADS, DN, DR, DV = 16, 128, 64, 128
QL, KVL = 192, 64
QL2 = QL - P
QE = KVL + DR
HG = 4
GROUPS = HEADS // HG
EXPERTS, EI, TOPK = 64, 176, 6
EH = EI // 2
SHI = 352
SH_CHUNKS = [(0, 128), (128, 128), (256, 96)]
DIN, DST, NH, HD, TAPS = 512, 64, 8, 64, 4
CH = DIN // P
PROJ = 2 * DIN + 2 * DST + NH
BCD = 2 * DST + NH
INTER = 704
FF_CHUNKS = [(128 * i, min(128, INTER - 128 * i)) for i in range((INTER + 127) // 128)]
ATT_SCALE = 1.0 / math.sqrt(DN + DR)
RMS_EPS, LN_EPS = 1e-6, 1e-5
START = 1
LOW = -3e38


def build(nc, a, out):
    ctx = ExitStack()
    with ctx:
        def sb(name, shape, dt=F32):
            return ctx.enter_context(nc.sbuf_tensor(name, shape, dt))

        def sem(name):
            return ctx.enter_context(nc.semaphore(name))

        x = sb("x", [P, TILES, DIM])
        xnT = sb("xnT", [P, KC, TOKENS])
        tables = sb("tables", [P, 4 * P + TB * DR * 2 + 2 * SEQ])
        ident = tables[:, 0:P]
        future = tables[:, P:2 * P]
        le = tables[:, 2 * P:3 * P]
        gt = tables[:, 3 * P:4 * P]
        o = 4 * P
        cosq = tables[:, o:o + TB * DR].rearrange("p (i d) -> p i d", i=TB)
        sinq = tables[:, o + TB * DR:o + 2 * TB * DR].rearrange("p (i d) -> p i d", i=TB)
        o += 2 * TB * DR
        cosk = tables[:, o:o + SEQ]
        sink = tables[:, o + SEQ:o + 2 * SEQ]
        ones = sb("ones", [P, P])
        identb = sb("identb", [P, P], BF16)
        futureb = sb("futureb", [P, P], BF16)
        stats = sb("stats", [P, TILES, 6])
        mv = sb("mv", [P, TILES, 2])
        rstd = sb("rstd", [P, TILES])
        rvar = sb("rvar", [P, TILES])

        w_a = sb("w_a", [P, KC, 3 * P])
        qn1 = sb("qn1", [P, 1])
        qn2 = sb("qn2", [QL2, 1])
        kvn = sb("kvn", [KVL, 1])
        wvo = sb("wvo", [P, HEADS // 2, DIM])
        gateT = sb("gateT", [P, KC, EXPERTS])
        sguT = sb("sguT", [P, KC, 2 * SHI])
        sdT = sb("sdT", [P, 3, DIM])
        w_in = sb("w_in", [P, KC, PROJ])
        conv_w = sb("conv_w", [P, CH, TAPS])
        conv_b = sb("conv_b", [P, CH])
        w_out = sb("w_out", [P, CH, DIM])
        a_neg = sb("a_neg", [P, NH])
        a_log = sb("a_log", [P, NH])
        dt_bias = sb("dt_bias", [P, NH])
        dskip = sb("dskip", [P, DIN])
        fgT = sb("fgT", [P, KC, INTER])
        fuT = sb("fuT", [P, KC, INTER])
        fdT = sb("fdT", [P, len(FF_CHUNKS), DIM])
        gate_s = sb("gate_s", [P, len(FF_CHUNKS)])
        up_s = sb("up_s", [P, len(FF_CHUNKS)])
        down_s = sb("down_s", [P, DIM])

        r1 = sb("r1", [P, 9216])
        r2 = sb("r2", [P, 12288])

        def carve(arena, at, shape, parts=P):
            n = int(np.prod(shape))
            ap = arena[0:parts, at:at + n]
            if len(shape) == 2:
                ap = ap.rearrange("p (a b) -> p a b", a=shape[0])
            if len(shape) == 3:
                ap = ap.rearrange("p (a b c) -> p a b c", a=shape[0], b=shape[1])
            return ap, at + n

        wqbT, e = carve(r1, 0, (HEADS, QL))
        wkvT, e = carve(r1, e, (2, HEADS, KVL))
        w_o, e = carve(r1, e, (HEADS, DIM))
        xn, _ = carve(r1, 0, (TILES, DIM))
        O, e = carve(r1, 0, (TB, HEADS * KVL))
        QT, e = carve(r1, e, (HG, SEQ))
        prob, e = carve(r1, e, (3, SEQ))
        probT, e = carve(r1, e, (2, SEQ))
        wqe1, e = carve(r2, 0, (HEADS, QE))
        wqe2, e = carve(r2, e, (HEADS, QE), QL2)
        cq1, e = carve(r2, e, (SEQ,))
        cq2, e = carve(r2, e, (SEQ,), QL2)
        KT, e = carve(r2, e, (SEQ,))
        V, e = carve(r2, e, (TB, KVL))
        OT, _ = carve(r2, e, (2, HEADS // 2 * P))
        sq, e = carve(r2, e, (3, SEQ))
        rq, e = carve(r2, e, (SEQ,))
        rk, e = carve(r2, e, (SEQ,))
        krope, e = carve(r2, e, (2, SEQ))
        qs, e = carve(r2, e, (TB, HG * QE))
        qtmp, e = carve(r2, e, (2, HG * DR))
        lgs, e = carve(r2, 0, (TILES, EXPERTS + 2))
        taken, e = carve(r2, e, (TILES, EXPERTS))
        comb, e = carve(r2, e, (TILES, EXPERTS))
        top8, e = carve(r2, e, (TILES, 8))
        rsum, e = carve(r2, e, (TILES,))
        w1b, e = carve(r2, e, (2, KC * EI))
        w2b, e = carve(r2, e, (2, 2 * DIM), EH)
        hid, e = carve(r2, e, (2, 2 * SEQ))
        sgl, e = carve(r2, e, (3, SEQ))
        shid, e = carve(r2, e, (3, SEQ))
        xb, e = carve(r2, 0, (KC, SEQ))
        xpad, e = carve(r2, e, (CH, SEQ + TAPS - 1))
        cv, e = carve(r2, e, (CH, SEQ))
        zs, e = carve(r2, e, (TB, DIN))
        bcd, e = carve(r2, e, (TB, BCD))
        dts, e = carve(r2, e, (8, TB * NH))
        xact, e = carve(r1, 0, (CH, SEQ))
        xa, e = carve(r1, e, (TB, DIN))
        AU, e = carve(r1, e, (NH, P))
        LT, e = carve(r1, e, (NH * P,))
        Gm, e = carve(r1, e, (P,))
        es, e = carve(r1, e, (TB, 3 * NH))
        BCT, e = carve(r1, e, (2, P), DST)
        xdisc, e = carve(r1, e, (DIN,))
        xdec, e = carve(r1, e, (DIN,))
        state, e = carve(r2, 9600, (DIN,), DST)
        ya, e = carve(r2, e, (DIN,))
        yb, e = carve(r2, e, (DIN,))
        yT, e = carve(r2, e, (CH, P))
        fsl, e = carve(r2, 0, (2, SEQ))
        fu, e = carve(r2, e, (2, SEQ))
        fhid, e = carve(r2, e, (len(FF_CHUNKS), SEQ))
        fo, e = carve(r2, e, (2, DIM))

        negmax = sb("negmax", [P, 16])
        rowsum = sb("rowsum", [P, 16])
        rrow = sb("rrow", [P, 16])

        bank = [ctx.enter_context(nc.psum_tensor(f"bank{i}", [P, 512], F32)) for i in range(8)]

        passed = {k: sem(f"passed_{k}") for k in ("act", "dve", "pe", "pool", "sp")}
        loads = {k: sem(f"load_{k}") for k in ("x", "tables", "prep", "attn", "ffn0", "mamba", "ffn1", "consts")}
        stage_done = [sem(f"stage_done{i}") for i in range(9)]

        def hold(eng, who, s, value):
            eng.wait_ge(s, value).then_inc(passed[who], 1)

        def stage_end(eng, n):
            eng.drain().then_inc(stage_done[n], 1)

        def stage_start(eng, n, engines=4):
            if n:
                eng.wait_ge(stage_done[n - 1], engines)

        block = ctx.enter_context(nc.Block())

        n_load = {}

        def load(eng, key, dst, src):
            eng.dma_start(dst, src).then_inc(loads[key], 16)
            n_load[key] = n_load.get(key, 0) + 16

        def bcast(v, n):
            return v.rearrange("(o n) -> o n", o=1).broadcast_to([P, n])

        def issue_loads(sp):
            load(sp, "x", x[:], a["x"].rearrange("(t p) c -> p t c", p=P))
            load(sp, "tables", tables[:], a["tables"])
            load(sp, "prep", wqbT, a["w_qbT"])
            load(sp, "prep", wkvT, a["w_kvT"])
            load(sp, "prep", w_o, a["w_o"].rearrange("(h p) n -> p h n", p=P))
            load(sp, "attn", w_a[:], a["w_a"])
            load(sp, "attn", wqe1[:, :, KVL:QE], a["w_qr"][0:P])
            load(sp, "attn", wqe2[:, :, KVL:QE], a["w_qr"][P:QL])
            load(sp, "attn", qn1[:], a["q_norm"].rearrange("(p o) -> p o", o=1)[0:P])
            load(sp, "attn", qn2[:], a["q_norm"].rearrange("(p o) -> p o", o=1)[P:QL])
            load(sp, "attn", kvn[:], a["kv_norm"].rearrange("(p o) -> p o", o=1))
            load(sp, "ffn0", gateT[:], a["gateT"].rearrange("(k p) n -> p k n", p=P))
            load(sp, "ffn0", sguT[:], a["sguT"].rearrange("(k p) n -> p k n", p=P))
            for c, (lo, n) in enumerate(SH_CHUNKS):
                load(sp, "ffn0", sdT[0:n, c, :], a["sdT"][lo:lo + n, :])
            load(sp, "mamba", w_in[:], a["w_in"].rearrange("(k p) n -> p k n", p=P))
            load(sp, "mamba", conv_w[:], a["conv_w"].rearrange("(c p) t -> p c t", p=P))
            load(sp, "mamba", conv_b[:], a["conv_b"])
            load(sp, "mamba", w_out[:], a["w_out"].rearrange("(k p) n -> p k n", p=P))
            load(sp, "mamba", a_log[:], bcast(a["A_log"], NH))
            load(sp, "mamba", dt_bias[:], bcast(a["dt_bias"], NH))
            load(sp, "mamba", dskip[:], bcast(a["D_skip"], DIN))
            load(sp, "ffn1", fgT[:], a["fgT"].rearrange("(k p) n -> p k n", p=P))
            load(sp, "ffn1", fuT[:], a["fuT"].rearrange("(k p) n -> p k n", p=P))
            last = len(FF_CHUNKS) - 1
            n = FF_CHUNKS[last][1]
            load(sp, "ffn1", fdT[:, 0:last, :], a["fdT"][0:P * last, :].rearrange("(k p) n -> p k n", p=P))
            load(sp, "ffn1", fdT[0:n, last, :], a["fdT"][P * last:, :])
            for dst, src in ((gate_s, "gate_s"), (up_s, "up_s")):
                load(sp, "ffn1", dst[:], a[src])
            load(sp, "ffn1", down_s[:], bcast(a["down_s"], DIM))

        def loaded(eng, key):
            eng.wait_ge(loads[key], total_loads[key])

        total_loads = {"x": 16, "tables": 16, "prep": 48, "attn": 96, "ffn0": 80, "mamba": 112, "ffn1": 112}

        ln = {k: sem(f"ln_{k}") for k in ("stat", "var", "root", "xn", "tr")}

        def ln_vector(dve, n):
            for t in range(TILES):
                nc.vector.bn_stats(stats[:, t, :], x[:, t, :]).then_inc(ln["stat"], 1)
            for t in range(TILES):
                dve.wait_ge(ln["stat"], 2 * TILES * n + t + 1)
                nc.vector.bn_aggr(mv[:, t, :], stats[:, t, :]).then_inc(ln["stat"], 1)
            dve.wait_ge(ln["stat"], 2 * TILES * (n + 1))
            nc.vector.tensor_scalar(rvar[:], mv[:, :, 1], LN_EPS, None, ALU.add).then_inc(ln["var"], 1)
            dve.wait_ge(ln["var"], 2 * n + 1)
            nc.vector.reciprocal(rvar[:], rvar[:]).then_inc(ln["var"], 1)
            dve.wait_ge(ln["root"], n + 1)
            for t in range(TILES):
                nc.vector.tensor_scalar(xn[:, t, :], x[:, t, :], mv[:, t, 0:1], rstd[:, t:t + 1],
                                        ALU.subtract, ALU.mult).then_inc(ln["xn"], 1)
            for u in (1, 3, 5, 7):
                ln_evacuate(dve, nc.vector.tensor_copy, n, u)

        def ln_evacuate(eng, copy, n, u):
            eng.wait_ge(ln["tr"], 8 * n + u + 1)
            k, g = u % KC, u // KC
            copy(xnT[:, k, g * SEQ:(g + 1) * SEQ], bank[u][:])

        def ln_scalar(act, n):
            act.wait_ge(ln["var"], 2 * n + 2)
            nc.scalar.activation(rstd[:], rvar[:], ACT.Sqrt).then_inc(ln["root"], 1)
            for u in (0, 2, 4, 6):
                ln_evacuate(act, nc.scalar.copy, n, u)

        def ln_tensor(pe, n):
            for u in range(8):
                k, g = u % KC, u // KC
                pe.wait_ge(ln["xn"], TILES * n + TB * (g + 1))
                for i in range(TB):
                    last = nc.tensor.transpose(bank[u][:, i * P:(i + 1) * P],
                                               xn[:, TB * g + i, k * P:(k + 1) * P], ident)
                last.then_inc(ln["tr"], 1)

        prep_w = sem("prep_w")
        prep_ev = sem("prep_ev")
        consts = sem("consts")

        def prep_tensor(pe):
            loaded(pe, "prep")
            for h in range(HEADS):
                c = (h % 8) * KVL
                nc.tensor.matmul(bank[h // 8][:, c:c + KVL], wqbT[:, h, 0:P], wkvT[:, 0, h, :],
                                 start=True, stop=True)
                last = nc.tensor.matmul(bank[2 + h // 8][0:QL2, c:c + KVL], wqbT[:, h, P:QL], wkvT[:, 0, h, :],
                                        start=True, stop=True)
            last.then_inc(prep_w, 1)
            for h in range(HEADS):
                c = (h // 2 % 2) * DIM
                r = KVL * (h % 2)
                last = nc.tensor.matmul(bank[4 + h // 4][r:r + KVL, c:c + DIM], wkvT[:, 1, h, :], w_o[:, h, :],
                                        start=True, stop=True)
            last.then_inc(prep_w, 1)

        def prep_scalar(act):
            act.wait_ge(prep_w, 1)
            for m in range(2):
                for dst, b, n in ((wqe1, 0, P), (wqe2, 2, QL2)):
                    nc.scalar.copy(dst[:, 8 * m:8 * m + 8, 0:KVL],
                                   bank[b + m][0:n, :].rearrange("p (h c) -> p h c", h=8))
            act.wait_ge(prep_w, 2)
            for m in range(4):
                nc.scalar.copy(wvo[:, 2 * m:2 * m + 2, :], bank[4 + m][:].rearrange("p (h c) -> p h c", h=2))

        A = {k: sem(f"a_{k}") for k in
             ("proj", "sq", "ms", "veps", "rec", "root", "cq", "kr", "kv", "vt", "v",
              "q", "qs", "rope", "rope_a", "qt", "qte", "s", "max", "exp", "pt", "pte", "pv", "rr", "o",
              "ot", "ote", "y", "res")}
        NU = HG * TB

        def att_tensor(pe):
            with pe.Fori(0, BATCH) as b:
                tok = b * SEQ
                pe.wait_ge(A["res"], b * TB + START)
                for m in range(3):
                    for k in range(KC):
                        last = nc.tensor.matmul(bank[m][:], w_a[:, k, m * P:(m + 1) * P],
                                                xnT[:, k, bass.ds(tok, SEQ)], start=(k == 0), stop=(k == KC - 1))
                    last.then_inc(A["proj"], 1)
                pe.wait_ge(A["sq"], 3 * b + 3)
                nc.tensor.matmul(bank[3][:], ones[:], sq[:, 0, :], start=True, stop=False)
                nc.tensor.matmul(bank[3][:], ones[0:QL2, :], sq[0:QL2, 1, :], start=False, stop=True)
                nc.tensor.matmul(bank[4][:], ones[0:KVL, :], sq[0:KVL, 2, :], start=True, stop=True)\
                    .then_inc(A["ms"], 1)
                hold(pe, "pe", A["kv"], b + 1)
                for i in range(TB):
                    last = nc.tensor.transpose(bank[5][:, i * KVL:(i + 1) * KVL],
                                               KT[0:KVL, i * P:(i + 1) * P], ident[0:KVL, 0:KVL])
                last.then_inc(A["vt"], 1)
                pe.wait_ge(A["cq"], 2 * b + 2)
                for i in range(TB):
                    q_product(pe, b * GROUPS, 0, i)
                pe.wait_ge(A["kr"], b + 1)
                pe.wait_ge(A["v"], b + 1)
                for i in range(TB):
                    q_transpose(pe, b * GROUPS, i)
                with pe.Fori(0, GROUPS - 1) as hg:
                    group_tensor(pe, b * GROUPS + hg, hg, True)
                group_tensor(pe, b * GROUPS + (GROUPS - 1), GROUPS - 1, False)
                for i in range(TB):
                    if i == 0:
                        pe.wait_ge(A["o"], HEADS * b + HEADS)
                    for half in range(2):
                        hold(pe, "pe", A["ote"], 2 * TB * b + max(0, 2 * i + half - 1) + START)
                        for c in range(4):
                            cc = 4 * half + c
                            last = nc.tensor.transpose(bank[3 + half][:, c * P:(c + 1) * P],
                                                       O[:, i, cc * P:(cc + 1) * P], ident)
                        last.then_inc(A["ot"], 1)
                    pe.wait_ge(A["ote"], 2 * TB * b + 2 * i + 2 + START)
                    if i >= 2:
                        pe.wait_ge(A["res"], TB * b + i - 1 + START)
                    for c in range(HEADS // 2):
                        last = nc.tensor.matmul(bank[6 + i % 2][:, 0:DIM], OT[:, i % 2, c * P:(c + 1) * P],
                                                wvo[:, c, :], start=(c == 0), stop=(c == HEADS // 2 - 1))
                    last.then_inc(A["y"], 1)

        def q_product(pe, g, hg, i):
            pe.wait_ge(A["qs"], TB * g + i + START)
            w1 = wqe1[:, bass.ds(hg * HG, HG), :].rearrange("p h c -> p (h c)") if not isinstance(hg, int) \
                else wqe1[:, hg * HG:(hg + 1) * HG, :].rearrange("p h c -> p (h c)")
            w2 = wqe2[:, bass.ds(hg * HG, HG), :].rearrange("p h c -> p (h c)") if not isinstance(hg, int) \
                else wqe2[:, hg * HG:(hg + 1) * HG, :].rearrange("p h c -> p (h c)")
            nc.tensor.matmul(bank[7][:], cq1[:, i * P:(i + 1) * P], w1, start=True, stop=False)
            nc.tensor.matmul(bank[7][:], cq2[:, i * P:(i + 1) * P], w2, start=False, stop=True)\
                .then_inc(A["q"], 1)

        def q_transpose(pe, g, i):
            pe.wait_ge(A["rope"], TB * g + i + 1)
            hold(pe, "pe", A["qte"], TB * g + max(0, i - 1) + START)
            for h in range(HG):
                last = nc.tensor.transpose(bank[3 + i % 2][:, h * P:(h + 1) * P],
                                           qs[:, i, h * QE:(h + 1) * QE], ident)
            last.then_inc(A["qt"], 1)

        def group_tensor(pe, g, hg, with_next):
            pe.wait_ge(A["qte"], TB * g + TB + START)

            def scores(u):
                h, i = u // TB, u % TB
                if u >= 3:
                    pe.wait_ge(A["exp"], NU * g + u - 2)
                n = (i + 1) * P
                nc.tensor.matmul(bank[u % 3][:, 0:n], QT[:, h, i * P:(i + 1) * P], KT[:, 0:n],
                                 start=True, stop=False)
                nc.tensor.matmul(bank[u % 3][:, i * P:n], identb[:], futureb[:], start=False, stop=True)\
                    .then_inc(A["s"], 1)

            def transposes(u):
                i = u % TB
                pe.wait_ge(A["exp"], NU * g + u + 1)
                if u >= 2:
                    hold(pe, "pe", A["pte"], NU * g + u - 1)
                for j in range(i + 1):
                    last = nc.tensor.transpose(bank[3 + u % 2][:, j * P:(j + 1) * P],
                                               prob[:, u % 3, j * P:(j + 1) * P], ident)
                last.then_inc(A["pt"], 1)

            def values(u):
                h, i = u // TB, u % TB
                pe.wait_ge(A["pte"], NU * g + u + 1)
                if i == 0 and h >= 2:
                    hold(pe, "pe", A["o"], HG * g + h - 1)
                for j in range(i + 1):
                    last = nc.tensor.matmul(bank[5 + h % 2][:, i * KVL:(i + 1) * KVL],
                                            probT[:, u % 2, j * P:(j + 1) * P], V[:, j, :],
                                            start=(j == 0), stop=(j == i))
                last.then_inc(A["pv"], 1)

            for u in range(NU + 3):
                if u < NU:
                    scores(u)
                elif with_next:
                    q_product(pe, g + 1, hg + 1, u - NU)
                if 2 <= u < NU + 2:
                    transposes(u - 2)
                if u >= 3:
                    values(u - 3)
            if with_next:
                q_product(pe, g + 1, hg + 1, 3)
                for i in range(TB):
                    q_transpose(pe, g + 1, i)

        def att_scalar(act):
            with act.Fori(0, BATCH) as b:
                for m, n, width in ((0, P, QL), (1, QL2, QL), (2, KVL, KVL)):
                    act.wait_ge(A["proj"], 3 * b + m + 1)
                    nc.scalar.activation(sq[0:n, m, :], bank[m][0:n, :], ACT.Square,
                                         scale=1.0 / math.sqrt(width)).then_inc(A["sq"], 1)
                act.wait_ge(A["rec"], 2 * b + 1)
                nc.scalar.activation(rq, rq, ACT.Sqrt, scale=ATT_SCALE * ATT_SCALE).then_inc(A["root"], 1)
                act.wait_ge(A["rec"], 2 * b + 2)
                nc.scalar.activation(rk[0:KVL, :], rk[0:KVL, :], ACT.Sqrt).then_inc(A["root"], 1)
                act.wait_ge(A["vt"], b + 1)
                nc.scalar.copy(V.rearrange("p i c -> p (i c)"), bank[5][:, 0:TB * KVL]).then_inc(A["v"], 1)
                for i in range(TB):
                    q_copy(act, b * GROUPS, i)
                for i in range(TB):
                    qt_copy(act, b * GROUPS, i)
                with act.Fori(0, GROUPS - 1) as hg:
                    group_scalar(act, b * GROUPS + hg, True)
                group_scalar(act, b * GROUPS + (GROUPS - 1), False)
                for i in range(TB):
                    for half in range(2):
                        act.wait_ge(A["ot"], 2 * TB * b + 2 * i + half + 1)
                        if i >= 2:
                            act.wait_ge(A["y"], TB * b + i - 1)
                        nc.scalar.copy(OT[:, i % 2, 4 * half * P:4 * (half + 1) * P], bank[3 + half][:])\
                            .then_inc(A["ote"], 1)

        def q_copy(act, g, i):
            act.wait_ge(A["q"], TB * g + i + 1)
            nc.scalar.copy(qs[:, i, :], bank[7][:]).then_inc(A["qs"], 1)

        def qt_copy(act, g, i):
            act.wait_ge(A["qt"], TB * g + i + 1)
            nc.scalar.copy(QT[:, :, i * P:(i + 1) * P], bank[3 + i % 2][:].rearrange("p (h c) -> p h c", h=HG))\
                .then_inc(A["qte"], 1)

        def group_scalar(act, g, with_next):
            def exps(u):
                i = u % TB
                act.wait_ge(A["max"], NU * g + u + 1)
                if u >= 3:
                    act.wait_ge(A["pt"], NU * g + u - 2)
                nc.scalar.activation(prob[:, u % 3, 0:(i + 1) * P], bank[u % 3][:, 0:(i + 1) * P], ACT.Exp,
                                     bias=negmax[:, u:u + 1], scale=1.0,
                                     accum_out=rowsum[:, u:u + 1]).then_inc(A["exp"], 1)

            def evacuate(u):
                i = u % TB
                act.wait_ge(A["pt"], NU * g + u + 1)
                if u >= 2:
                    act.wait_ge(A["pv"], NU * g + u - 1)
                nc.scalar.copy(probT[:, u % 2, 0:(i + 1) * P], bank[3 + u % 2][:, 0:(i + 1) * P])\
                    .then_inc(A["pte"], 1)

            for u in range(NU + 2):
                if u < NU:
                    exps(u)
                if u >= 2:
                    evacuate(u - 2)
                if u >= NU and with_next:
                    q_copy(act, g + 1, u - NU)
            if with_next:
                for i in range(2, TB):
                    q_copy(act, g + 1, i)
                for i in range(TB):
                    qt_copy(act, g + 1, i)

        def att_vector(dve):
            with dve.Fori(0, BATCH) as b:
                for m, (dst, n) in enumerate(((rq, P), (rk, KVL))):
                    dve.wait_ge(A["ms"], b + 1)
                    nc.vector.tensor_scalar(dst[0:n, :], bank[3 + m][0:n, :], RMS_EPS, None, ALU.add)\
                        .then_inc(A["veps"], 1)
                    dve.wait_ge(A["veps"], 2 * b + m + 1)
                    nc.vector.reciprocal(dst[0:n, :], dst[0:n, :]).then_inc(A["rec"], 1)
                dve.wait_ge(A["proj"], 3 * b + 3)
                nc.vector.tensor_tensor(krope[KVL:QE, 0, :], bank[2][KVL:QE, :], cosk[KVL:QE, :], ALU.mult)\
                    .then_inc(A["rope_a"], 1)
                nc.vector.tensor_tensor(krope[KVL:QE, 1, :], bank[1][KVL:QE, :], sink[KVL:QE, :], ALU.mult)\
                    .then_inc(A["rope_a"], 1)
                dve.wait_ge(A["rope_a"], 2 * b + 2)
                nc.vector.tensor_tensor(KT[KVL:QE, :], krope[KVL:QE, 0, :], krope[KVL:QE, 1, :], ALU.add)\
                    .then_inc(A["kr"], 1)
                dve.wait_ge(A["root"], 2 * b + 2)
                nc.vector.scalar_tensor_tensor(out=KT[0:KVL, :], in0=bank[2][0:KVL, :], scalar=kvn[:],
                                               in1=rk[0:KVL, :], op0=ALU.mult, op1=ALU.mult).then_inc(A["kv"], 1)
                nc.vector.scalar_tensor_tensor(out=cq1, in0=bank[0][:], scalar=qn1[:], in1=rq,
                                               op0=ALU.mult, op1=ALU.mult).then_inc(A["cq"], 1)
                nc.vector.scalar_tensor_tensor(out=cq2, in0=bank[1][0:QL2, :], scalar=qn2[:], in1=rq[0:QL2, :],
                                               op0=ALU.mult, op1=ALU.mult).then_inc(A["cq"], 1)
                with dve.Fori(0, GROUPS - 1) as hg:
                    group_vector(dve, b * GROUPS + hg, hg)
                group_vector(dve, b * GROUPS + (GROUPS - 1), GROUPS - 1)
                for i in range(TB):
                    dve.wait_ge(A["y"], TB * b + i + 1)
                    xt = x[:, bass.ds(b * TB + i, 1), :].rearrange("p o c -> p (o c)")
                    nc.vector.tensor_tensor(xt, bank[6 + i % 2][:, 0:DIM], xt, ALU.add).then_inc(A["res"], 1)

        def group_vector(dve, g, hg):
            def maximum(u):
                i = u % TB
                dve.wait_ge(A["s"], NU * g + u + 1)
                nc.vector.tensor_reduce(negmax[:, u:u + 1], bank[u % 3][:, 0:(i + 1) * P], axis=AX.X,
                                        op=ALU.max, negate=True).then_inc(A["max"], 1)

            def head_out(h):
                hold(dve, "dve", A["exp"], NU * g + TB * (h + 1))
                nc.vector.reciprocal(rrow[:, TB * h:TB * (h + 1)], rowsum[:, TB * h:TB * (h + 1)])\
                    .then_inc(A["rr"], 1)
                dve.wait_ge(A["rr"], HG * g + h + 1)
                dve.wait_ge(A["pv"], NU * g + TB * (h + 1))
                col = (hg * HG + h) * KVL
                dst = O[:, :, bass.ds(col, KVL)] if not isinstance(col, int) else O[:, :, col:col + KVL]
                nc.vector.tensor_tensor(dst,
                                        bank[5 + h % 2][:, 0:TB * KVL].rearrange("p (i c) -> p i c", i=TB),
                                        rrow[:, TB * h:TB * (h + 1)].unsqueeze(2).to_broadcast([P, TB, KVL]),
                                        ALU.mult).then_inc(A["o"], 1)

            for u in range(NU + 4):
                if u < NU:
                    maximum(u)
                if u >= 7 and (u - 7) % TB == 0:
                    head_out((u - 7) // TB)

        def att_pool(pool):
            with pool.Fori(0, BATCH * GROUPS) as g:
                for i in range(TB):
                    q = qs[:, i, :].rearrange("p (h c) -> p h c", h=HG)
                    ta = qtmp[:, 0, :].rearrange("p (h c) -> p h c", h=HG)
                    tb = qtmp[:, 1, :].rearrange("p (h c) -> p h c", h=HG)
                    half = DR // 2
                    c = cosq[:, i, :].unsqueeze(1).to_broadcast([P, HG, DR])
                    s1 = sinq[:, i, 0:half].unsqueeze(1).to_broadcast([P, HG, half])
                    s2 = sinq[:, i, half:DR].unsqueeze(1).to_broadcast([P, HG, half])
                    hold(pool, "pool", A["qs"], TB * g + i + 1 + START)
                    nc.gpsimd.tensor_tensor(ta, q[:, :, KVL:QE], c, ALU.mult).then_inc(A["rope_a2"], 1)
                    nc.gpsimd.tensor_tensor(tb[:, :, 0:half], q[:, :, KVL + half:QE], s1, ALU.mult)\
                        .then_inc(A["rope_a2"], 1)
                    nc.gpsimd.tensor_tensor(tb[:, :, half:DR], q[:, :, KVL:KVL + half], s2, ALU.mult)\
                        .then_inc(A["rope_a2"], 1)
                    hold(pool, "pool", A["rope_a2"], 3 * TB * g + 3 * i + 3)
                    nc.gpsimd.tensor_tensor(q[:, :, KVL:QE], ta, tb, ALU.add).then_inc(A["rope"], 1)
                    hold(pool, "pool", A["rope"], TB * g + i + 1)

        A["rope_a2"] = sem("a_rope_parts")

        M = {k: sem(f"m_{k}") for k in
             ("lg", "lgs", "pad", "top", "top6", "rep", "sub", "exp", "sel", "sum", "rec", "comb",
              "up", "hid", "down", "acc", "sup", "ssil", "shid", "sdown", "sacc")}

        def route_tensor(pe):
            for t in range(TILES):
                for k in range(KC):
                    last = nc.tensor.matmul(bank[t // 8][:, (t % 8) * EXPERTS:(t % 8 + 1) * EXPERTS],
                                            xnT[:, k, t * P:(t + 1) * P], gateT[:, k, :],
                                            start=(k == 0), stop=(k == KC - 1))
            last.then_inc(M["lg"], 1)

        def route_vector(dve):
            nc.vector.memset(lgs[:, :, EXPERTS:EXPERTS + 2], -LOW).then_inc(M["pad"], 1)
            dve.wait_ge(M["lg"], 1)
            for m in range(2):
                nc.vector.tensor_copy(lgs[:, 8 * m:8 * m + 8, 0:EXPERTS],
                                      bank[m][:].rearrange("p (t e) -> p t e", t=8)).then_inc(M["lgs"], 1)
            dve.wait_ge(M["lgs"], 2)
            for t in range(TILES):
                nc.vector.max(top8[:, t, :], lgs[:, t, 0:EXPERTS]).then_inc(M["top"], 1)
            dve.wait_ge(M["top"], TILES)
            nc.vector.tensor_tensor(comb, lgs[:, :, 0:EXPERTS],
                                    top8[:, :, 0:1].to_broadcast([P, TILES, EXPERTS]), ALU.subtract)\
                .then_inc(M["sub"], 1)
            dve.wait_ge(M["sub"], 1)
            nc.vector.memset(top8[:, :, TOPK:8], -LOW).then_inc(M["top6"], 1)
            dve.wait_ge(M["top6"], 1)
            dve.wait_ge(M["pad"], 1)
            for t in range(TILES):
                nc.vector.match_replace(taken_pad[:, t, :], top8[:, t, :], lgs[:, t, :], LOW)\
                    .then_inc(M["rep"], 1)
            dve.wait_ge(M["rep"], TILES)
            dve.wait_ge(M["exp"], 1)
            nc.vector.scalar_tensor_tensor(out=taken, in0=taken_pad[:, :, 0:EXPERTS], scalar=0.9 * LOW,
                                           in1=comb, op0=ALU.is_lt, op1=ALU.mult).then_inc(M["sel"], 1)
            dve.wait_ge(M["sel"], 1)
            nc.vector.tensor_reduce(rsum, taken, axis=AX.X, op=ALU.add).then_inc(M["sum"], 1)
            dve.wait_ge(M["sum"], 1)
            nc.vector.reciprocal(rsum, rsum).then_inc(M["rec"], 1)
            dve.wait_ge(M["rec"], 1)
            nc.vector.tensor_tensor(comb, taken, rsum.unsqueeze(2).to_broadcast([P, TILES, EXPERTS]), ALU.mult)\
                .then_inc(M["comb"], 1)
            dve.wait_ge(M["comb"], 1)

        def route_scalar(act):
            act.wait_ge(M["sub"], 1)
            nc.scalar.activation(comb, comb, ACT.Exp).then_inc(M["exp"], 1)

        NE2 = EXPERTS // 2
        UG = 2 * TB
        DG = 2 * TB * TB

        def experts_sp(sp):
            with sp.Fori(0, NE2) as e2:
                for j in range(2):
                    sp.wait_ge(M["down"], DG * e2 + START)
                    sp.dma_start(w1b[:, j, :], a["w1T"][bass.ds(2 * e2 + j, 1), :, :]
                                 .rearrange("o p n -> p (o n)")).then_inc(W1S[j], 16)
                    sp.dma_start(w2b[:, j, :], a["w2T"][bass.ds(2 * e2 + j, 1), :, :]
                                 .rearrange("o p n -> p (o n)")).then_inc(W1S[j], 16)

        W1S = [sem(f"m_weights{j}") for j in range(2)]

        def experts_tensor(pe):
            pe.wait_ge(M["sacc"], TILES + START)
            with pe.Fori(0, NE2) as e2:
                def up(n):
                    j, g = n // TB, n % TB
                    if g == 0:
                        pe.wait_ge(W1S[j], 32 * e2 + 32)
                    for c in range(2):
                        if n >= 1:
                            pe.wait_ge(M["hid"], 2 * UG * e2 + 2 * (n - 1) + c + 1)
                        for k in range(KC):
                            last = nc.tensor.matmul(bank[c][0:EH, :],
                                                    w1b[:, j, k * EI + c * EH:k * EI + (c + 1) * EH],
                                                    xnT[:, k, g * SEQ:(g + 1) * SEQ],
                                                    start=(k == 0), stop=(k == KC - 1))
                        last.then_inc(M["up"], 1)

                def down(n):
                    j, g = n // TB, n % TB
                    pe.wait_ge(M["hid"], 2 * UG * e2 + 2 * n + 2)
                    for i in range(TB):
                        d = n * TB + i
                        if d >= 4:
                            pe.wait_ge(M["acc"], DG * e2 + d - 3 + START)
                        for c in range(2):
                            last = nc.tensor.matmul(bank[4 + d % 4][:, 0:DIM],
                                                    hid[0:EH, n % 2, c * SEQ + i * P:c * SEQ + (i + 1) * P],
                                                    w2b[:, j, c * DIM:(c + 1) * DIM],
                                                    start=(c == 0), stop=(c == 1))
                        last.then_inc(M["down"], 1)

                pe.wait_ge(M["acc"], DG * e2 + START)
                for n in range(UG + 1):
                    if n < UG:
                        up(n)
                    if n:
                        down(n - 1)

        def experts_scalar(act):
            with act.Fori(0, NE2) as e2:
                for n in range(UG):
                    for c in range(2):
                        act.wait_ge(M["up"], 2 * UG * e2 + 2 * n + c + 1)
                        if n >= 2 and c == 0:
                            act.wait_ge(M["down"], DG * e2 + TB * (n - 1) + START)
                        if n < 2 and c == 0:
                            act.wait_ge(M["down"], DG * e2 + START)
                        nc.scalar.activation(hid[0:EH, n % 2, c * SEQ:(c + 1) * SEQ], bank[c][0:EH, :], ACT.Silu)\
                            .then_inc(M["hid"], 1)

        def experts_vector(dve):
            dve.wait_ge(M["sacc"], TILES + START)
            with dve.Fori(0, NE2) as e2:
                for n in range(UG):
                    j, g = n // TB, n % TB
                    for i in range(TB):
                        d = n * TB + i
                        t = g * TB + i
                        dve.wait_ge(M["down"], DG * e2 + d + 1 + START)
                        dve.wait_ge(M["acc"], DG * e2 + max(0, d - TILES + 1) + START)
                        nc.vector.scalar_tensor_tensor(
                            out=x[:, t, :], in0=bank[4 + d % 4][:, 0:DIM], scalar=comb[:, t, bass.ds(2 * e2 + j, 1)],
                            in1=x[:, t, :], op0=ALU.mult, op1=ALU.add).then_inc(M["acc"], 1)

        def shared_tensor(pe):
            with pe.Fori(0, BATCH) as g:
                pe.wait_ge(M["sacc"], TB * g + START)
                n = 0
                for c, (lo, w) in enumerate(SH_CHUNKS):
                    for half in range(2):
                        for k in range(KC):
                            last = nc.tensor.matmul(bank[3 * half + c][0:w, :],
                                                    sguT[:, k, SHI * half + lo:SHI * half + lo + w],
                                                    xnT[:, k, bass.ds(g * SEQ, SEQ)],
                                                    start=(k == 0), stop=(k == KC - 1))
                        last.then_inc(M["sup"], 1)
                pe.wait_ge(M["shid"], 3 * g + 3 + START)
                for i in range(TB):
                    if i >= 2:
                        pe.wait_ge(M["sacc"], TB * g + i - 1 + START)
                    for c, (lo, w) in enumerate(SH_CHUNKS):
                        last = nc.tensor.matmul(bank[6 + i % 2][:, 0:DIM], shid[0:w, c, i * P:(i + 1) * P],
                                                sdT[0:w, c, :], start=(c == 0), stop=(c == 2))
                    last.then_inc(M["sdown"], 1)

        def shared_scalar(act):
            with act.Fori(0, BATCH) as g:
                for c, (lo, w) in enumerate(SH_CHUNKS):
                    act.wait_ge(M["sup"], 6 * g + 2 * c + 1)
                    act.wait_ge(M["shid"], 3 * g + START)
                    nc.scalar.activation(sgl[0:w, c, :], bank[c][0:w, :], ACT.Silu).then_inc(M["ssil"], 1)

        def shared_vector(dve):
            with dve.Fori(0, BATCH) as g:
                for c, (lo, w) in enumerate(SH_CHUNKS):
                    dve.wait_ge(M["sup"], 6 * g + 2 * c + 2)
                    dve.wait_ge(M["ssil"], 3 * g + c + 1)
                    dve.wait_ge(M["sdown"], TB * g + START)
                    nc.vector.tensor_tensor(shid[0:w, c, :], bank[3 + c][0:w, :], sgl[0:w, c, :], ALU.mult)\
                        .then_inc(M["shid"], 1)
                for i in range(TB):
                    dve.wait_ge(M["sdown"], TB * g + i + 1 + START)
                    xt = x[:, bass.ds(g * TB + i, 1), :].rearrange("p o c -> p (o c)")
                    nc.vector.tensor_tensor(xt, bank[6 + i % 2][:, 0:DIM], xt, ALU.add).then_inc(M["sacc"], 1)

        taken_pad, _ = carve(r1, 4096, (TILES, EXPERTS + 2))

        S = {k: sem(f"s_{k}") for k in
             ("aneg", "pad", "xb", "br", "brc", "tap", "conv", "act", "z", "zs", "bcd", "bcde", "d1", "d2", "d3", "d4",
              "dexp", "dln", "adt", "xt", "xte", "bct", "bcte", "cum", "es", "au", "seg", "lt", "g", "gm",
              "mt", "xd1", "xd", "yo", "st0", "st", "y1", "y2", "y3", "y4", "yt", "yte", "out", "res")}
        SCREDIT = ("xb", "conv", "act", "brc", "zs", "bcde", "res", "xte", "bcte", "yte", "es", "gm", "lt", "y1", "y2",
                   "yo", "st", "mt", "y4", "seg", "cum", "out", "xt", "bct", "br", "adt", "yt", "au")
        draw, dmin, dexp, dw, dln, dpos, dsel, dtv = (dts[:, n, :] for n in range(8))

        def ssm_pool(pool):
            for c in range(CH):
                nc.gpsimd.memset(xpad[:, c, 0:TAPS - 1], 0.0).then_inc(S["pad"], 1)
            with pool.Fori(0, BATCH) as b:
                hold(pool, "pool", S["res"], TB * b + START)
                nc.gpsimd.tensor_copy(xb, xnT[:, :, bass.ds(b * SEQ, SEQ)]).then_inc(S["xb"], 1)
                for i in range(TB):
                    n = TB * b + i
                    hold(pool, "pool", S["adt"], b + 1 + START)
                    hold(pool, "pool", S["seg"], n + START)
                    nc.gpsimd.tensor_tensor(AU, le.unsqueeze(1).to_broadcast([P, NH, P]),
                                            adt3[:, i, :].unsqueeze(2).to_broadcast([P, NH, P]), ALU.mult)\
                        .then_inc(S["au"], 1)
                    hold(pool, "pool", S["xte"], n + 1 + START)
                    hold(pool, "pool", S["st"], n + START)
                    nc.gpsimd.tensor_tensor(heads(xdisc), heads(xa[:, i, :]),
                                            dtv3[:, i, :].unsqueeze(2).to_broadcast([P, NH, HD]), ALU.mult)\
                        .then_inc(S["xd1"], 1)
                    hold(pool, "pool", S["xd1"], n + 1)
                    hold(pool, "pool", S["es"], n + 1 + START)
                    nc.gpsimd.tensor_tensor(heads(xdec), heads(xdisc),
                                            es[:, i, NH:2 * NH].unsqueeze(2).to_broadcast([P, NH, HD]), ALU.mult)\
                        .then_inc(S["xd"], 1)

        def heads(ap):
            return ap.rearrange("p (h c) -> p h c", h=NH)

        dtv3 = dtv.rearrange("p (i h) -> p i h", i=TB)
        adt3 = dsel.rearrange("p (i h) -> p i h", i=TB)

        def ssm_tensor(pe):
            with pe.Fori(0, BATCH) as b:
                for c in range(CH):
                    pe.wait_ge(S["brc"], CH * b + START)
                    for k in range(KC):
                        last = nc.tensor.matmul(bank[c][:], w_in[:, k, c * P:(c + 1) * P],
                                                xnT[:, k, bass.ds(b * SEQ, SEQ)], start=(k == 0), stop=(k == KC - 1))
                    last.then_inc(S["br"], 1)
                pe.wait_ge(S["xb"], b + 1 + START)
                for i in range(TB):
                    n = TB * b + i
                    pe.wait_ge(S["zs"], TB * b + max(0, i - 1) + START)
                    for k in range(KC):
                        last = nc.tensor.matmul(bank[4 + i % 2][:], xb[:, k, i * P:(i + 1) * P],
                                                w_in[:, k, DIN:2 * DIN], start=(k == 0), stop=(k == KC - 1))
                    last.then_inc(S["z"], 1)
                    pe.wait_ge(S["bcde"], TB * b + max(0, i - 1) + START)
                    for k in range(KC):
                        last = nc.tensor.matmul(bank[6 + i % 2][:, 0:BCD], xb[:, k, i * P:(i + 1) * P],
                                                w_in[:, k, 2 * DIN:PROJ], start=(k == 0), stop=(k == KC - 1))
                    last.then_inc(S["bcd"], 1)
                def part1(i):
                    n = TB * b + i
                    if i == 0:
                        pe.wait_ge(S["bcde"], TB * (b + 1) + START)
                        pe.wait_ge(S["zs"], TB * (b + 1) + START)
                    hold(pe, "pe", S["act"], CH * b + CH + START)
                    hold(pe, "pe", S["xte"], n + START)
                    for c in range(CH):
                        last = nc.tensor.transpose(bank[6][:, c * P:(c + 1) * P], xact[:, c, i * P:(i + 1) * P], ident)
                    last.then_inc(S["xt"], 1)
                    hold(pe, "pe", S["gm"], n + START)
                    for m in range(2):
                        last = nc.tensor.transpose(bank[0][0:DST, m * P:(m + 1) * P],
                                                   bcd[:, i, m * DST:(m + 1) * DST], ident)
                    last.then_inc(S["bct"], 1)
                    pe.wait_ge(S["adt"], b + 1 + START)
                    pe.wait_ge(S["res"], n + START)
                    for m, w in enumerate((le, gt, ones[:])):
                        last = nc.tensor.matmul(bank[7][:, m * NH:(m + 1) * NH], w, adt3[:, i, :],
                                                start=True, stop=True)
                    last.then_inc(S["cum"], 1)
                    pe.wait_ge(S["au"], n + 1 + START)
                    pe.wait_ge(S["lt"], 2 * n + START)
                    for m in range(2):
                        last = nc.tensor.matmul(bank[1 + m][:], gt, AU[:, 4 * m:4 * m + 4, :]
                                                .rearrange("p h l -> p (h l)"), start=True, stop=True)
                    last.then_inc(S["seg"], 1)
                    pe.wait_ge(S["bcte"], n + 1 + START)
                    nc.tensor.matmul(bank[0][:, 0:P], BCT[:, 0, :], BCT[:, 1, :], start=True, stop=True)\
                        .then_inc(S["g"], 1)

                def part2(i):
                    n = TB * b + i
                    if i:
                        pe.wait_ge(S["st"], n + START)
                        nc.tensor.matmul(bank[4][:], BCT[:, 1, :], state, start=True, stop=True).then_inc(S["yo"], 1)
                    pe.wait_ge(S["xd"], n + 1)
                    nc.tensor.matmul(bank[5][0:DST, :], bcd[:, i, 0:DST], xdec, start=True, stop=True)\
                        .then_inc(S["st0"], 1)
                    pe.wait_ge(S["y2"], n + START)
                    pe.wait_ge(S["mt"], n + 1 + START)
                    for h in range(NH):
                        last = nc.tensor.matmul(bank[3][:, h * HD:(h + 1) * HD], LT[:, h * P:(h + 1) * P],
                                                xdisc[:, h * HD:(h + 1) * HD], start=True, stop=True)
                    last.then_inc(S["y1"], 1)

                def part3(i):
                    n = TB * b + i
                    hold(pe, "pe", S["y4"], n + 1 + START)
                    hold(pe, "pe", S["xte"], TB * b + min(TB, i + 1) + START)
                    hold(pe, "pe", S["yte"], n + START)
                    for c in range(CH):
                        last = nc.tensor.transpose(bank[6][:, c * P:(c + 1) * P], ya[:, c * P:(c + 1) * P], ident)
                    last.then_inc(S["yt"], 1)
                    pe.wait_ge(S["yte"], n + 1 + START)
                    for c in range(CH):
                        last = nc.tensor.matmul(bank[7][:, 0:DIM], yT[:, c, :], w_out[:, c, :],
                                                start=(c == 0), stop=(c == CH - 1))
                    last.then_inc(S["out"], 1)

                for i in range(TB):
                    part1(i)
                    part2(i)
                    part3(i)

        def ssm_scalar(act):
            with act.Fori(0, BATCH) as b:
                for c in range(CH):
                    hold(act, "act", S["br"], CH * b + c + 1 + START)
                    hold(act, "act", S["conv"], CH * b + START)
                    nc.scalar.copy(xpad[:, c, TAPS - 1:SEQ + TAPS - 1], bank[c][:]).then_inc(S["brc"], 1)
                for i in range(TB):
                    act.wait_ge(S["z"], TB * b + i + 1)
                    nc.scalar.activation(zs[:, i, :], bank[4 + i % 2][:], ACT.Silu).then_inc(S["zs"], 1)
                for c in range(CH):
                    act.wait_ge(S["conv"], CH * b + c + 1 + START)
                    nc.scalar.activation(xact[:, c, :], cv[:, c, :], ACT.Silu, bias=conv_b[:, c:c + 1])\
                        .then_inc(S["act"], 1)
                act.wait_ge(S["d1"], b + 1)
                nc.scalar.activation(dexp, dmin, ACT.Exp).then_inc(S["dexp"], 1)
                act.wait_ge(S["d2"], b + 1)
                nc.scalar.activation(dln, dw, ACT.Ln).then_inc(S["dln"], 1)
                for i in range(TB):
                    n = TB * b + i
                    act.wait_ge(S["xt"], n + 1 + START)
                    nc.scalar.copy(xa[:, i, :], bank[6][:]).then_inc(S["xte"], 1)
                    act.wait_ge(S["bct"], n + 1 + START)
                    nc.scalar.copy(BCT.rearrange("p m l -> p (m l)"), bank[0][0:DST, 0:2 * P]).then_inc(S["bcte"], 1)
                    act.wait_ge(S["cum"], n + 1 + START)
                    nc.scalar.activation(es[:, i, :], bank[7][:, 0:3 * NH], ACT.Exp).then_inc(S["es"], 1)
                    act.wait_ge(S["seg"], n + 1 + START)
                    act.wait_ge(S["y1"], n + START)
                    for m in range(2):
                        nc.scalar.activation(LT[:, m * 4 * P:(m + 1) * 4 * P], bank[1 + m][:], ACT.Exp)\
                            .then_inc(S["lt"], 1)
                    act.wait_ge(S["yt"], n + 1 + START)
                    nc.scalar.copy(yT.rearrange("p c l -> p (c l)"), bank[6][:]).then_inc(S["yte"], 1)

        def ssm_vector(dve):
            dve.wait_ge(S["aneg"], 1)
            nc.vector.tensor_scalar(a_neg[:], a_neg[:], -1.0, None, ALU.mult).then_inc(S["aneg"], 1)
            dve.wait_ge(S["aneg"], 2)
            dve.wait_ge(S["pad"], CH)
            with dve.Fori(0, BATCH) as b:
                for c in range(CH):
                    dve.wait_ge(S["brc"], CH * b + c + 1 + START)
                    dve.wait_ge(S["act"], CH * b + START)
                    nc.vector.tensor_scalar(cv[:, c, :], xpad[:, c, 0:SEQ], conv_w[:, c, 0:1], None, ALU.mult)\
                        .then_inc(S["tap"], 1)
                for m in range(1, TAPS):
                    for c in range(CH):
                        dve.wait_ge(S["tap"], (TAPS - 1) * CH * b + CH * (m - 1) + c + 1)
                        ins = nc.vector.scalar_tensor_tensor(out=cv[:, c, :], in0=xpad[:, c, m:m + SEQ],
                                                             scalar=conv_w[:, c, m:m + 1], in1=cv[:, c, :],
                                                             op0=ALU.mult, op1=ALU.add)
                        ins.then_inc(S["tap"] if m < TAPS - 1 else S["conv"], 1)
                for i in range(TB):
                    dve.wait_ge(S["bcd"], TB * b + i + 1)
                    nc.vector.tensor_copy(bcd[:, i, :], bank[6 + i % 2][:, 0:BCD]).then_inc(S["bcde"], 1)
                dve.wait_ge(S["bcde"], TB * (b + 1) + START)
                nc.vector.tensor_tensor(draw.rearrange("p (i h) -> p i h", i=TB), bcd[:, :, 2 * DST:BCD],
                                        dt_bias[:].unsqueeze(1).to_broadcast([P, TB, NH]), ALU.add)\
                    .then_inc(S["d3"], 1)
                dve.wait_ge(S["d3"], 5 * b + 1)
                nc.vector.scalar_tensor_tensor(out=dmin, in0=draw, scalar=-1.0, in1=draw,
                                               op0=ALU.mult, op1=ALU.min).then_inc(S["d1"], 1)
                nc.vector.tensor_scalar(dpos, draw, 0.0, None, ALU.max).then_inc(S["d3"], 1)
                dve.wait_ge(S["dexp"], b + 1)
                nc.vector.tensor_scalar(dw, dexp, 1.0, None, ALU.add).then_inc(S["d2"], 1)
                dve.wait_ge(S["d2"], b + 1)
                nc.vector.tensor_scalar(dmin, dw, -1.0, 1e-30, ALU.add, ALU.max).then_inc(S["d4"], 1)
                dve.wait_ge(S["d4"], 4 * b + 1)
                nc.vector.reciprocal(dmin, dmin).then_inc(S["d4"], 1)
                dve.wait_ge(S["d4"], 4 * b + 2)
                nc.vector.tensor_tensor(dmin, dmin, dexp, ALU.mult).then_inc(S["d4"], 1)
                dve.wait_ge(S["dln"], b + 1)
                dve.wait_ge(S["d4"], 4 * b + 3)
                nc.vector.tensor_tensor(dmin, dmin, dln, ALU.mult).then_inc(S["d4"], 1)
                nc.vector.scalar_tensor_tensor(out=draw, in0=dw, scalar=1.0, in1=dexp,
                                               op0=ALU.is_equal, op1=ALU.mult).then_inc(S["d3"], 1)
                dve.wait_ge(S["d4"], 4 * b + 4)
                dve.wait_ge(S["d3"], 5 * b + 2)
                nc.vector.tensor_tensor(dpos, dpos, dmin, ALU.add).then_inc(S["d3"], 1)
                dve.wait_ge(S["d3"], 5 * b + 4)
                nc.vector.tensor_tensor(dtv, dpos, draw, ALU.add).then_inc(S["d3"], 1)
                dve.wait_ge(S["d3"], 5 * b + 5)
                nc.vector.tensor_tensor(adt3, dtv3, a_neg[:].unsqueeze(1).to_broadcast([P, TB, NH]), ALU.mult)\
                    .then_inc(S["adt"], 1)
                for i in range(TB):
                    n = TB * b + i
                    dve.wait_ge(S["g"], n + 1)
                    nc.vector.tensor_tensor(Gm, bank[0][:, 0:P], le, ALU.mult).then_inc(S["gm"], 1)
                    dve.wait_ge(S["lt"], 2 * n + 2 + START)
                    dve.wait_ge(S["gm"], n + 1 + START)
                    lt3 = LT.rearrange("p (h l) -> p h l", h=NH)
                    nc.vector.tensor_tensor(lt3, lt3, Gm.unsqueeze(1).to_broadcast([P, NH, P]), ALU.mult)\
                        .then_inc(S["mt"], 1)
                    dve.wait_ge(S["st0"], n + 1)
                    if i:
                        dve.wait_ge(S["yo"], (TB - 1) * b + i + START)
                        nc.vector.tensor_tensor(heads(state), heads(state),
                                                es[0:DST, i, 2 * NH:3 * NH].unsqueeze(2).to_broadcast([DST, NH, HD]),
                                                ALU.mult).then_inc(S["tap2"], 1)
                        dve.wait_ge(S["tap2"], (TB - 1) * b + i)
                        nc.vector.tensor_tensor(state, state, bank[5][0:DST, :], ALU.add).then_inc(S["st"], 1)
                    else:
                        nc.vector.tensor_copy(state, bank[5][0:DST, :]).then_inc(S["st"], 1)
                    dve.wait_ge(S["xte"], n + 1 + START)
                    hold(dve, "dve", S["yt"], n + START)
                    nc.vector.tensor_tensor(ya, xa[:, i, :], dskip[:], ALU.mult).then_inc(S["y3"], 1)
                    if i:
                        dve.wait_ge(S["es"], n + 1 + START)
                        nc.vector.tensor_tensor(heads(yb), heads(bank[4][:]),
                                                es[:, i, 0:NH].unsqueeze(2).to_broadcast([P, NH, HD]), ALU.mult)\
                            .then_inc(S["y3"], 1)
                        dve.wait_ge(S["y3"], YC * b + 3 * i + 0)
                        nc.vector.tensor_tensor(ya, ya, yb, ALU.add).then_inc(S["y3"], 1)
                    dve.wait_ge(S["y1"], n + 1 + START)
                    dve.wait_ge(S["y3"], YC * b + 3 * i + 1)
                    nc.vector.tensor_tensor(ya, ya, bank[3][:], ALU.add).then_inc(S["y2"], 1)
                    dve.wait_ge(S["y2"], n + 1 + START)
                    nc.vector.tensor_tensor(ya, ya, zs[:, i, :], ALU.mult).then_inc(S["y4"], 1)
                    dve.wait_ge(S["out"], n + 1 + START)
                    xt = x[:, bass.ds(b * TB + i, 1), :].rearrange("p o c -> p (o c)")
                    nc.vector.tensor_tensor(xt, bank[7][:, 0:DIM], xt, ALU.add).then_inc(S["res"], 1)

        YC = 1 + 3 * (TB - 1)
        S["tap2"] = sem("s_tap2")

        F = {k: sem(f"f_{k}") for k in ("gate", "up", "sil", "hid", "down", "sc", "res")}
        FCREDIT = ("hid", "down", "res", "sil")
        NF = len(FF_CHUNKS)

        def ff_tensor(pe):
            with pe.Fori(0, BATCH) as g:
                for c, (lo, w) in enumerate(FF_CHUNKS):
                    hold(pe, "pe", F["hid"], NF * g + max(0, c - 1) + START)
                    for k in range(KC):
                        last = nc.tensor.matmul(bank[c % 2][0:w, :], fgT[:, k, lo:lo + w],
                                                xnT[:, k, bass.ds(g * SEQ, SEQ)], start=(k == 0), stop=(k == KC - 1))
                    last.then_inc(F["gate"], 1)
                    for k in range(KC):
                        last = nc.tensor.matmul(bank[2 + c % 2][0:w, :], fuT[:, k, lo:lo + w],
                                                xnT[:, k, bass.ds(g * SEQ, SEQ)], start=(k == 0), stop=(k == KC - 1))
                    last.then_inc(F["up"], 1)
                for i in range(TB):
                    pe.wait_ge(F["hid"], NF * g + NF + START)
                    pe.wait_ge(F["res"], TB * g + START)
                    for c, (lo, w) in enumerate(FF_CHUNKS):
                        last = nc.tensor.matmul(bank[4 + i][:, 0:DIM], fhid[0:w, c, i * P:(i + 1) * P],
                                                fdT[0:w, c, :], start=(c == 0), stop=(c == NF - 1))
                    last.then_inc(F["down"], 1)

        def ff_scalar(act):
            with act.Fori(0, BATCH) as g:
                for c, (lo, w) in enumerate(FF_CHUNKS):
                    act.wait_ge(F["gate"], NF * g + c + 1)
                    act.wait_ge(F["hid"], NF * g + max(0, c - 1) + START)
                    nc.scalar.activation(fsl[0:w, c % 2, :], bank[c % 2][0:w, :], ACT.Silu,
                                         scale=gate_s[0:w, c:c + 1]).then_inc(F["sil"], 1)

        def ff_vector(dve):
            with dve.Fori(0, BATCH) as g:
                for c, (lo, w) in enumerate(FF_CHUNKS):
                    dve.wait_ge(F["up"], NF * g + c + 1)
                    dve.wait_ge(F["sil"], NF * g + c + 1 + START)
                    dve.wait_ge(F["down"], TB * g + START)
                    nc.vector.scalar_tensor_tensor(out=fhid[0:w, c, :], in0=bank[2 + c % 2][0:w, :],
                                                   scalar=up_s[0:w, c:c + 1], in1=fsl[0:w, c % 2, :],
                                                   op0=ALU.mult, op1=ALU.mult).then_inc(F["hid"], 1)
                for i in range(TB):
                    dve.wait_ge(F["down"], TB * g + i + 1 + START)
                    dve.wait_ge(F["res"], TB * g + max(0, i - 1) + START)
                    nc.vector.tensor_tensor(fo[:, i % 2, :], bank[4 + i][:, 0:DIM], down_s[:], ALU.mult)\
                        .then_inc(F["sc"], 1)
                    dve.wait_ge(F["sc"], TB * g + i + 1)
                    xt = x[:, bass.ds(g * TB + i, 1), :].rearrange("p o c -> p (o c)")
                    nc.vector.tensor_tensor(xt, fo[:, i % 2, :], xt, ALU.add).then_inc(F["res"], 1)

        @block.sync
        def _(sp):
            issue_loads(sp)
            assert n_load == total_loads, n_load
            if STAGES >= 5:
                sp.wait_ge(M["comb"], 1)
                experts_sp(sp)
            sp.wait_ge(stage_done[LAST], 4)
            sp.dma_start(out.rearrange("(t p) c -> p t c", p=P), x[:]).then_inc(loads["consts"], 16)
            sp.wait_ge(loads["consts"], 16)

        @block.gpsimd
        def _(pool):
            for s in [A[k] for k in ("res", "qs", "qte", "ote")] + [M[k] for k in ("down", "acc", "shid", "sdown", "sacc")]:
                pool.sem_inc(s, START)
            for s in [S[k] for k in SCREDIT] + [F[k] for k in FCREDIT]:
                pool.sem_inc(s, START)
            nc.gpsimd.memset(ones[:], 1.0).then_inc(consts, 1)
            loaded(pool, "tables")
            nc.gpsimd.tensor_copy(identb[:], ident).then_inc(consts, 1)
            nc.gpsimd.tensor_copy(futureb[:], future).then_inc(consts, 1)
            stage_end(pool, 0)
            stage_end(pool, 1)
            stage_start(pool, 2)
            att_pool(pool)
            stage_end(pool, 2)
            stage_end(pool, 3)
            stage_end(pool, 4)
            stage_end(pool, 5)
            if STAGES >= 7:
                stage_start(pool, 6)
                ssm_pool(pool)
                stage_end(pool, 6)
                stage_end(pool, 7)
                stage_end(pool, 8)

        @block.scalar
        def _(act):
            loaded(act, "attn")
            prep_scalar(act)
            stage_end(act, 0)
            stage_start(act, 1)
            ln_scalar(act, 0)
            stage_end(act, 1)
            stage_start(act, 2)
            att_scalar(act)
            stage_end(act, 2)
            stage_start(act, 3)
            ln_scalar(act, 1)
            stage_end(act, 3)
            stage_start(act, 4)
            if STAGES >= 5:
                route_scalar(act)
                shared_scalar(act)
                experts_scalar(act)
            stage_end(act, 4)
            if STAGES >= 7:
                stage_start(act, 5)
                ln_scalar(act, 2)
                loaded(act, "mamba")
                nc.scalar.activation(a_neg[:], a_log[:], ACT.Exp).then_inc(S["aneg"], 1)
                stage_end(act, 5)
                stage_start(act, 6)
                ssm_scalar(act)
                stage_end(act, 6)
            if STAGES >= 9:
                stage_start(act, 7)
                ln_scalar(act, 3)
                loaded(act, "ffn1")
                stage_end(act, 7)
                stage_start(act, 8)
                ff_scalar(act)
                stage_end(act, 8)

        @block.vector
        def _(dve):
            loaded(dve, "x")
            stage_end(dve, 0)
            stage_start(dve, 1)
            ln_vector(dve, 0)
            stage_end(dve, 1)
            stage_start(dve, 2)
            att_vector(dve)
            stage_end(dve, 2)
            stage_start(dve, 3)
            ln_vector(dve, 1)
            stage_end(dve, 3)
            stage_start(dve, 4)
            if STAGES >= 5:
                route_vector(dve)
                shared_vector(dve)
                experts_vector(dve)
            stage_end(dve, 4)
            if STAGES >= 7:
                stage_start(dve, 5)
                ln_vector(dve, 2)
                stage_end(dve, 5)
                stage_start(dve, 6)
                loaded(dve, "mamba")
                ssm_vector(dve)
                stage_end(dve, 6)
            if STAGES >= 9:
                stage_start(dve, 7)
                ln_vector(dve, 3)
                stage_end(dve, 7)
                stage_start(dve, 8)
                loaded(dve, "ffn1")
                ff_vector(dve)
                stage_end(dve, 8)

        @block.tensor
        def _(pe):
            prep_tensor(pe)
            stage_end(pe, 0)
            stage_start(pe, 1)
            loaded(pe, "tables")
            ln_tensor(pe, 0)
            stage_end(pe, 1)
            stage_start(pe, 2)
            att_tensor(pe)
            stage_end(pe, 2)
            stage_start(pe, 3)
            ln_tensor(pe, 1)
            stage_end(pe, 3)
            stage_start(pe, 4)
            if STAGES >= 5:
                loaded(pe, "ffn0")
                route_tensor(pe)
                pe.wait_ge(M["lgs"], 2)
                shared_tensor(pe)
                experts_tensor(pe)
            stage_end(pe, 4)
            if STAGES >= 7:
                stage_start(pe, 5)
                ln_tensor(pe, 2)
                stage_end(pe, 5)
                stage_start(pe, 6)
                loaded(pe, "mamba")
                ssm_tensor(pe)
                stage_end(pe, 6)
            if STAGES >= 9:
                stage_start(pe, 7)
                ln_tensor(pe, 3)
                stage_end(pe, 7)
                stage_start(pe, 8)
                loaded(pe, "ffn1")
                ff_tensor(pe)
                stage_end(pe, 8)


STAGES = 9
LAST = STAGES - 1 if STAGES > 4 else 4


def shape_tables():
    r = np.arange(P)
    ident = np.eye(P, dtype=np.float32)
    future = np.where(r[None, :] > r[:, None], -1e30, 0.0)
    le = (r[:, None] <= r[None, :]).astype(np.float32)
    gt = (r[:, None] > r[None, :]).astype(np.float32)
    f = np.float32
    pos2 = np.arange(0, DR, 2, dtype=f)
    inv = f(1.0) / np.power(f(10000.0), pos2 / f(DR)).astype(f)
    wavelen = f(2.0 * np.pi) / inv
    ramp = np.clip((f(1024) / wavelen - f(1.0)) / f(3.0), f(0), f(1)).astype(f)
    inv = (inv * (f(1.0) - ramp) + inv / f(16.0) * ramp).astype(f)
    freqs = np.outer(np.arange(SEQ, dtype=f), inv).astype(f)
    emb = np.concatenate([freqs, freqs], axis=-1)
    factor = f(0.1 * math.log(16.0) + 1.0)
    cos, sin = np.cos(emb) * factor, np.sin(emb) * factor
    sin[:, :DR // 2] *= -1
    tok = [t.reshape(TB, P, DR).transpose(1, 0, 2).reshape(P, TB * DR) for t in (cos, sin)]
    feat = [np.concatenate([np.zeros((KVL, SEQ)), t.T], axis=0) for t in (cos, sin)]
    return np.concatenate([ident, future, le, gt, *tok, *feat], axis=1).astype(f)


def lay_out(i):
    c = np.ascontiguousarray
    w_qb = i["L0_attn_w_qb"].reshape(QL, HEADS, DN + DR)
    w_kvb = i["L0_attn_w_kvb"].reshape(KVL, HEADS, 2, DN)
    w_qa, w_kva = i["L0_attn_w_qa"], i["L0_attn_w_kva"]
    kr = w_kva[:, KVL:]
    w_a = np.concatenate([w_qa, kr[:, DR // 2:], kr[:, :DR // 2], w_kva], axis=1)
    columns = lambda v: c(np.pad(v, (0, P * len(FF_CHUNKS) - INTER)).reshape(len(FF_CHUNKS), P).T)
    return {
        "x": c(i["L0_attn_x"].reshape(TOKENS, DIM)),
        "tables": shape_tables(),
        "w_qbT": c(w_qb[:, :, :DN].transpose(2, 1, 0)),
        "w_qr": c(w_qb[:, :, DN:]),
        "w_kvT": c(w_kvb.transpose(3, 2, 1, 0)),
        "w_o": c(i["L0_attn_w_o"]),
        "w_a": c(w_a.reshape(KC, P, 3 * P).transpose(1, 0, 2)),
        "q_norm": c(i["L0_attn_q_norm_w"]),
        "kv_norm": c(i["L0_attn_kv_norm_w"]),
        "gateT": c(i["L0_ffn_gate_w"].T),
        "w1T": c(i["L0_ffn_experts_w1"].transpose(0, 2, 1).reshape(EXPERTS, KC, P, EI).transpose(0, 2, 1, 3)
                 .reshape(EXPERTS, P, KC * EI)),
        "w2T": c(i["L0_ffn_experts_w2"].transpose(0, 2, 1).reshape(EXPERTS, 2, EH, DIM).transpose(0, 2, 1, 3)
                 .reshape(EXPERTS, EH, 2 * DIM)),
        "sguT": c(i["L0_ffn_shared_gate_up"].T),
        "sdT": c(i["L0_ffn_shared_down"].T),
        "w_in": c(i["L1_attn_in_proj_w"].T),
        "conv_w": c(i["L1_attn_conv_w"].reshape(DIN, TAPS)),
        "conv_b": c(i["L1_attn_conv_b"].reshape(CH, P).T),
        "w_out": c(i["L1_attn_out_proj_w"].T),
        "A_log": c(i["L1_attn_A_log"]),
        "dt_bias": c(i["L1_attn_dt_bias"]),
        "D_skip": c(i["L1_attn_D_skip"]),
        "fgT": c(i["L1_ffn_gate_w"].T),
        "fuT": c(i["L1_ffn_up_w"].T),
        "fdT": c(i["L1_ffn_down_w"].T),
        "gate_s": columns(i["L1_ffn_gate_s"]),
        "up_s": columns(i["L1_ffn_up_s"]),
        "down_s": c(i["L1_ffn_down_s"]),
    }


def kernel(**inputs):
    import concourse.bacc as bacc
    from concourse.bass_utils import run_bass_kernel_spmd

    nc = bacc.Bacc("TRN2", target_bir_lowering=False, num_devices=1)
    arrays = lay_out({k: np.asarray(v) for k, v in inputs.items()})
    args = {k: nc.dram_tensor(k + "_dram", v.shape, F32, kind="ExternalInput").ap() for k, v in arrays.items()}
    out = nc.dram_tensor("out_dram", (TOKENS, DIM), F32, kind="ExternalOutput").ap()
    build(nc, args, out)
    r = run_bass_kernel_spmd(nc, [{k + "_dram": v for k, v in arrays.items()}], core_ids=[0])
    return r.results[0]["out_dram"].reshape(BATCH, SEQ, DIM)
```

```python
import math
from contextlib import ExitStack

import numpy as np

import concourse.bass as bass
from concourse import mybir

F32 = mybir.dt.float32
BF16 = mybir.dt.bfloat16
ALU = mybir.AluOpType
ACT = mybir.ActivationFunctionType
AX = mybir.AxisListType

P = 128
BATCH, SEQ, DIM = 4, 512, 256
TOKENS = BATCH * SEQ
TILES = TOKENS // P
TB = SEQ // P
KC = DIM // P
HEADS, DN, DR, DV = 16, 128, 64, 128
QL, KVL = 192, 64
QL2 = QL - P
QE = KVL + DR
HG = 4
GROUPS = HEADS // HG
EXPERTS, EI, TOPK = 64, 176, 6
EH = EI // 2
ROWS = 2 * P
MAX_TILES = TOKENS * TOPK // ROWS + EXPERTS
LOOP_TILES = 4
FAR = 32768
SHI = 352
SH_CHUNKS = [(0, 128), (128, 128), (256, 96)]
DIN, DST, NH, HD, TAPS = 512, 64, 8, 64, 4
CH = DIN // P
PROJ = 2 * DIN + 2 * DST + NH
BCD = 2 * DST + NH
INTER = 704
FF_CHUNKS = [(128 * i, min(128, INTER - 128 * i)) for i in range((INTER + 127) // 128)]
ATT_SCALE = 1.0 / math.sqrt(DN + DR)
RMS_EPS, LN_EPS = 1e-6, 1e-5
START = 4
LOW = -3e38


N_MARKS = TOKENS // ROWS + MAX_TILES // LOOP_TILES


def build(nc, a, out):
    ctx = ExitStack()
    with ctx:
        def sb(name, shape, dt=F32):
            return ctx.enter_context(nc.sbuf_tensor(name, shape, dt))

        def sem(name):
            return ctx.enter_context(nc.semaphore(name))

        x = sb("x", [P, TILES, DIM])
        xnT = sb("xnT", [P, KC, TOKENS])
        tables = sb("tables", [P, 4 * P + TB * DR * 2 + 2 * SEQ + N_MARKS])
        ident = tables[:, 0:P]
        future = tables[:, P:2 * P]
        le = tables[:, 2 * P:3 * P]
        gt = tables[:, 3 * P:4 * P]
        o = 4 * P
        cosq = tables[:, o:o + TB * DR].rearrange("p (i d) -> p i d", i=TB)
        sinq = tables[:, o + TB * DR:o + 2 * TB * DR].rearrange("p (i d) -> p i d", i=TB)
        o += 2 * TB * DR
        cosk = tables[:, o:o + SEQ]
        sink = tables[:, o + SEQ:o + 2 * SEQ]
        o += 2 * SEQ
        partition = tables[:, o:o + 1]
        full = tables[:, o + 1:o + TOKENS // ROWS]
        loop_marks = tables[:, o + TOKENS // ROWS:o + N_MARKS]
        ones = sb("ones", [P, P])
        identb = sb("identb", [P, P], BF16)
        futureb = sb("futureb", [P, P], BF16)
        stats = sb("stats", [P, TILES, 6])
        mv = sb("mv", [P, TILES, 2])
        rstd = sb("rstd", [P, TILES])
        rvar = sb("rvar", [P, TILES])

        w_a = sb("w_a", [P, KC, 3 * P])
        qn1 = sb("qn1", [P, 1])
        qn2 = sb("qn2", [QL2, 1])
        kvn = sb("kvn", [KVL, 1])
        wvo = sb("wvo", [P, HEADS // 2, DIM])
        gateT = sb("gateT", [P, KC, EXPERTS])
        sguT = sb("sguT", [P, KC, 2 * SHI])
        sdT = sb("sdT", [P, 3, DIM])
        w_in = sb("w_in", [P, KC, PROJ])
        conv_w = sb("conv_w", [P, CH, TAPS])
        conv_b = sb("conv_b", [P, CH])
        w_out = sb("w_out", [P, CH, DIM])
        a_neg = sb("a_neg", [P, NH])
        a_log = sb("a_log", [P, NH])
        dt_bias = sb("dt_bias", [P, NH])
        dskip = sb("dskip", [P, DIN])
        fgT = sb("fgT", [P, KC, INTER])
        fuT = sb("fuT", [P, KC, INTER])
        fdT = sb("fdT", [P, len(FF_CHUNKS), DIM])
        gate_s = sb("gate_s", [P, len(FF_CHUNKS)])
        up_s = sb("up_s", [P, len(FF_CHUNKS)])
        down_s = sb("down_s", [P, DIM])

        r1 = sb("r1", [P, 9472])
        r2 = sb("r2", [P, 14336])
        w2buf = sb("w2buf", [EH, LOOP_TILES, 2 * DIM])
        zeros = sb("zeros", [P, DIM])
        slots = sb("slots", [P, TILES, TOPK], mybir.dt.uint32)
        tile_row = sb("tile_row", [1, P], mybir.dt.int32)
        trips = sb("trips", [1, 2], mybir.dt.int32)
        sent = nc.dram_tensor("sent", (MAX_TILES * ROWS, DIM), F32).ap()
        returned = sent

        def carve(arena, at, shape, parts=P):
            n = int(np.prod(shape))
            ap = arena[0:parts, at:at + n]
            if len(shape) == 2:
                ap = ap.rearrange("p (a b) -> p a b", a=shape[0])
            if len(shape) == 3:
                ap = ap.rearrange("p (a b c) -> p a b c", a=shape[0], b=shape[1])
            return ap, at + n

        wqbT, e = carve(r1, 0, (HEADS, QL))
        wkvT, e = carve(r1, e, (2, HEADS, KVL))
        w_o, e = carve(r1, e, (HEADS, DIM))
        xn, _ = carve(r1, 0, (TILES, DIM))
        O, e = carve(r1, 0, (TB, HEADS * KVL))
        QT, e = carve(r1, e, (HG, SEQ))
        probT, e = carve(r1, e, (2, SEQ))
        prob, e = carve(r1, e, (4, SEQ))
        wqe1, e = carve(r2, 0, (HEADS, QE))
        wqe2, e = carve(r2, e, (HEADS, QE), QL2)
        cq1, e = carve(r2, e, (SEQ,))
        cq2, e = carve(r2, e, (SEQ,), QL2)
        KT, e = carve(r2, e, (SEQ,))
        V, e = carve(r2, e, (TB, KVL))
        OT, e = carve(r2, e, (2, HEADS // 2 * P))
        sq, e = carve(r2, e, (3, SEQ))
        rq, e = carve(r2, e, (SEQ,))
        rk, e = carve(r2, e, (SEQ,))
        krope, e = carve(r2, e, (2, SEQ))
        qs, e = carve(r2, e, (TB, HG * QE))
        qtmp, e = carve(r2, e, (2, HG * DR))
        qtmp_v = krope.rearrange("p a b -> p (a b)")[:, 0:2 * HG * DR].rearrange("p (a b) -> p a b", a=2)
        lgs, e = carve(r2, 0, (TILES, EXPERTS + 2))
        taken, e = carve(r2, e, (TILES, EXPERTS))
        comb, e = carve(r2, e, (TILES, EXPERTS))
        top8, e = carve(r2, e, (TILES, 8))
        rsum, e = carve(r2, e, (TILES,))
        mask, e = carve(r2, e, (TILES, EXPERTS))
        before, e = carve(r2, e, (TILES + 1, EXPERTS))
        key, e = carve(r2, e, (TILES, EXPERTS))
        near8, e = carve(r2, e, (TILES, 8))
        filled, e = carve(r2, e, (EXPERTS, TOKENS // ROWS - 1))
        n_tiles, e = carve(r2, e, (EXPERTS,))
        tile_end, e = carve(r2, e, (EXPERTS,))
        row_base, e = carve(r2, e, (EXPERTS,))
        weight, e = carve(r2, e, (TILES, 8))
        tile_exp, e = carve(r2, e, (1,))
        tile_exp0, e = carve(r2, e, (1,), 1)
        ended, e = carve(r2, e, (EXPERTS,))
        sgl, e = carve(r2, e, (3, SEQ))
        shid, e = carve(r2, e, (3, SEQ))
        w1b, e = carve(r2, e, (LOOP_TILES, KC * EI))
        eT, e = carve(r2, e, (2, 2 * ROWS))
        hid, e = carve(r2, e, (2, 2 * ROWS))
        gath, _ = carve(r1, 0, (8, DIM))
        taken_pad, e = carve(r1, 4096, (TILES, EXPERTS + 2))
        eraw, e = carve(r1, e, (LOOP_TILES, 2 * DIM))
        ey, e = carve(r1, e, (2, 2 * DIM))
        w2b = w2buf[:]
        xb, e = carve(r2, 0, (KC, SEQ))
        xpad, e = carve(r2, e, (CH, SEQ + TAPS - 1))
        cv, e = carve(r2, e, (CH, SEQ))
        zs, e = carve(r2, e, (TB, DIN))
        bcd, e = carve(r2, e, (TB, BCD))
        dts, e = carve(r2, e, (8, TB * NH))
        xact, e = carve(r1, 0, (CH, SEQ))
        xa, e = carve(r1, e, (TB, DIN))
        AU, e = carve(r1, e, (NH, P))
        LT, e = carve(r1, e, (NH * P,))
        Gm, e = carve(r1, e, (P,))
        es, e = carve(r1, e, (TB, 3 * NH))
        BCT, e = carve(r1, e, (2, P), DST)
        xdisc, e = carve(r1, e, (DIN,))
        xdec, e = carve(r1, e, (DIN,))
        state, e = carve(r2, 9600, (DIN,), DST)
        ya, e = carve(r2, e, (DIN,))
        yb, e = carve(r2, e, (DIN,))
        yT, e = carve(r2, e, (CH, P))
        fsl, e = carve(r2, 0, (2, SEQ))
        fu, e = carve(r2, e, (2, SEQ))
        fhid, e = carve(r2, e, (len(FF_CHUNKS), SEQ))
        fo, e = carve(r2, e, (2, DIM))

        negmax = sb("negmax", [P, 16])
        rowsum = sb("rowsum", [P, 16])
        rrow = sb("rrow", [P, 16])

        bank = [ctx.enter_context(nc.psum_tensor(f"bank{i}", [P, 512], F32)) for i in range(8)]

        passed = {k: sem(f"passed_{k}") for k in ("act", "dve", "pe", "pool", "sp")}
        loads = {k: sem(f"load_{k}") for k in ("x", "tables", "prep", "attn", "ffn0", "mamba", "ffn1", "out")}
        stage_done = [sem(f"stage_done{i}") for i in range(9)]

        def hold(eng, who, s, value):
            eng.wait_ge(s, value).then_inc(passed[who], 1)

        def stage_end(eng, n):
            eng.drain().then_inc(stage_done[n], 1)

        def stage_start(eng, n, engines=4):
            if n:
                eng.wait_ge(stage_done[n - 1], engines)

        block = ctx.enter_context(nc.Block())

        n_load = {}

        def load(eng, key, dst, src):
            eng.dma_start(dst, src).then_inc(loads[key], 16)
            n_load[key] = n_load.get(key, 0) + 16

        def bcast(v, n):
            return v.rearrange("(o n) -> o n", o=1).broadcast_to([P, n])

        def issue_loads(sp):
            load(sp, "x", x[:], a["x"].rearrange("(t p) c -> p t c", p=P))
            load(sp, "tables", tables[:], a["tables"])
            load(sp, "prep", wqbT, a["w_qbT"])
            load(sp, "prep", wkvT, a["w_kvT"])
            load(sp, "prep", w_o, a["w_o"].rearrange("(h p) n -> p h n", p=P))
            load(sp, "attn", w_a[:], a["w_a"])
            load(sp, "attn", wqe1[:, :, KVL:QE], a["w_qr"][0:P])
            load(sp, "attn", wqe2[:, :, KVL:QE], a["w_qr"][P:QL])
            load(sp, "attn", qn1[:], a["q_norm"].rearrange("(p o) -> p o", o=1)[0:P])
            load(sp, "attn", qn2[:], a["q_norm"].rearrange("(p o) -> p o", o=1)[P:QL])
            load(sp, "attn", kvn[:], a["kv_norm"].rearrange("(p o) -> p o", o=1))
            load(sp, "ffn0", gateT[:], a["gateT"].rearrange("(k p) n -> p k n", p=P))
            load(sp, "ffn0", sguT[:], a["sguT"].rearrange("(k p) n -> p k n", p=P))
            for c, (lo, n) in enumerate(SH_CHUNKS):
                load(sp, "ffn0", sdT[0:n, c, :], a["sdT"][lo:lo + n, :])
            load(sp, "mamba", w_in[:], a["w_in"].rearrange("(k p) n -> p k n", p=P))
            load(sp, "mamba", conv_w[:], a["conv_w"].rearrange("(c p) t -> p c t", p=P))
            load(sp, "mamba", conv_b[:], a["conv_b"])
            load(sp, "mamba", w_out[:], a["w_out"].rearrange("(k p) n -> p k n", p=P))
            load(sp, "mamba", a_log[:], bcast(a["A_log"], NH))
            load(sp, "mamba", dt_bias[:], bcast(a["dt_bias"], NH))
            load(sp, "mamba", dskip[:], bcast(a["D_skip"], DIN))
            load(sp, "ffn1", fgT[:], a["fgT"].rearrange("(k p) n -> p k n", p=P))
            load(sp, "ffn1", fuT[:], a["fuT"].rearrange("(k p) n -> p k n", p=P))
            last = len(FF_CHUNKS) - 1
            n = FF_CHUNKS[last][1]
            load(sp, "ffn1", fdT[:, 0:last, :], a["fdT"][0:P * last, :].rearrange("(k p) n -> p k n", p=P))
            load(sp, "ffn1", fdT[0:n, last, :], a["fdT"][P * last:, :])
            for dst, src in ((gate_s, "gate_s"), (up_s, "up_s")):
                load(sp, "ffn1", dst[:], a[src])
            load(sp, "ffn1", down_s[:], bcast(a["down_s"], DIM))

        def loaded(eng, key):
            eng.wait_ge(loads[key], total_loads[key])

        total_loads = {"x": 16, "tables": 16, "prep": 48, "attn": 96, "ffn0": 80, "mamba": 112, "ffn1": 112}

        ln = {k: sem(f"ln_{k}") for k in ("stat", "var", "root", "xn", "tr")}

        def ln_vector(dve, n):
            for t in range(TILES):
                nc.vector.bn_stats(stats[:, t, :], x[:, t, :]).then_inc(ln["stat"], 1)
            for t in range(TILES):
                dve.wait_ge(ln["stat"], 2 * TILES * n + t + 1)
                nc.vector.bn_aggr(mv[:, t, :], stats[:, t, :]).then_inc(ln["stat"], 1)
            dve.wait_ge(ln["stat"], 2 * TILES * (n + 1))
            nc.vector.tensor_scalar(rvar[:], mv[:, :, 1], LN_EPS, None, ALU.add).then_inc(ln["var"], 1)
            dve.wait_ge(ln["var"], 2 * n + 1)
            nc.vector.reciprocal(rvar[:], rvar[:]).then_inc(ln["var"], 1)
            dve.wait_ge(ln["root"], n + 1)
            for t in range(TILES):
                nc.vector.tensor_scalar(xn[:, t, :], x[:, t, :], mv[:, t, 0:1], rstd[:, t:t + 1],
                                        ALU.subtract, ALU.mult).then_inc(ln["xn"], 1)
            for u in (1, 3, 5, 7):
                ln_evacuate(dve, nc.vector.tensor_copy, n, u)

        def ln_evacuate(eng, copy, n, u):
            eng.wait_ge(ln["tr"], 8 * n + u + 1)
            k, g = u % KC, u // KC
            copy(xnT[:, k, g * SEQ:(g + 1) * SEQ], bank[u][:])

        def ln_scalar(act, n):
            act.wait_ge(ln["var"], 2 * n + 2)
            nc.scalar.activation(rstd[:], rvar[:], ACT.Sqrt).then_inc(ln["root"], 1)
            for u in (0, 2, 4, 6):
                ln_evacuate(act, nc.scalar.copy, n, u)

        def ln_tensor(pe, n):
            for u in range(8):
                k, g = u % KC, u // KC
                pe.wait_ge(ln["xn"], TILES * n + TB * (g + 1))
                for i in range(TB):
                    last = nc.tensor.transpose(bank[u][:, i * P:(i + 1) * P],
                                               xn[:, TB * g + i, k * P:(k + 1) * P], ident)
                last.then_inc(ln["tr"], 1)

        prep_w = sem("prep_w")
        prep_ev = sem("prep_ev")
        consts = sem("consts")

        def prep_tensor(pe):
            loaded(pe, "prep")
            for h in range(HEADS):
                c = (h % 8) * KVL
                nc.tensor.matmul(bank[h // 8][:, c:c + KVL], wqbT[:, h, 0:P], wkvT[:, 0, h, :],
                                 start=True, stop=True)
                last = nc.tensor.matmul(bank[2 + h // 8][0:QL2, c:c + KVL], wqbT[:, h, P:QL], wkvT[:, 0, h, :],
                                        start=True, stop=True)
            last.then_inc(prep_w, 1)
            for h in range(HEADS):
                c = (h // 2 % 2) * DIM
                r = KVL * (h % 2)
                last = nc.tensor.matmul(bank[4 + h // 4][r:r + KVL, c:c + DIM], wkvT[:, 1, h, :], w_o[:, h, :],
                                        start=True, stop=True)
            last.then_inc(prep_w, 1)

        def prep_scalar(act):
            act.wait_ge(prep_w, 1)
            for m in range(2):
                for dst, b, n in ((wqe1, 0, P), (wqe2, 2, QL2)):
                    nc.scalar.copy(dst[:, 8 * m:8 * m + 8, 0:KVL],
                                   bank[b + m][0:n, :].rearrange("p (h c) -> p h c", h=8))
            act.wait_ge(prep_w, 2)
            for m in range(4):
                nc.scalar.copy(wvo[:, 2 * m:2 * m + 2, :], bank[4 + m][:].rearrange("p (h c) -> p h c", h=2))

        A = {k: sem(f"a_{k}") for k in
             ("proj", "sq", "ms", "root", "inv", "cq", "kr", "kv", "vt", "v",
              "q", "qs", "rope", "rope_v", "rope_w", "rope_a", "qt", "qte", "s", "max", "exp", "pt", "pte", "pv", "rr", "o",
              "ot", "ote", "y", "res")}
        NU = HG * TB

        Q_STEPS = (2, 5, 8, 11)

        def att_tensor(pe):
            def project(b):
                for m in range(3):
                    for k in range(KC):
                        last = nc.tensor.matmul(bank[m][:], w_a[:, k, m * P:(m + 1) * P],
                                                xnT[:, k, row_tokens(b)], start=(k == 0), stop=(k == KC - 1))
                    last.then_inc(A["proj"], 1)

            def mean_squares(b, n):
                if n == 0:
                    pe.wait_ge(A["sq"], 3 * b + 3)
                    nc.tensor.matmul(bank[5][:], ones[:], sq[:, 0, :], start=True, stop=False)
                    nc.tensor.matmul(bank[5][:], ones[0:QL2, :], sq[0:QL2, 1, :], start=False, stop=True)\
                        .then_inc(A["ms"], 1)
                else:
                    pe.wait_ge(A["inv"], 4 * b + 1)
                    nc.tensor.matmul(bank[5][:], ones[0:KVL, :], sq[0:KVL, 2, :], start=True, stop=True)\
                        .then_inc(A["ms"], 1)

            def row_values(b):
                hold(pe, "pe", A["kv"], b + 1)
                for i in range(TB):
                    last = nc.tensor.transpose(bank[5][:, i * KVL:(i + 1) * KVL],
                                               KT[0:KVL, i * P:(i + 1) * P], ident[0:KVL, 0:KVL])
                last.then_inc(A["vt"], 1)

            def first_queries(b):
                pe.wait_ge(A["cq"], 2 * b + 2)
                for i in range(TB):
                    if i >= 2:
                        pe.wait_ge(A["qs"], TB * GROUPS * b + i - 1 + START)
                    q_product(pe, b * GROUPS, 0, i, 7 - i % 2)
                pe.wait_ge(A["kr"], b + 1)
                pe.wait_ge(A["v"], b + 1)
                for i in range(TB):
                    if i % 2:
                        hold(pe, "pe", A["rope_v"], 2 * b + i // 2 + 1)
                    else:
                        hold(pe, "pe", A["rope"], ROPES * b + i // 2 + 1)
                    if i == 3:
                        hold(pe, "pe", A["qte"], TB * GROUPS * b + 1 + START)
                    q_transpose(pe, i)

            def output(b, i):
                for half in range(2):
                    hold(pe, "pe", A["ote"], 2 * TB * b + max(0, 2 * i + half - 1) + START)
                    for c in range(4):
                        cc = 4 * half + c
                        last = nc.tensor.transpose(bank[3 + half][:, c * P:(c + 1) * P],
                                                   O[:, i, cc * P:(cc + 1) * P], ident)
                    last.then_inc(A["ot"], 1)
                pe.wait_ge(A["ote"], 2 * TB * b + 2 * i + 2 + START)
                if i >= 2:
                    pe.wait_ge(A["res"], TB * b + i - 1 + START)
                for c in range(HEADS // 2):
                    last = nc.tensor.matmul(bank[6 + i % 2][:, 0:DIM], OT[:, i % 2, c * P:(c + 1) * P],
                                            wvo[:, c, :], start=(c == 0), stop=(c == HEADS // 2 - 1))
                last.then_inc(A["y"], 1)

            def row(b, with_next):
                with pe.Fori(0, GROUPS - 1) as hg:
                    group_tensor(pe, b * GROUPS + hg, ROPES * b + 2 + TB * hg, hg, True)
                group_tensor(pe, b * GROUPS + (GROUPS - 1), None, GROUPS - 1, False)
                if with_next:
                    project(b + 1)
                pe.wait_ge(A["o"], HEADS * b + HEADS)
                output(b, 0)
                if with_next:
                    mean_squares(b + 1, 0)
                output(b, 1)
                if with_next:
                    mean_squares(b + 1, 1)
                output(b, 2)
                output(b, 3)
                if with_next:
                    row_values(b + 1)
                if with_next:
                    pe.wait_ge(A["res"], TB * b + TB + START)
                    first_queries(b + 1)

            project(0)
            mean_squares(0, 0)
            mean_squares(0, 1)
            row_values(0)
            first_queries(0)
            with pe.Fori(0, BATCH - 1) as b:
                row(b, True)
            row(BATCH - 1, False)

        ROPES = 2 + TB * (GROUPS - 1)

        def row_tokens(b):
            return slice(b * SEQ, (b + 1) * SEQ) if isinstance(b, int) else bass.ds(b * SEQ, SEQ)

        def q_product(pe, g, hg, i, at):
            w1 = wqe1[:, bass.ds(hg * HG, HG), :].rearrange("p h c -> p (h c)") if not isinstance(hg, int) \
                else wqe1[:, hg * HG:(hg + 1) * HG, :].rearrange("p h c -> p (h c)")
            w2 = wqe2[:, bass.ds(hg * HG, HG), :].rearrange("p h c -> p (h c)") if not isinstance(hg, int) \
                else wqe2[:, hg * HG:(hg + 1) * HG, :].rearrange("p h c -> p (h c)")
            nc.tensor.matmul(bank[at][:], cq1[:, i * P:(i + 1) * P], w1, start=True, stop=False)
            nc.tensor.matmul(bank[at][:], cq2[:, i * P:(i + 1) * P], w2, start=False, stop=True)\
                .then_inc(A["q"], 1)

        def q_transpose(pe, i):
            for h in range(HG):
                last = nc.tensor.transpose(bank[(NU + i) % 3][:, h * P:(h + 1) * P],
                                           qs[:, i, h * QE:(h + 1) * QE], ident)
            last.then_inc(A["qt"], 1)

        def group_tensor(pe, g, roped, hg, with_next):
            def scores(u):
                h, i = u // TB, u % TB
                if u >= 3:
                    pe.wait_ge(A["exp"], NU * g + u - 2)
                if u < TB:
                    pe.wait_ge(A["qte"], TB * g + min(TB, i + 3) + START)
                n = (i + 1) * P
                nc.tensor.matmul(bank[u % 3][:, 0:n], QT[:, h, i * P:(i + 1) * P], KT[:, 0:n],
                                 start=True, stop=False)
                nc.tensor.matmul(bank[u % 3][:, i * P:n], identb[:], futureb[:], start=False, stop=True)\
                    .then_inc(A["s"], 1)

            def transposes(u):
                i = u % TB
                pe.wait_ge(A["exp"], NU * g + u + 1)
                if u >= 2:
                    hold(pe, "pe", A["pte"], NU * g + u - 1)
                for j in range(i + 1):
                    last = nc.tensor.transpose(bank[3 + u % 2][:, j * P:(j + 1) * P],
                                               prob[:, u % 4, j * P:(j + 1) * P], ident)
                last.then_inc(A["pt"], 1)

            def values(u):
                h, i = u // TB, u % TB
                pe.wait_ge(A["pte"], NU * g + u + 1)
                if i == 0 and h >= 2:
                    hold(pe, "pe", A["o"], HG * g + h - 1)
                for j in range(i + 1):
                    last = nc.tensor.matmul(bank[5 + h % 2][:, i * KVL:(i + 1) * KVL],
                                            probT[:, u % 2, j * P:(j + 1) * P], V[:, j, :],
                                            start=(j == 0), stop=(j == i))
                last.then_inc(A["pv"], 1)

            for u in range(NU + TB):
                if u < NU:
                    scores(u)
                elif with_next:
                    if u < NU + 3:
                        hold(pe, "pe", A["exp"], NU * g + u - 2)
                    else:
                        hold(pe, "pe", A["qte"], TB * (g + 1) + 1 + START)
                    hold(pe, "pe", A["rope"], roped + u - NU + 1)
                    q_transpose(pe, u - NU)
                if with_next and u in Q_STEPS:
                    pe.wait_ge(A["qs"], TB * (g + 1) + Q_STEPS.index(u) + START)
                    q_product(pe, g + 1, hg + 1, Q_STEPS.index(u), 7)
                if 2 <= u < NU + 2:
                    transposes(u - 2)
                if 3 <= u < NU + 3:
                    values(u - 3)

        def att_scalar(act):
            def squares(b):
                for m, n, width in ((0, P, QL), (1, QL2, QL), (2, KVL, KVL)):
                    act.wait_ge(A["proj"], 3 * b + m + 1)
                    nc.scalar.activation(sq[0:n, m, :], bank[m][0:n, :], ACT.Square,
                                         scale=1.0 / math.sqrt(width)).then_inc(A["sq"], 1)

            def root(b, n):
                act.wait_ge(A["inv"], 4 * b + 2 * n + 2)
                if n == 0:
                    nc.scalar.activation(rq, rq, ACT.Sqrt, scale=ATT_SCALE * ATT_SCALE).then_inc(A["root"], 1)
                else:
                    nc.scalar.activation(rk[0:KVL, :], rk[0:KVL, :], ACT.Sqrt).then_inc(A["root"], 1)

            def values(b):
                act.wait_ge(A["vt"], b + 1)
                nc.scalar.copy(V.rearrange("p i c -> p (i c)"), bank[5][:, 0:TB * KVL]).then_inc(A["v"], 1)

            def first_queries(b):
                for i in range(TB):
                    q_copy(act, b * GROUPS, i, 7 - i % 2)
                for i in range(TB):
                    qt_copy(act, b * GROUPS, i)

            def output(b, i):
                for half in range(2):
                    act.wait_ge(A["ot"], 2 * TB * b + 2 * i + half + 1)
                    if i >= 2:
                        act.wait_ge(A["y"], TB * b + i - 1)
                    nc.scalar.copy(OT[:, i % 2, 4 * half * P:4 * (half + 1) * P], bank[3 + half][:])\
                        .then_inc(A["ote"], 1)

            def row(b, with_next):
                with act.Fori(0, GROUPS - 1) as hg:
                    group_scalar(act, b * GROUPS + hg, True)
                group_scalar(act, b * GROUPS + (GROUPS - 1), False)
                if with_next:
                    squares(b + 1)
                output(b, 0)
                output(b, 1)
                if with_next:
                    root(b + 1, 0)
                output(b, 2)
                if with_next:
                    root(b + 1, 1)
                output(b, 3)
                if with_next:
                    values(b + 1)
                if with_next:
                    first_queries(b + 1)

            squares(0)
            root(0, 0)
            root(0, 1)
            values(0)
            first_queries(0)
            with act.Fori(0, BATCH - 1) as b:
                row(b, True)
            row(BATCH - 1, False)

        def q_copy(act, g, i, at=7):
            act.wait_ge(A["q"], TB * g + i + 1)
            nc.scalar.copy(qs[:, i, :], bank[at][:]).then_inc(A["qs"], 1)

        def qt_copy(act, g, i):
            act.wait_ge(A["qt"], TB * g + i + 1)
            nc.scalar.copy(QT[:, :, i * P:(i + 1) * P], bank[(NU + i) % 3][:].rearrange("p (h c) -> p h c", h=HG))\
                .then_inc(A["qte"], 1)

        def group_scalar(act, g, with_next):
            def exps(u):
                i = u % TB
                act.wait_ge(A["max"], NU * g + u + 1)
                if u >= 4:
                    act.wait_ge(A["pt"], NU * g + u - 3)
                nc.scalar.activation(prob[:, u % 4, 0:(i + 1) * P], bank[u % 3][:, 0:(i + 1) * P], ACT.Exp,
                                     bias=negmax[:, u:u + 1], scale=1.0,
                                     accum_out=rowsum[:, u:u + 1]).then_inc(A["exp"], 1)

            for u in range(NU + TB):
                if u < NU:
                    exps(u)
                elif with_next:
                    qt_copy(act, g + 1, u - NU)
                if with_next and u in Q_STEPS:
                    q_copy(act, g + 1, Q_STEPS.index(u))

        def att_vector(dve):
            def rope_keys(b):
                dve.wait_ge(A["proj"], 3 * b + 3)
                nc.vector.tensor_tensor(krope[KVL:QE, 0, :], bank[2][KVL:QE, :], cosk[KVL:QE, :], ALU.mult)\
                    .then_inc(A["rope_a"], 1)
                nc.vector.tensor_tensor(krope[KVL:QE, 1, :], bank[1][KVL:QE, :], sink[KVL:QE, :], ALU.mult)\
                    .then_inc(A["rope_a"], 1)
                dve.wait_ge(A["rope_a"], 2 * b + 2)
                nc.vector.tensor_tensor(KT[KVL:QE, :], krope[KVL:QE, 0, :], krope[KVL:QE, 1, :], ALU.add)\
                    .then_inc(A["kr"], 1)

            def inverse(b, n):
                r = rq if n == 0 else rk[0:KVL, :]
                dve.wait_ge(A["ms"], 2 * b + n + 1)
                nc.vector.tensor_scalar(r, bank[5][:] if n == 0 else bank[5][0:KVL, :], RMS_EPS, None, ALU.add)\
                    .then_inc(A["inv"], 1)
                dve.wait_ge(A["inv"], 4 * b + 2 * n + 1)
                nc.vector.reciprocal(r, r).then_inc(A["inv"], 1)

            def latents(b, n):
                dve.wait_ge(A["root"], 2 * b + n + 1)
                if n == 0:
                    dve.wait_ge(A["sq"], 3 * b + 3)
                    nc.vector.scalar_tensor_tensor(out=cq1, in0=bank[0][:], scalar=qn1[:], in1=rq,
                                                   op0=ALU.mult, op1=ALU.mult).then_inc(A["cq"], 1)
                    nc.vector.scalar_tensor_tensor(out=cq2, in0=bank[1][0:QL2, :], scalar=qn2[:],
                                                   in1=rq[0:QL2, :], op0=ALU.mult, op1=ALU.mult)\
                        .then_inc(A["cq"], 1)
                else:
                    nc.vector.scalar_tensor_tensor(out=KT[0:KVL, :], in0=bank[2][0:KVL, :], scalar=kvn[:],
                                                   in1=rk[0:KVL, :], op0=ALU.mult, op1=ALU.mult)\
                        .then_inc(A["kv"], 1)

            def first_ropes(b):
                for i in (1, 3):
                    hold(dve, "dve", A["qs"], TB * GROUPS * b + i + 1 + START)
                    rope(nc.vector, dve, "dve", i, A["rope_w"], 6 * b + 3 * (i // 2) + 3, A["rope_v"], qtmp_v)
                    hold(dve, "dve", A["rope_v"], 2 * b + i // 2 + 1)

            def residual(b, i):
                dve.wait_ge(A["y"], TB * b + i + 1)
                xt = x[:, bass.ds(b * TB + i, 1), :].rearrange("p o c -> p (o c)") if not isinstance(b, int) \
                    else x[:, b * TB + i, :]
                nc.vector.tensor_tensor(xt, bank[6 + i % 2][:, 0:DIM], xt, ALU.add).then_inc(A["res"], 1)

            def row(b, with_next):
                with dve.Fori(0, GROUPS - 1) as hg:
                    group_vector(dve, b * GROUPS + hg, hg)
                group_vector(dve, b * GROUPS + (GROUPS - 1), GROUPS - 1)
                if with_next:
                    rope_keys(b + 1)
                residual(b, 0)
                if with_next:
                    inverse(b + 1, 0)
                residual(b, 1)
                if with_next:
                    inverse(b + 1, 1)
                    latents(b + 1, 0)
                residual(b, 2)
                if with_next:
                    latents(b + 1, 1)
                residual(b, 3)
                if with_next:
                    first_ropes(b + 1)

            rope_keys(0)
            inverse(0, 0)
            latents(0, 0)
            inverse(0, 1)
            latents(0, 1)
            first_ropes(0)
            with dve.Fori(0, BATCH - 1) as b:
                row(b, True)
            row(BATCH - 1, False)

        def group_vector(dve, g, hg):
            def maximum(u):
                i = u % TB
                dve.wait_ge(A["s"], NU * g + u + 1)
                nc.vector.tensor_reduce(negmax[:, u:u + 1], bank[u % 3][:, 0:(i + 1) * P], axis=AX.X,
                                        op=ALU.max, negate=True).then_inc(A["max"], 1)

            def head_out(h):
                hold(dve, "dve", A["exp"], NU * g + TB * (h + 1))
                nc.vector.reciprocal(rrow[:, TB * h:TB * (h + 1)], rowsum[:, TB * h:TB * (h + 1)])\
                    .then_inc(A["rr"], 1)
                dve.wait_ge(A["rr"], HG * g + h + 1)
                dve.wait_ge(A["pv"], NU * g + TB * (h + 1))
                col = (hg * HG + h) * KVL
                dst = O[:, :, bass.ds(col, KVL)] if not isinstance(col, int) else O[:, :, col:col + KVL]
                nc.vector.tensor_tensor(dst,
                                        bank[5 + h % 2][:, 0:TB * KVL].rearrange("p (i c) -> p i c", i=TB),
                                        rrow[:, TB * h:TB * (h + 1)].unsqueeze(2).to_broadcast([P, TB, KVL]),
                                        ALU.mult).then_inc(A["o"], 1)

            def evacuate(u):
                i = u % TB
                dve.wait_ge(A["pt"], NU * g + u + 1)
                if u >= 2:
                    dve.wait_ge(A["pv"], NU * g + u - 1)
                nc.vector.tensor_copy(probT[:, u % 2, 0:(i + 1) * P], bank[3 + u % 2][:, 0:(i + 1) * P])\
                    .then_inc(A["pte"], 1)

            for u in range(NU + 4):
                if u < NU:
                    maximum(u)
                if 2 <= u < NU + 2:
                    evacuate(u - 2)
                if u >= 7 and (u - 7) % TB == 0:
                    head_out((u - 7) // TB)

        def rope(api, eng, who, i, parts_done, n_parts, done, tmp):
            q = qs[:, i, :].rearrange("p (h c) -> p h c", h=HG)
            ta = tmp[:, 0, :].rearrange("p (h c) -> p h c", h=HG)
            tb = tmp[:, 1, :].rearrange("p (h c) -> p h c", h=HG)
            half = DR // 2
            c = cosq[:, i, :].unsqueeze(1).to_broadcast([P, HG, DR])
            s1 = sinq[:, i, 0:half].unsqueeze(1).to_broadcast([P, HG, half])
            s2 = sinq[:, i, half:DR].unsqueeze(1).to_broadcast([P, HG, half])
            api.tensor_tensor(ta, q[:, :, KVL:QE], c, ALU.mult).then_inc(parts_done, 1)
            api.tensor_tensor(tb[:, :, 0:half], q[:, :, KVL + half:QE], s1, ALU.mult).then_inc(parts_done, 1)
            api.tensor_tensor(tb[:, :, half:DR], q[:, :, KVL:KVL + half], s2, ALU.mult).then_inc(parts_done, 1)
            hold(eng, who, parts_done, n_parts)
            api.tensor_tensor(q[:, :, KVL:QE], ta, tb, ALU.add).then_inc(done, 1)

        def att_pool(pool):
            def turn(b, n, copied, i):
                hold(pool, "pool", A["qs"], copied + START)
                rope(nc.gpsimd, pool, "pool", i, A["rope_a2"], 3 * ROPES * b + 3 * n + 3, A["rope"], qtmp)
                hold(pool, "pool", A["rope"], ROPES * b + n + 1)

            with pool.Fori(0, BATCH) as b:
                for i in (0, 2):
                    turn(b, i // 2, TB * GROUPS * b + i + 1, i)
                with pool.Fori(0, GROUPS - 1) as hg:
                    for i in range(TB):
                        turn(b, TB * hg + 2 + i, TB * GROUPS * b + TB * hg + TB + i + 1, i)

        A["rope_a2"] = sem("a_rope_parts")

        M = {k: sem(f"m_{k}") for k in
             ("lg", "step", "sub", "exp", "mask", "count", "slots", "ends", "row", "zero", "sent", "in", "tr", "trc",
              "up", "hid", "down", "ey", "out", "used", "sup", "ssil", "shid", "sdown", "sacc", "trips")}
        ZERO_PARTS = 4
        ZEROED = 1 + 16 * ZERO_PARTS
        MCREDIT = ("tr", "trc", "up", "hid", "down", "ey", "shid", "sdown", "sacc")
        loaded_tile = [sem(f"m_tile{j}") for j in range(LOOP_TILES)]
        gathered = [sem(f"m_gath{j}") for j in range(8)]

        def route_tensor(pe):
            for t in range(TILES):
                for k in range(KC):
                    last = nc.tensor.matmul(bank[t // 8][:, (t % 8) * EXPERTS:(t % 8 + 1) * EXPERTS],
                                            xnT[:, k, t * P:(t + 1) * P], gateT[:, k, :],
                                            start=(k == 0), stop=(k == KC - 1))
            last.then_inc(M["lg"], 1)

            pe.wait_ge(M["mask"], 1)
            for m in range(2):
                half = mask[:, 8 * m:8 * m + 8, :].rearrange("p t e -> p (t e)")
                nc.tensor.matmul(bank[m][:], le, half, start=True, stop=True)
                last = nc.tensor.matmul(bank[2 + m][:], ones[:], half, start=True, stop=True)
            last.then_inc(M["count"], 1)
            pe.wait_ge(M["ends"], 1)
            nc.tensor.transpose(bank[4][0:1, 0:P], tile_exp, ident).then_inc(M["row"], 1)

        def route_vector(dve):
            steps = [0]

            def step(ins):
                steps[0] += 1
                ins.then_inc(M["step"], 1)
                dve.wait_ge(M["step"], steps[0])

            V_ = nc.vector
            step(V_.memset(lgs[:, :, EXPERTS:EXPERTS + 2], -LOW))
            dve.wait_ge(M["lg"], 1)
            for m in range(2):
                step(V_.tensor_copy(lgs[:, 8 * m:8 * m + 8, 0:EXPERTS],
                                    bank[m][:].rearrange("p (t e) -> p t e", t=8)))
            for t in range(TILES):
                last = V_.max(top8[:, t, :], lgs[:, t, 0:EXPERTS])
            step(last)
            V_.tensor_tensor(comb, lgs[:, :, 0:EXPERTS], top8[:, :, 0:1].to_broadcast([P, TILES, EXPERTS]),
                             ALU.subtract).then_inc(M["sub"], 1)
            dve.wait_ge(M["sub"], 1)
            step(V_.memset(top8[:, :, TOPK:8], -LOW))
            for t in range(TILES):
                last = V_.match_replace(taken_pad[:, t, :], top8[:, t, :], lgs[:, t, :], LOW)
            step(last)
            V_.tensor_scalar(mask, taken_pad[:, :, 0:EXPERTS], 0.9 * LOW, None, ALU.is_lt).then_inc(M["mask"], 1)
            dve.wait_ge(M["mask"], 1)
            dve.wait_ge(M["count"], 1)
            step(V_.memset(before[:, 0, :], 0.0))
            for t in range(TILES):
                step(V_.tensor_tensor(before[:, t + 1, :], before[:, t, :],
                                      bank[2 + t // 8][:, (t % 8) * EXPERTS:(t % 8 + 1) * EXPERTS], ALU.add))
            step(V_.tensor_tensor(filled, before[:, TILES, :].unsqueeze(2).to_broadcast([P, EXPERTS, TOKENS // ROWS - 1]),
                                  full.unsqueeze(1).to_broadcast([P, EXPERTS, TOKENS // ROWS - 1]), ALU.is_gt))
            step(V_.tensor_reduce(n_tiles, filled, axis=AX.X, op=ALU.add))
            step(V_.tensor_scalar(n_tiles, n_tiles, 1.0, None, ALU.add))
            step(V_.tensor_tensor_scan(tile_end, ones[:, 0:EXPERTS], n_tiles, 0.0, ALU.mult, ALU.add))
            step(V_.tensor_scalar(ended, tile_end, partition, None, ALU.is_le))
            step(V_.tensor_reduce(tile_exp, ended, axis=AX.X, op=ALU.add))
            V_.tensor_scalar(tile_exp, tile_exp, EXPERTS - 1.0, None, ALU.min).then_inc(M["ends"], 1)
            step(V_.tensor_tensor(row_base, tile_end, n_tiles, ALU.subtract))
            step(V_.tensor_scalar(row_base, row_base, 1.0 * ROWS, None, ALU.mult))
            for m in range(2):
                step(V_.tensor_tensor(key[:, 8 * m:8 * m + 8, :], before[:, 8 * m:8 * m + 8, :],
                                      bank[m][:].rearrange("p (t e) -> p t e", t=8), ALU.add))
            step(V_.tensor_tensor(key, key, row_base.unsqueeze(1).to_broadcast([P, TILES, EXPERTS]), ALU.add))
            step(V_.tensor_scalar(key, key, -1.0, FAR + 1.0, ALU.mult, ALU.add))
            step(V_.tensor_tensor(key, key, mask, ALU.mult))
            for t in range(TILES):
                last = V_.max(near8[:, t, :], key[:, t, :])
            step(last)
            V_.tensor_scalar(slots[:], near8[:, :, 0:TOPK], -1.0, 1.0 * FAR, ALU.mult, ALU.add)\
                .then_inc(M["slots"], 1)
            marks = MAX_TILES // LOOP_TILES
            step(V_.tensor_tensor(ended[0:1, 0:marks], tile_end[0:1, EXPERTS - 1:EXPERTS].to_broadcast([1, marks]),
                                  loop_marks[0:1, :], ALU.is_gt))
            step(V_.tensor_reduce(tile_exp0, ended[0:1, 0:marks], axis=AX.X, op=ALU.add))
            step(V_.tensor_copy(trips[0:1, 0:1], tile_exp0))
            dve.wait_ge(M["row"], 1)
            V_.tensor_copy(tile_row[:], bank[4][0:1, 0:P]).then_inc(M["trips"], 1)
            dve.wait_ge(M["trips"], 1)
            dve.wait_ge(M["exp"], 1)
            step(V_.tensor_tensor(taken, mask, comb, ALU.mult))
            step(V_.tensor_reduce(rsum, taken, axis=AX.X, op=ALU.add))
            step(V_.reciprocal(rsum, rsum))
            step(V_.tensor_tensor(comb, taken, rsum.unsqueeze(2).to_broadcast([P, TILES, EXPERTS]), ALU.mult))
            for k in range(TOPK):
                step(V_.tensor_tensor(taken, key, near8[:, :, k:k + 1].to_broadcast([P, TILES, EXPERTS]),
                                      ALU.is_equal))
                step(V_.tensor_tensor(taken, taken, comb, ALU.mult))
                step(V_.tensor_reduce(weight[:, :, k], taken, axis=AX.X, op=ALU.add))

        def route_scalar(act):
            act.wait_ge(M["sub"], 1)
            nc.scalar.activation(comb, comb, ACT.Exp).then_inc(M["exp"], 1)

        def send_pool(pool):
            pool.wait_ge(M["slots"], 1)
            pool.wait_ge(M["zero"], ZEROED)
            for t in range(TILES):
                for k in range(TOPK):
                    nc.gpsimd.indirect_dma_start(
                        sent[:, :], bass.IndirectOffsetOnAxis(ap=slots[:, t, k:k + 1], axis=0),
                        xn[:, t, :], None).then_inc(M["sent"], 16)

        def return_pool(pool):
            pool.wait_ge(M["out"], 1)
            for t in range(TILES):
                for k in range(TOPK):
                    n = t * TOPK + k
                    if n >= 8:
                        pool.wait_ge(M["used"], n - 7)
                    nc.gpsimd.indirect_dma_start(
                        gath[:, n % 8, :], None, returned[:, :],
                        bass.IndirectOffsetOnAxis(ap=slots[:, t, k:k + 1], axis=0)).then_inc(gathered[n % 8], 16)

        def return_vector(dve):
            dve.wait_ge(M["sacc"], TILES + START)
            for t in range(TILES):
                for k in range(TOPK):
                    n = t * TOPK + k
                    dve.wait_ge(gathered[n % 8], 16 * (n // 8 + 1))
                    if k:
                        dve.wait_ge(M["used"], n)
                    nc.vector.scalar_tensor_tensor(out=x[:, t, :], in0=gath[:, n % 8, :],
                                                   scalar=weight[:, t, k:k + 1], in1=x[:, t, :],
                                                   op0=ALU.mult, op1=ALU.add).then_inc(M["used"], 1)

        LT4 = LOOP_TILES

        def steps_of(eng):
            eng.wait_ge(M["trips"], 1)
            return eng.value_load(trips[0:1, 0:1], min_val=EXPERTS // LT4, max_val=MAX_TILES // LT4)

        def experts_sp(sp):
            steps = steps_of(sp)
            sp.wait_ge(M["sent"], 16 * TILES * TOPK)
            with sp.Fori(0, steps) as it:
                for j in range(LT4):
                    e = sp.value_load(tile_row[0:1, bass.ds(it * LT4 + j, 1)], min_val=0, max_val=EXPERTS - 1)
                    sp.wait_ge(M["tr"], LT4 * it + j + 1 - LT4 + START)
                    sp.wait_ge(M["down"], LT4 * it + j + 1 - LT4 + START)
                    sp.dma_start(eraw[:, j, :].rearrange("p (o c) -> p o c", o=2),
                                 sent[bass.ds((it * LT4 + j) * ROWS, ROWS), :].rearrange("(o p) c -> p o c", p=P))\
                        .then_inc(loaded_tile[j], 16)
                    sp.dma_start(w1b[:, j, :], a["w1T"][bass.ds(e, 1), :, :]
                                 .rearrange("o p n -> p (o n)")).then_inc(loaded_tile[j], 16)
                    sp.dma_start(w2b[:, j, :], a["w2T"][bass.ds(e, 1), :, :]
                                 .rearrange("o p n -> p (o n)")).then_inc(loaded_tile[j], 16)

        def experts_tensor(pe):
            steps = steps_of(pe)
            pe.wait_ge(M["sacc"], TILES + START)
            with pe.Fori(0, steps) as it:
                def turn(j):
                    hold(pe, "pe", loaded_tile[j], 48 * it + 48)
                    hold(pe, "pe", M["trc"], LT4 * it + max(0, j - 1) + START)
                    for k in range(KC):
                        for half in range(2):
                            c = (2 * k + half) * P
                            last = nc.tensor.transpose(bank[j % 2][:, c:c + P],
                                                       eraw[:, j, half * DIM + k * P:half * DIM + (k + 1) * P], ident)
                    last.then_inc(M["tr"], 1)

                def up(j):
                    pe.wait_ge(M["trc"], LT4 * it + j + 1 + START)
                    pe.wait_ge(M["hid"], LT4 * it + max(0, j - 1) + START)
                    for c in range(2):
                        for k in range(KC):
                            last = nc.tensor.matmul(bank[2 + j % 2][0:EH, c * ROWS:(c + 1) * ROWS],
                                                    w1b[:, j, k * EI + c * EH:k * EI + (c + 1) * EH],
                                                    eT[:, j % 2, k * ROWS:(k + 1) * ROWS],
                                                    start=(k == 0), stop=(k == KC - 1))
                    last.then_inc(M["up"], 1)

                def down(j):
                    pe.wait_ge(M["hid"], LT4 * it + j + 1 + START)
                    pe.wait_ge(M["ey"], LT4 * it + max(0, j - 1) + START)
                    for half in range(2):
                        for c in range(2):
                            last = nc.tensor.matmul(bank[4 + j % 2][:, half * DIM:(half + 1) * DIM],
                                                    hid[0:EH, j % 2, c * ROWS + half * P:c * ROWS + (half + 1) * P],
                                                    w2b[:, j, c * DIM:(c + 1) * DIM],
                                                    start=(c == 0), stop=(c == 1))
                    last.then_inc(M["down"], 1)

                turn(0)
                turn(1)
                up(0)
                for j in range(1, LT4):
                    up(j)
                    down(j - 1)
                    if j + 1 < LT4:
                        turn(j + 1)
                down(LT4 - 1)

        def experts_scalar(act):
            steps = steps_of(act)
            with act.Fori(0, steps) as it:
                def store(j):
                    act.wait_ge(M["ey"], LT4 * it + j + 1 + START)
                    act.dma_start(returned[bass.ds((it * LT4 + j) * ROWS, ROWS), :].rearrange("(o p) c -> p o c", p=P),
                                  ey[:, j % 2, :].rearrange("p (o c) -> p o c", o=2)).then_inc(stored[j % 2], 16)

                for j in range(LT4):
                    act.wait_ge(M["up"], LT4 * it + j + 1 + START)
                    act.wait_ge(M["down"], LT4 * it + max(0, j - 1) + START)
                    nc.scalar.activation(hid[0:EH, j % 2, :], bank[2 + j % 2][0:EH, :], ACT.Silu)\
                        .then_inc(M["hid"], 1)
                    if j:
                        store(j - 1)
                store(LT4 - 1)
            for p in range(2):
                hold(act, "act", stored[p], 16 * (LT4 // 2) * steps + 16)
            act.wait_ge(M["exp"], 1)
            act.sem_inc(M["out"], 1)

        stored = [sem(f"m_stored{p}") for p in range(2)]

        def experts_vector(dve):
            steps = steps_of(dve)
            with dve.Fori(0, steps) as it:
                def turned(j):
                    dve.wait_ge(M["tr"], LT4 * it + j + 1 + START)
                    hold(dve, "dve", M["up"], LT4 * it + max(0, j - 1) + START)
                    nc.vector.tensor_copy(eT[:, j % 2, :], bank[j % 2][:]).then_inc(M["trc"], 1)

                def result(j):
                    dve.wait_ge(M["down"], LT4 * it + j + 1 + START)
                    hold(dve, "dve", stored[j % 2], 16 * (LT4 // 2) * it + 16 * (j // 2) + 16)
                    nc.vector.tensor_copy(ey[:, j % 2, :], bank[4 + j % 2][:]).then_inc(M["ey"], 1)

                turned(0)
                turned(1)
                for j in range(1, LT4):
                    result(j - 1)
                    if j + 1 < LT4:
                        turned(j + 1)
                result(LT4 - 1)

        def shared_tensor(pe):
            with pe.Fori(0, BATCH) as g:
                pe.wait_ge(M["sacc"], TB * g + START)
                n = 0
                for c, (lo, w) in enumerate(SH_CHUNKS):
                    for half in range(2):
                        for k in range(KC):
                            last = nc.tensor.matmul(bank[3 * half + c][0:w, :],
                                                    sguT[:, k, SHI * half + lo:SHI * half + lo + w],
                                                    xnT[:, k, bass.ds(g * SEQ, SEQ)],
                                                    start=(k == 0), stop=(k == KC - 1))
                        last.then_inc(M["sup"], 1)
                pe.wait_ge(M["shid"], 3 * g + 3 + START)
                for i in range(TB):
                    if i >= 2:
                        pe.wait_ge(M["sacc"], TB * g + i - 1 + START)
                    for c, (lo, w) in enumerate(SH_CHUNKS):
                        last = nc.tensor.matmul(bank[6 + i % 2][:, 0:DIM], shid[0:w, c, i * P:(i + 1) * P],
                                                sdT[0:w, c, :], start=(c == 0), stop=(c == 2))
                    last.then_inc(M["sdown"], 1)

        def shared_scalar(act):
            with act.Fori(0, BATCH) as g:
                for c, (lo, w) in enumerate(SH_CHUNKS):
                    act.wait_ge(M["sup"], 6 * g + 2 * c + 1)
                    act.wait_ge(M["shid"], 3 * g + START)
                    nc.scalar.activation(sgl[0:w, c, :], bank[c][0:w, :], ACT.Silu).then_inc(M["ssil"], 1)

        def shared_vector(dve):
            with dve.Fori(0, BATCH) as g:
                for c, (lo, w) in enumerate(SH_CHUNKS):
                    dve.wait_ge(M["sup"], 6 * g + 2 * c + 2)
                    dve.wait_ge(M["ssil"], 3 * g + c + 1)
                    dve.wait_ge(M["sdown"], TB * g + START)
                    nc.vector.tensor_tensor(shid[0:w, c, :], bank[3 + c][0:w, :], sgl[0:w, c, :], ALU.mult)\
                        .then_inc(M["shid"], 1)
                for i in range(TB):
                    dve.wait_ge(M["sdown"], TB * g + i + 1 + START)
                    xt = x[:, bass.ds(g * TB + i, 1), :].rearrange("p o c -> p (o c)")
                    nc.vector.tensor_tensor(xt, bank[6 + i % 2][:, 0:DIM], xt, ALU.add).then_inc(M["sacc"], 1)

        S = {k: sem(f"s_{k}") for k in
             ("aneg", "pad", "xb", "br", "brc", "tap", "conv", "act", "z", "zs", "bcd", "bcde", "d1", "d2", "d3", "d4",
              "dexp", "dln", "adt", "xt", "xte", "bct", "bcte", "cum", "es", "au", "seg", "lt", "g", "gm",
              "mt", "xd1", "xd", "yo", "st0", "st", "y1", "y2", "y3", "y4", "yt", "yte", "out", "res")}
        SCREDIT = ("xb", "conv", "act", "brc", "zs", "bcde", "res", "xte", "bcte", "yte", "es", "gm", "lt", "y1", "y2",
                   "yo", "st", "mt", "y4", "seg", "cum", "out", "xt", "bct", "br", "adt", "yt", "au")
        draw, dmin, dexp, dw, dln, dpos, dsel, dtv = (dts[:, n, :] for n in range(8))

        def ssm_pool(pool):
            for c in range(CH):
                nc.gpsimd.memset(xpad[:, c, 0:TAPS - 1], 0.0).then_inc(S["pad"], 1)
            with pool.Fori(0, BATCH) as b:
                hold(pool, "pool", S["res"], TB * b + START)
                nc.gpsimd.tensor_copy(xb, xnT[:, :, bass.ds(b * SEQ, SEQ)]).then_inc(S["xb"], 1)
                for i in range(TB):
                    n = TB * b + i
                    hold(pool, "pool", S["adt"], b + 1 + START)
                    hold(pool, "pool", S["seg"], n + START)
                    nc.gpsimd.tensor_tensor(AU, le.unsqueeze(1).to_broadcast([P, NH, P]),
                                            adt3[:, i, :].unsqueeze(2).to_broadcast([P, NH, P]), ALU.mult)\
                        .then_inc(S["au"], 1)
                    hold(pool, "pool", S["xte"], n + 1 + START)
                    hold(pool, "pool", S["st"], n + START)
                    nc.gpsimd.tensor_tensor(heads(xdisc), heads(xa[:, i, :]),
                                            dtv3[:, i, :].unsqueeze(2).to_broadcast([P, NH, HD]), ALU.mult)\
                        .then_inc(S["xd1"], 1)
                    hold(pool, "pool", S["xd1"], n + 1)
                    hold(pool, "pool", S["es"], n + 1 + START)
                    nc.gpsimd.tensor_tensor(heads(xdec), heads(xdisc),
                                            es[:, i, NH:2 * NH].unsqueeze(2).to_broadcast([P, NH, HD]), ALU.mult)\
                        .then_inc(S["xd"], 1)

        def heads(ap):
            return ap.rearrange("p (h c) -> p h c", h=NH)

        dtv3 = dtv.rearrange("p (i h) -> p i h", i=TB)
        adt3 = dsel.rearrange("p (i h) -> p i h", i=TB)

        def ssm_tensor(pe):
            with pe.Fori(0, BATCH) as b:
                for c in range(CH):
                    pe.wait_ge(S["brc"], CH * b + START)
                    for k in range(KC):
                        last = nc.tensor.matmul(bank[c][:], w_in[:, k, c * P:(c + 1) * P],
                                                xnT[:, k, bass.ds(b * SEQ, SEQ)], start=(k == 0), stop=(k == KC - 1))
                    last.then_inc(S["br"], 1)
                pe.wait_ge(S["xb"], b + 1 + START)
                for i in range(TB):
                    n = TB * b + i
                    pe.wait_ge(S["zs"], TB * b + max(0, i - 1) + START)
                    for k in range(KC):
                        last = nc.tensor.matmul(bank[4 + i % 2][:], xb[:, k, i * P:(i + 1) * P],
                                                w_in[:, k, DIN:2 * DIN], start=(k == 0), stop=(k == KC - 1))
                    last.then_inc(S["z"], 1)
                    pe.wait_ge(S["bcde"], TB * b + max(0, i - 1) + START)
                    for k in range(KC):
                        last = nc.tensor.matmul(bank[6 + i % 2][:, 0:BCD], xb[:, k, i * P:(i + 1) * P],
                                                w_in[:, k, 2 * DIN:PROJ], start=(k == 0), stop=(k == KC - 1))
                    last.then_inc(S["bcd"], 1)
                def part1(i):
                    n = TB * b + i
                    if i == 0:
                        pe.wait_ge(S["bcde"], TB * (b + 1) + START)
                        pe.wait_ge(S["zs"], TB * (b + 1) + START)
                    hold(pe, "pe", S["act"], CH * b + CH + START)
                    hold(pe, "pe", S["yte"], n - min(i, 1) + START)
                    for c in range(CH):
                        last = nc.tensor.transpose(bank[6][:, c * P:(c + 1) * P], xact[:, c, i * P:(i + 1) * P], ident)
                    last.then_inc(S["xt"], 1)
                    hold(pe, "pe", S["gm"], n + START)
                    for m in range(2):
                        last = nc.tensor.transpose(bank[0][0:DST, m * P:(m + 1) * P],
                                                   bcd[:, i, m * DST:(m + 1) * DST], ident)
                    last.then_inc(S["bct"], 1)
                    pe.wait_ge(S["adt"], b + 1 + START)
                    pe.wait_ge(S["res"], n - min(i, 1) + START)
                    for m, w in enumerate((le, gt, ones[:])):
                        last = nc.tensor.matmul(bank[7][:, m * NH:(m + 1) * NH], w, adt3[:, i, :],
                                                start=True, stop=True)
                    last.then_inc(S["cum"], 1)
                    pe.wait_ge(S["au"], n + 1 + START)
                    pe.wait_ge(S["lt"], 2 * n + START)
                    for m in range(2):
                        last = nc.tensor.matmul(bank[1 + m][:], gt, AU[:, 4 * m:4 * m + 4, :]
                                                .rearrange("p h l -> p (h l)"), start=True, stop=True)
                    last.then_inc(S["seg"], 1)
                    pe.wait_ge(S["bcte"], n + 1 + START)
                    nc.tensor.matmul(bank[0][:, 0:P], BCT[:, 0, :], BCT[:, 1, :], start=True, stop=True)\
                        .then_inc(S["g"], 1)

                def part2(i):
                    n = TB * b + i
                    pe.wait_ge(S["st"], n + START)
                    if i:
                        nc.tensor.matmul(bank[4][:], BCT[:, 1, :], state, start=True, stop=True).then_inc(S["yo"], 1)
                    pe.wait_ge(S["xd"], n + 1)
                    nc.tensor.matmul(bank[5][0:DST, :], bcd[:, i, 0:DST], xdec, start=True, stop=True)\
                        .then_inc(S["st0"], 1)
                    pe.wait_ge(S["y2"], n + START)
                    pe.wait_ge(S["mt"], n + 1 + START)
                    for h in range(NH):
                        last = nc.tensor.matmul(bank[3][:, h * HD:(h + 1) * HD], LT[:, h * P:(h + 1) * P],
                                                xdisc[:, h * HD:(h + 1) * HD], start=True, stop=True)
                    last.then_inc(S["y1"], 1)

                def part3(i):
                    n = TB * b + i
                    hold(pe, "pe", S["y4"], n + 1 + START)
                    hold(pe, "pe", S["xte"], TB * b + min(TB, i + 2) + START)
                    hold(pe, "pe", S["yte"], n + START)
                    for c in range(CH):
                        last = nc.tensor.transpose(bank[6][:, c * P:(c + 1) * P], ya[:, c * P:(c + 1) * P], ident)
                    last.then_inc(S["yt"], 1)
                    pe.wait_ge(S["yte"], n + 1 + START)
                    pe.wait_ge(S["es"], TB * b + min(TB, i + 2) + START)
                    for c in range(CH):
                        last = nc.tensor.matmul(bank[7][:, 0:DIM], yT[:, c, :], w_out[:, c, :],
                                                start=(c == 0), stop=(c == CH - 1))
                    last.then_inc(S["out"], 1)

                part1(0)
                for i in range(TB):
                    part2(i)
                    if i + 1 < TB:
                        part1(i + 1)
                    part3(i)

        def ssm_scalar(act):
            with act.Fori(0, BATCH) as b:
                for c in range(CH):
                    hold(act, "act", S["br"], CH * b + c + 1 + START)
                    hold(act, "act", S["conv"], CH * b + START)
                    nc.scalar.copy(xpad[:, c, TAPS - 1:SEQ + TAPS - 1], bank[c][:]).then_inc(S["brc"], 1)
                for i in range(TB):
                    act.wait_ge(S["z"], TB * b + i + 1)
                    nc.scalar.activation(zs[:, i, :], bank[4 + i % 2][:], ACT.Silu).then_inc(S["zs"], 1)
                for c in range(CH):
                    act.wait_ge(S["conv"], CH * b + c + 1 + START)
                    nc.scalar.activation(xact[:, c, :], cv[:, c, :], ACT.Silu, bias=conv_b[:, c:c + 1])\
                        .then_inc(S["act"], 1)
                act.wait_ge(S["d1"], b + 1)
                nc.scalar.activation(dexp, dmin, ACT.Exp).then_inc(S["dexp"], 1)
                act.wait_ge(S["d2"], b + 1)
                nc.scalar.activation(dln, dw, ACT.Ln).then_inc(S["dln"], 1)

                def part1(i):
                    n = TB * b + i
                    act.wait_ge(S["xt"], n + 1 + START)
                    nc.scalar.copy(xa[:, i, :], bank[6][:]).then_inc(S["xte"], 1)
                    act.wait_ge(S["bct"], n + 1 + START)
                    nc.scalar.copy(BCT.rearrange("p m l -> p (m l)"), bank[0][0:DST, 0:2 * P]).then_inc(S["bcte"], 1)
                    act.wait_ge(S["cum"], n + 1 + START)
                    nc.scalar.activation(es[:, i, :], bank[7][:, 0:3 * NH], ACT.Exp).then_inc(S["es"], 1)
                    act.wait_ge(S["seg"], n + 1 + START)
                    act.wait_ge(S["y1"], n + START)
                    for m in range(2):
                        nc.scalar.activation(LT[:, m * 4 * P:(m + 1) * 4 * P], bank[1 + m][:], ACT.Exp)\
                            .then_inc(S["lt"], 1)

                part1(0)
                for i in range(TB):
                    if i + 1 < TB:
                        part1(i + 1)
                    act.wait_ge(S["yt"], TB * b + i + 1 + START)
                    nc.scalar.copy(yT.rearrange("p c l -> p (c l)"), bank[6][:]).then_inc(S["yte"], 1)

        def ssm_vector(dve):
            dve.wait_ge(S["aneg"], 1)
            nc.vector.tensor_scalar(a_neg[:], a_neg[:], -1.0, None, ALU.mult).then_inc(S["aneg"], 1)
            dve.wait_ge(S["aneg"], 2)
            dve.wait_ge(S["pad"], CH)
            with dve.Fori(0, BATCH) as b:
                for c in range(CH):
                    dve.wait_ge(S["brc"], CH * b + c + 1 + START)
                    dve.wait_ge(S["act"], CH * b + START)
                    nc.vector.tensor_scalar(cv[:, c, :], xpad[:, c, 0:SEQ], conv_w[:, c, 0:1], None, ALU.mult)\
                        .then_inc(S["tap"], 1)

                def tap(m):
                    for c in range(CH):
                        dve.wait_ge(S["tap"], (TAPS - 1) * CH * b + CH * (m - 1) + c + 1)
                        ins = nc.vector.scalar_tensor_tensor(out=cv[:, c, :], in0=xpad[:, c, m:m + SEQ],
                                                             scalar=conv_w[:, c, m:m + 1], in1=cv[:, c, :],
                                                             op0=ALU.mult, op1=ALU.add)
                        ins.then_inc(S["tap"] if m < TAPS - 1 else S["conv"], 1)

                def take_bcd(i):
                    dve.wait_ge(S["bcd"], TB * b + i + 1)
                    nc.vector.tensor_copy(bcd[:, i, :], bank[6 + i % 2][:, 0:BCD]).then_inc(S["bcde"], 1)

                tap(1)
                take_bcd(0)
                take_bcd(1)
                tap(2)
                take_bcd(2)
                take_bcd(3)
                dve.wait_ge(S["bcde"], TB * (b + 1) + START)
                nc.vector.tensor_tensor(draw.rearrange("p (i h) -> p i h", i=TB), bcd[:, :, 2 * DST:BCD],
                                        dt_bias[:].unsqueeze(1).to_broadcast([P, TB, NH]), ALU.add)\
                    .then_inc(S["d3"], 1)
                dve.wait_ge(S["d3"], 5 * b + 1)
                nc.vector.scalar_tensor_tensor(out=dmin, in0=draw, scalar=-1.0, in1=draw,
                                               op0=ALU.mult, op1=ALU.min).then_inc(S["d1"], 1)
                nc.vector.tensor_scalar(dpos, draw, 0.0, None, ALU.max).then_inc(S["d3"], 1)
                tap(3)
                dve.wait_ge(S["dexp"], b + 1)
                nc.vector.tensor_scalar(dw, dexp, 1.0, None, ALU.add).then_inc(S["d2"], 1)
                dve.wait_ge(S["d2"], b + 1)
                nc.vector.tensor_scalar(dmin, dw, -1.0, 1e-30, ALU.add, ALU.max).then_inc(S["d4"], 1)
                dve.wait_ge(S["d4"], 4 * b + 1)
                nc.vector.reciprocal(dmin, dmin).then_inc(S["d4"], 1)
                dve.wait_ge(S["d4"], 4 * b + 2)
                nc.vector.tensor_tensor(dmin, dmin, dexp, ALU.mult).then_inc(S["d4"], 1)
                dve.wait_ge(S["dln"], b + 1)
                dve.wait_ge(S["d4"], 4 * b + 3)
                nc.vector.tensor_tensor(dmin, dmin, dln, ALU.mult).then_inc(S["d4"], 1)
                nc.vector.scalar_tensor_tensor(out=draw, in0=dw, scalar=1.0, in1=dexp,
                                               op0=ALU.is_equal, op1=ALU.mult).then_inc(S["d3"], 1)
                dve.wait_ge(S["d4"], 4 * b + 4)
                dve.wait_ge(S["d3"], 5 * b + 2)
                nc.vector.tensor_tensor(dpos, dpos, dmin, ALU.add).then_inc(S["d3"], 1)
                dve.wait_ge(S["d3"], 5 * b + 4)
                nc.vector.tensor_tensor(dtv, dpos, draw, ALU.add).then_inc(S["d3"], 1)
                dve.wait_ge(S["d3"], 5 * b + 5)
                nc.vector.tensor_tensor(adt3, dtv3, a_neg[:].unsqueeze(1).to_broadcast([P, TB, NH]), ALU.mult)\
                    .then_inc(S["adt"], 1)

                def decays(i):
                    n = TB * b + i
                    dve.wait_ge(S["g"], n + 1)
                    nc.vector.tensor_tensor(Gm, bank[0][:, 0:P], le, ALU.mult).then_inc(S["gm"], 1)
                    dve.wait_ge(S["lt"], 2 * n + 2 + START)
                    dve.wait_ge(S["gm"], n + 1 + START)
                    lt3 = LT.rearrange("p (h l) -> p h l", h=NH)
                    nc.vector.tensor_tensor(lt3, lt3, Gm.unsqueeze(1).to_broadcast([P, NH, P]), ALU.mult)\
                        .then_inc(S["mt"], 1)

                def outputs(i):
                    n = TB * b + i
                    dve.wait_ge(S["st0"], n + 1)
                    if i:
                        dve.wait_ge(S["yo"], (TB - 1) * b + i + START)
                        nc.vector.tensor_tensor(heads(state), heads(state),
                                                es[0:DST, i, 2 * NH:3 * NH].unsqueeze(2).to_broadcast([DST, NH, HD]),
                                                ALU.mult).then_inc(S["tap2"], 1)
                        dve.wait_ge(S["tap2"], (TB - 1) * b + i)
                        nc.vector.tensor_tensor(state, state, bank[5][0:DST, :], ALU.add).then_inc(S["st"], 1)
                    else:
                        nc.vector.tensor_copy(state, bank[5][0:DST, :]).then_inc(S["st"], 1)
                    dve.wait_ge(S["xte"], n + 1 + START)
                    hold(dve, "dve", S["yt"], n + START)
                    nc.vector.tensor_tensor(ya, xa[:, i, :], dskip[:], ALU.mult).then_inc(S["y3"], 1)
                    if i:
                        dve.wait_ge(S["es"], n + 1 + START)
                        nc.vector.tensor_tensor(heads(yb), heads(bank[4][:]),
                                                es[:, i, 0:NH].unsqueeze(2).to_broadcast([P, NH, HD]), ALU.mult)\
                            .then_inc(S["y3"], 1)
                        dve.wait_ge(S["y3"], YC * b + 3 * i + 0)
                        nc.vector.tensor_tensor(ya, ya, yb, ALU.add).then_inc(S["y3"], 1)
                    dve.wait_ge(S["y1"], n + 1 + START)
                    dve.wait_ge(S["y3"], YC * b + 3 * i + 1)
                    nc.vector.tensor_tensor(ya, ya, bank[3][:], ALU.add).then_inc(S["y2"], 1)
                    dve.wait_ge(S["y2"], n + 1 + START)
                    nc.vector.tensor_tensor(ya, ya, zs[:, i, :], ALU.mult).then_inc(S["y4"], 1)

                def residual(i):
                    n = TB * b + i
                    dve.wait_ge(S["out"], n + 1 + START)
                    xt = x[:, bass.ds(b * TB + i, 1), :].rearrange("p o c -> p (o c)")
                    nc.vector.tensor_tensor(xt, bank[7][:, 0:DIM], xt, ALU.add).then_inc(S["res"], 1)

                decays(0)
                for i in range(TB):
                    outputs(i)
                    if i + 1 < TB:
                        decays(i + 1)
                    residual(i)

        YC = 1 + 3 * (TB - 1)
        S["tap2"] = sem("s_tap2")

        F = {k: sem(f"f_{k}") for k in ("gate", "up", "sil", "hid", "down", "sc", "res")}
        FCREDIT = ("hid", "down", "res", "sil")
        NF = len(FF_CHUNKS)

        def ff_tensor(pe):
            with pe.Fori(0, BATCH) as g:
                for c, (lo, w) in enumerate(FF_CHUNKS):
                    hold(pe, "pe", F["hid"], NF * g + max(0, c - 1) + START)
                    for k in range(KC):
                        last = nc.tensor.matmul(bank[c % 2][0:w, :], fgT[:, k, lo:lo + w],
                                                xnT[:, k, bass.ds(g * SEQ, SEQ)], start=(k == 0), stop=(k == KC - 1))
                    last.then_inc(F["gate"], 1)
                    for k in range(KC):
                        last = nc.tensor.matmul(bank[2 + c % 2][0:w, :], fuT[:, k, lo:lo + w],
                                                xnT[:, k, bass.ds(g * SEQ, SEQ)], start=(k == 0), stop=(k == KC - 1))
                    last.then_inc(F["up"], 1)
                for i in range(TB):
                    pe.wait_ge(F["hid"], NF * g + NF + START)
                    pe.wait_ge(F["res"], TB * g + START)
                    for c, (lo, w) in enumerate(FF_CHUNKS):
                        last = nc.tensor.matmul(bank[4 + i][:, 0:DIM], fhid[0:w, c, i * P:(i + 1) * P],
                                                fdT[0:w, c, :], start=(c == 0), stop=(c == NF - 1))
                    last.then_inc(F["down"], 1)

        def ff_scalar(act):
            with act.Fori(0, BATCH) as g:
                for c, (lo, w) in enumerate(FF_CHUNKS):
                    act.wait_ge(F["gate"], NF * g + c + 1)
                    act.wait_ge(F["hid"], NF * g + max(0, c - 1) + START)
                    nc.scalar.activation(fsl[0:w, c % 2, :], bank[c % 2][0:w, :], ACT.Silu,
                                         scale=gate_s[0:w, c:c + 1]).then_inc(F["sil"], 1)

        def ff_vector(dve):
            with dve.Fori(0, BATCH) as g:
                for c, (lo, w) in enumerate(FF_CHUNKS):
                    dve.wait_ge(F["up"], NF * g + c + 1)
                    dve.wait_ge(F["sil"], NF * g + c + 1 + START)
                    dve.wait_ge(F["down"], TB * g + START)
                    nc.vector.scalar_tensor_tensor(out=fhid[0:w, c, :], in0=bank[2 + c % 2][0:w, :],
                                                   scalar=up_s[0:w, c:c + 1], in1=fsl[0:w, c % 2, :],
                                                   op0=ALU.mult, op1=ALU.mult).then_inc(F["hid"], 1)
                for i in range(TB):
                    dve.wait_ge(F["down"], TB * g + i + 1 + START)
                    dve.wait_ge(F["res"], TB * g + max(0, i - 1) + START)
                    nc.vector.tensor_tensor(fo[:, i % 2, :], bank[4 + i][:, 0:DIM], down_s[:], ALU.mult)\
                        .then_inc(F["sc"], 1)
                    dve.wait_ge(F["sc"], TB * g + i + 1)
                    xt = x[:, bass.ds(g * TB + i, 1), :].rearrange("p o c -> p (o c)")
                    nc.vector.tensor_tensor(xt, fo[:, i % 2, :], xt, ALU.add).then_inc(F["res"], 1)

        @block.sync
        def _(sp):
            issue_loads(sp)
            assert n_load == total_loads, n_load
            sp.wait_ge(M["zero"], 1)
            per = MAX_TILES * ROWS // P // ZERO_PARTS
            for n in range(ZERO_PARTS):
                sp.dma_start(sent[n * per * P:(n + 1) * per * P, :].rearrange("(p r) c -> p r c", r=per),
                             zeros[:].unsqueeze(1).to_broadcast([P, per, DIM])).then_inc(M["zero"], 16)
            if STAGES >= 5:
                experts_sp(sp)
            sp.wait_ge(stage_done[LAST], 4)
            sp.dma_start(out.rearrange("(t p) c -> p t c", p=P), x[:]).then_inc(loads["out"], 16)
            sp.wait_ge(loads["out"], 16)

        @block.gpsimd
        def _(pool):
            for s in [A[k] for k in ("res", "qs", "qte", "ote")] + [M[k] for k in MCREDIT]:
                pool.sem_inc(s, START)
            for s in [S[k] for k in SCREDIT] + [F[k] for k in FCREDIT]:
                pool.sem_inc(s, START)
            for s in stored:
                pool.sem_inc(s, 16)
            nc.gpsimd.memset(zeros[:], 0.0).then_inc(M["zero"], 1)
            nc.gpsimd.memset(ones[:], 1.0).then_inc(consts, 1)
            loaded(pool, "tables")
            nc.gpsimd.tensor_copy(identb[:], ident).then_inc(consts, 1)
            nc.gpsimd.tensor_copy(futureb[:], future).then_inc(consts, 1)
            stage_end(pool, 0)
            stage_end(pool, 1)
            stage_start(pool, 2)
            att_pool(pool)
            stage_end(pool, 2)
            stage_end(pool, 3)
            stage_start(pool, 4)
            if STAGES >= 5:
                send_pool(pool)
                return_pool(pool)
            stage_end(pool, 4)
            stage_end(pool, 5)
            if STAGES >= 7:
                stage_start(pool, 6)
                ssm_pool(pool)
                stage_end(pool, 6)
                stage_end(pool, 7)
                stage_end(pool, 8)

        @block.scalar
        def _(act):
            loaded(act, "attn")
            prep_scalar(act)
            stage_end(act, 0)
            stage_start(act, 1)
            ln_scalar(act, 0)
            stage_end(act, 1)
            stage_start(act, 2)
            att_scalar(act)
            stage_end(act, 2)
            stage_start(act, 3)
            ln_scalar(act, 1)
            stage_end(act, 3)
            stage_start(act, 4)
            if STAGES >= 5:
                route_scalar(act)
                shared_scalar(act)
                experts_scalar(act)
            stage_end(act, 4)
            if STAGES >= 7:
                stage_start(act, 5)
                ln_scalar(act, 2)
                loaded(act, "mamba")
                nc.scalar.activation(a_neg[:], a_log[:], ACT.Exp).then_inc(S["aneg"], 1)
                stage_end(act, 5)
                stage_start(act, 6)
                ssm_scalar(act)
                stage_end(act, 6)
            if STAGES >= 9:
                stage_start(act, 7)
                ln_scalar(act, 3)
                loaded(act, "ffn1")
                stage_end(act, 7)
                stage_start(act, 8)
                ff_scalar(act)
                stage_end(act, 8)

        @block.vector
        def _(dve):
            loaded(dve, "x")
            stage_end(dve, 0)
            stage_start(dve, 1)
            ln_vector(dve, 0)
            stage_end(dve, 1)
            stage_start(dve, 2)
            att_vector(dve)
            stage_end(dve, 2)
            stage_start(dve, 3)
            ln_vector(dve, 1)
            stage_end(dve, 3)
            stage_start(dve, 4)
            if STAGES >= 5:
                route_vector(dve)
                shared_vector(dve)
                experts_vector(dve)
                return_vector(dve)
            stage_end(dve, 4)
            if STAGES >= 7:
                stage_start(dve, 5)
                ln_vector(dve, 2)
                stage_end(dve, 5)
                stage_start(dve, 6)
                loaded(dve, "mamba")
                ssm_vector(dve)
                stage_end(dve, 6)
            if STAGES >= 9:
                stage_start(dve, 7)
                ln_vector(dve, 3)
                stage_end(dve, 7)
                stage_start(dve, 8)
                loaded(dve, "ffn1")
                ff_vector(dve)
                stage_end(dve, 8)

        @block.tensor
        def _(pe):
            prep_tensor(pe)
            stage_end(pe, 0)
            stage_start(pe, 1)
            loaded(pe, "tables")
            ln_tensor(pe, 0)
            stage_end(pe, 1)
            stage_start(pe, 2)
            att_tensor(pe)
            stage_end(pe, 2)
            stage_start(pe, 3)
            ln_tensor(pe, 1)
            stage_end(pe, 3)
            stage_start(pe, 4)
            if STAGES >= 5:
                loaded(pe, "ffn0")
                route_tensor(pe)
                pe.wait_ge(M["trips"], 1)
                shared_tensor(pe)
                experts_tensor(pe)
            stage_end(pe, 4)
            if STAGES >= 7:
                stage_start(pe, 5)
                ln_tensor(pe, 2)
                stage_end(pe, 5)
                stage_start(pe, 6)
                loaded(pe, "mamba")
                ssm_tensor(pe)
                stage_end(pe, 6)
            if STAGES >= 9:
                stage_start(pe, 7)
                ln_tensor(pe, 3)
                stage_end(pe, 7)
                stage_start(pe, 8)
                loaded(pe, "ffn1")
                ff_tensor(pe)
                stage_end(pe, 8)


STAGES = 9
LAST = STAGES - 1 if STAGES > 4 else 4


def shape_tables():
    r = np.arange(P)
    ident = np.eye(P, dtype=np.float32)
    future = np.where(r[None, :] > r[:, None], -1e30, 0.0)
    le = (r[:, None] <= r[None, :]).astype(np.float32)
    gt = (r[:, None] > r[None, :]).astype(np.float32)
    f = np.float32
    pos2 = np.arange(0, DR, 2, dtype=f)
    inv = f(1.0) / np.power(f(10000.0), pos2 / f(DR)).astype(f)
    wavelen = f(2.0 * np.pi) / inv
    ramp = np.clip((f(1024) / wavelen - f(1.0)) / f(3.0), f(0), f(1)).astype(f)
    inv = (inv * (f(1.0) - ramp) + inv / f(16.0) * ramp).astype(f)
    freqs = np.outer(np.arange(SEQ, dtype=f), inv).astype(f)
    emb = np.concatenate([freqs, freqs], axis=-1)
    factor = f(0.1 * math.log(16.0) + 1.0)
    cos, sin = np.cos(emb) * factor, np.sin(emb) * factor
    sin[:, :DR // 2] *= -1
    tok = [t.reshape(TB, P, DR).transpose(1, 0, 2).reshape(P, TB * DR) for t in (cos, sin)]
    feat = [np.concatenate([np.zeros((KVL, SEQ)), t.T], axis=0) for t in (cos, sin)]
    marks = [r[:, None]] + [np.tile(ROWS * np.arange(1, TOKENS // ROWS), (P, 1)),
                            np.tile(LOOP_TILES * np.arange(MAX_TILES // LOOP_TILES), (P, 1))]
    return np.concatenate([ident, future, le, gt, *tok, *feat, *marks], axis=1).astype(f)


def lay_out(i):
    c = np.ascontiguousarray
    w_qb = i["L0_attn_w_qb"].reshape(QL, HEADS, DN + DR)
    w_kvb = i["L0_attn_w_kvb"].reshape(KVL, HEADS, 2, DN)
    w_qa, w_kva = i["L0_attn_w_qa"], i["L0_attn_w_kva"]
    kr = w_kva[:, KVL:]
    w_a = np.concatenate([w_qa, kr[:, DR // 2:], kr[:, :DR // 2], w_kva], axis=1)
    columns = lambda v: c(np.pad(v, (0, P * len(FF_CHUNKS) - INTER)).reshape(len(FF_CHUNKS), P).T)
    return {
        "x": c(i["L0_attn_x"].reshape(TOKENS, DIM)),
        "tables": shape_tables(),
        "w_qbT": c(w_qb[:, :, :DN].transpose(2, 1, 0)),
        "w_qr": c(w_qb[:, :, DN:]),
        "w_kvT": c(w_kvb.transpose(3, 2, 1, 0)),
        "w_o": c(i["L0_attn_w_o"]),
        "w_a": c(w_a.reshape(KC, P, 3 * P).transpose(1, 0, 2)),
        "q_norm": c(i["L0_attn_q_norm_w"]),
        "kv_norm": c(i["L0_attn_kv_norm_w"]),
        "gateT": c(i["L0_ffn_gate_w"].T),
        "w1T": c(i["L0_ffn_experts_w1"].transpose(0, 2, 1).reshape(EXPERTS, KC, P, EI).transpose(0, 2, 1, 3)
                 .reshape(EXPERTS, P, KC * EI)),
        "w2T": c(i["L0_ffn_experts_w2"].transpose(0, 2, 1).reshape(EXPERTS, 2, EH, DIM).transpose(0, 2, 1, 3)
                 .reshape(EXPERTS, EH, 2 * DIM)),
        "sguT": c(i["L0_ffn_shared_gate_up"].T),
        "sdT": c(i["L0_ffn_shared_down"].T),
        "w_in": c(i["L1_attn_in_proj_w"].T),
        "conv_w": c(i["L1_attn_conv_w"].reshape(DIN, TAPS)),
        "conv_b": c(i["L1_attn_conv_b"].reshape(CH, P).T),
        "w_out": c(i["L1_attn_out_proj_w"].T),
        "A_log": c(i["L1_attn_A_log"]),
        "dt_bias": c(i["L1_attn_dt_bias"]),
        "D_skip": c(i["L1_attn_D_skip"]),
        "fgT": c(i["L1_ffn_gate_w"].T),
        "fuT": c(i["L1_ffn_up_w"].T),
        "fdT": c(i["L1_ffn_down_w"].T),
        "gate_s": columns(i["L1_ffn_gate_s"]),
        "up_s": columns(i["L1_ffn_up_s"]),
        "down_s": c(i["L1_ffn_down_s"]),
    }


def kernel(**inputs):
    import concourse.bacc as bacc
    from concourse.bass_utils import run_bass_kernel_spmd

    nc = bacc.Bacc("TRN2", target_bir_lowering=False, num_devices=1)
    arrays = lay_out({k: np.asarray(v) for k, v in inputs.items()})
    args = {k: nc.dram_tensor(k + "_dram", v.shape, F32, kind="ExternalInput").ap() for k, v in arrays.items()}
    out = nc.dram_tensor("out_dram", (TOKENS, DIM), F32, kind="ExternalOutput").ap()
    build(nc, args, out)
    r = run_bass_kernel_spmd(nc, [{k + "_dram": v for k, v in arrays.items()}], core_ids=[0])
    return r.results[0]["out_dram"].reshape(BATCH, SEQ, DIM)
```

```python
import math
from contextlib import ExitStack

import numpy as np

import concourse.bass as bass
from concourse import mybir

F32 = mybir.dt.float32
BF16 = mybir.dt.bfloat16
ALU = mybir.AluOpType
ACT = mybir.ActivationFunctionType
AX = mybir.AxisListType

P = 128
BATCH, SEQ, DIM = 4, 512, 256
TOKENS = BATCH * SEQ
TILES = TOKENS // P
TB = SEQ // P
KC = DIM // P
HEADS, DN, DR, DV = 16, 128, 64, 128
QL, KVL = 192, 64
QL2 = QL - P
QE = KVL + DR
HG = 4
GROUPS = HEADS // HG
EXPERTS, EI, TOPK = 64, 176, 6
EH = EI // 2
ROWS = 2 * P
MAX_TILES = TOKENS * TOPK // ROWS + EXPERTS
LOOP_TILES = 4
FAR = 32768
SHI = 352
SH_CHUNKS = [(0, 128), (128, 128), (256, 96)]
DIN, DST, NH, HD, TAPS = 512, 64, 8, 64, 4
CH = DIN // P
PROJ = 2 * DIN + 2 * DST + NH
BCD = 2 * DST + NH
INTER = 704
FF_CHUNKS = [(128 * i, min(128, INTER - 128 * i)) for i in range((INTER + 127) // 128)]
ATT_SCALE = 1.0 / math.sqrt(DN + DR)
RMS_EPS, LN_EPS = 1e-6, 1e-5
START = 4
LOW = -3e38


N_MARKS = TOKENS // ROWS + MAX_TILES // LOOP_TILES


def build(nc, a, out):
    ctx = ExitStack()
    with ctx:
        def sb(name, shape, dt=F32):
            return ctx.enter_context(nc.sbuf_tensor(name, shape, dt))

        def sem(name):
            return ctx.enter_context(nc.semaphore(name))

        x = sb("x", [P, TILES, DIM])
        xnT = sb("xnT", [P, KC, TOKENS])
        tables = sb("tables", [P, 4 * P + TB * DR * 2 + 2 * SEQ + N_MARKS])
        ident = tables[:, 0:P]
        future = tables[:, P:2 * P]
        le = tables[:, 2 * P:3 * P]
        gt = tables[:, 3 * P:4 * P]
        o = 4 * P
        cosq = tables[:, o:o + TB * DR].rearrange("p (i d) -> p i d", i=TB)
        sinq = tables[:, o + TB * DR:o + 2 * TB * DR].rearrange("p (i d) -> p i d", i=TB)
        o += 2 * TB * DR
        cosk = tables[:, o:o + SEQ]
        sink = tables[:, o + SEQ:o + 2 * SEQ]
        o += 2 * SEQ
        partition = tables[:, o:o + 1]
        full = tables[:, o + 1:o + TOKENS // ROWS]
        loop_marks = tables[:, o + TOKENS // ROWS:o + N_MARKS]
        ones = sb("ones", [P, P])
        identb = sb("identb", [P, P], BF16)
        futureb = sb("futureb", [P, P], BF16)
        stats = sb("stats", [P, TILES, 6])
        mv = sb("mv", [P, TILES, 2])
        rstd = sb("rstd", [P, TILES])
        rvar = sb("rvar", [P, TILES])

        w_a = sb("w_a", [P, KC, 3 * P])
        qn1 = sb("qn1", [P, 1])
        qn2 = sb("qn2", [QL2, 1])
        kvn = sb("kvn", [KVL, 1])
        wvo = sb("wvo", [P, HEADS // 2, DIM])
        gateT = sb("gateT", [P, KC, EXPERTS])
        sguT = sb("sguT", [P, KC, 2 * SHI])
        sdT = sb("sdT", [P, 3, DIM])
        w_in = sb("w_in", [P, KC, PROJ])
        conv_w = sb("conv_w", [P, CH, TAPS])
        conv_b = sb("conv_b", [P, CH])
        w_out = sb("w_out", [P, CH, DIM])
        a_neg = sb("a_neg", [P, NH])
        a_log = sb("a_log", [P, NH])
        dt_bias = sb("dt_bias", [P, NH])
        dskip = sb("dskip", [P, DIN])
        fgT = sb("fgT", [P, KC, INTER])
        fuT = sb("fuT", [P, KC, INTER])
        fdT = sb("fdT", [P, len(FF_CHUNKS), DIM])
        gate_s = sb("gate_s", [P, len(FF_CHUNKS)])
        up_s = sb("up_s", [P, len(FF_CHUNKS)])
        down_s = sb("down_s", [P, DIM])

        r1 = sb("r1", [P, 9472])
        r2 = sb("r2", [P, 14336])
        w2buf = sb("w2buf", [P, LOOP_TILES * 2 * DIM])
        weight = sb("weight", [P, TILES, TOPK])
        row_slots = sb("row_slots", [P, TB, TOPK], mybir.dt.uint32)
        row_weight = sb("row_weight", [P, TB, TOPK])
        zeros = sb("zeros", [P, DIM])
        slots = sb("slots", [P, TILES, TOPK], mybir.dt.uint32)
        tile_row = sb("tile_row", [1, P], mybir.dt.int32)
        trips = sb("trips", [1, 2], mybir.dt.int32)
        sent = nc.dram_tensor("sent", (MAX_TILES * ROWS, DIM), F32).ap()
        returned = sent

        def carve(arena, at, shape, parts=P):
            n = int(np.prod(shape))
            ap = arena[0:parts, at:at + n]
            if len(shape) == 2:
                ap = ap.rearrange("p (a b) -> p a b", a=shape[0])
            if len(shape) == 3:
                ap = ap.rearrange("p (a b c) -> p a b c", a=shape[0], b=shape[1])
            return ap, at + n

        wqbT, e = carve(r1, 0, (HEADS, QL))
        wkvT, e = carve(r1, e, (2, HEADS, KVL))
        w_o, e = carve(r1, e, (HEADS, DIM))
        xn, _ = carve(r1, 0, (TILES, DIM))
        O, e = carve(r1, 0, (TB, HEADS * KVL))
        QT, e = carve(r1, e, (HG, SEQ))
        probT, e = carve(r1, e, (2, SEQ))
        prob, e = carve(r1, e, (4, SEQ))
        wqe1, e = carve(r2, 0, (HEADS, QE))
        wqe2, e = carve(r2, e, (HEADS, QE), QL2)
        cq1, e = carve(r2, e, (SEQ,))
        cq2, e = carve(r2, e, (SEQ,), QL2)
        KT, e = carve(r2, e, (SEQ,))
        V, e = carve(r2, e, (TB, KVL))
        OT, e = carve(r2, e, (2, HEADS // 2 * P))
        sq, e = carve(r2, e, (3, SEQ))
        rq, e = carve(r2, e, (SEQ,))
        rk, e = carve(r2, e, (SEQ,))
        krope, e = carve(r2, e, (2, SEQ))
        qs, e = carve(r2, e, (TB, HG * QE))
        qtmp, e = carve(r2, e, (2, HG * DR))
        qtmp_v = krope.rearrange("p a b -> p (a b)")[:, 0:2 * HG * DR].rearrange("p (a b) -> p a b", a=2)
        lgs, e = carve(r2, 0, (TILES, EXPERTS + 2))
        taken, e = carve(r2, e, (TILES, EXPERTS))
        comb, e = carve(r2, e, (TILES, EXPERTS))
        top8, e = carve(r2, e, (TILES, 8))
        rsum, e = carve(r2, e, (TILES,))
        mask, e = carve(r2, e, (TILES, EXPERTS))
        before, e = carve(r2, e, (TILES + 1, EXPERTS))
        key, e = carve(r2, e, (TILES, EXPERTS))
        near8, e = carve(r2, e, (TILES, 8))
        filled, e = carve(r2, e, (EXPERTS, TOKENS // ROWS - 1))
        n_tiles, e = carve(r2, e, (EXPERTS,))
        tile_end, e = carve(r2, e, (EXPERTS,))
        row_base, e = carve(r2, e, (EXPERTS,))
        tile_exp, e = carve(r2, e, (1,))
        tile_exp0, e = carve(r2, e, (1,), 1)
        ended, e = carve(r2, e, (EXPERTS,))
        sgl, e = carve(r2, e, (3, SEQ))
        shid, e = carve(r2, e, (3, SEQ))
        w1b, e = carve(r2, e, (LOOP_TILES, KC * EI))
        eT, e = carve(r2, e, (2, 2 * ROWS))
        hid, e = carve(r2, e, (2, 2 * ROWS))
        taken_pad, e = carve(r1, 4096, (TILES, EXPERTS + 2))
        eraw, e = carve(r1, e, (LOOP_TILES, 2 * DIM))
        ey, e = carve(r1, e, (2, 2 * DIM))
        w2b, _ = carve(w2buf, 0, (LOOP_TILES, 2 * DIM), EH)
        gath, e = carve(w2buf, 0, (8, DIM))
        xnr, _ = carve(r2, 12288, (TB, DIM))
        xb, e = carve(r2, 0, (KC, SEQ))
        xpad, e = carve(r2, e, (CH, SEQ + TAPS - 1))
        cv, e = carve(r2, e, (CH, SEQ))
        zs, e = carve(r2, e, (TB, DIN))
        bcd, e = carve(r2, e, (TB, BCD))
        dts, e = carve(r2, e, (8, TB * NH))
        xact, e = carve(r1, 0, (CH, SEQ))
        xa, e = carve(r1, e, (TB, DIN))
        AU, e = carve(r1, e, (NH, P))
        LT, e = carve(r1, e, (NH * P,))
        Gm, e = carve(r1, e, (P,))
        es, e = carve(r1, e, (TB, 3 * NH))
        BCT, e = carve(r1, e, (2, P), DST)
        xdisc, e = carve(r1, e, (DIN,))
        xdec, e = carve(r1, e, (DIN,))
        state, e = carve(r2, 9600, (DIN,), DST)
        ya, e = carve(r2, e, (DIN,))
        yb, e = carve(r2, e, (DIN,))
        yT, e = carve(r2, e, (CH, P))
        fsl, e = carve(r2, 0, (2, SEQ))
        fu, e = carve(r2, e, (2, SEQ))
        fhid, e = carve(r2, e, (len(FF_CHUNKS), SEQ))
        fo, e = carve(r2, e, (2, DIM))

        negmax = sb("negmax", [P, 16])
        rowsum = sb("rowsum", [P, 16])
        rrow = sb("rrow", [P, 16])

        bank = [ctx.enter_context(nc.psum_tensor(f"bank{i}", [P, 512], F32)) for i in range(8)]

        passed = {k: sem(f"passed_{k}") for k in ("act", "dve", "pe", "pool", "sp")}
        loads = {k: sem(f"load_{k}") for k in ("x", "tables", "prep", "attn", "ffn0", "mamba", "ffn1", "out")}
        stage_done = [sem(f"stage_done{i}") for i in range(4)]

        def hold(eng, who, s, value):
            eng.wait_ge(s, value).then_inc(passed[who], 1)

        def stage_end(eng, n):
            eng.drain().then_inc(stage_done[n % 4], 1)

        def stage_start(eng, n, engines=4):
            if n:
                eng.wait_ge(stage_done[(n - 1) % 4], engines * ((n - 1) // 4 + 1))

        block = ctx.enter_context(nc.Block())

        n_load = {}

        def load(eng, key, dst, src):
            eng.dma_start(dst, src).then_inc(loads[key], 16)
            n_load[key] = n_load.get(key, 0) + 16

        def bcast(v, n):
            return v.rearrange("(o n) -> o n", o=1).broadcast_to([P, n])

        def issue_loads(sp):
            load(sp, "prep", wqbT, a["w_qbT"])
            load(sp, "prep", wkvT, a["w_kvT"])
            load(sp, "prep", w_o, a["w_o"].rearrange("(h p) n -> p h n", p=P))
            load(sp, "x", x[:], a["x"].rearrange("(t p) c -> p t c", p=P))
            load(sp, "tables", tables[:], a["tables"])
            load(sp, "attn", w_a[:], a["w_a"])
            load(sp, "attn", wqe1[:, :, KVL:QE], a["w_qr"][0:P])
            load(sp, "attn", wqe2[:, :, KVL:QE], a["w_qr"][P:QL])
            load(sp, "attn", qn1[:], a["q_norm"].rearrange("(p o) -> p o", o=1)[0:P])
            load(sp, "attn", qn2[:], a["q_norm"].rearrange("(p o) -> p o", o=1)[P:QL])
            load(sp, "attn", kvn[:], a["kv_norm"].rearrange("(p o) -> p o", o=1))
            load(sp, "ffn0", gateT[:], a["gateT"].rearrange("(k p) n -> p k n", p=P))
            load(sp, "ffn0", sguT[:], a["sguT"].rearrange("(k p) n -> p k n", p=P))
            for c, (lo, n) in enumerate(SH_CHUNKS):
                load(sp, "ffn0", sdT[0:n, c, :], a["sdT"][lo:lo + n, :])
            load(sp, "mamba", w_in[:], a["w_in"].rearrange("(k p) n -> p k n", p=P))
            load(sp, "mamba", conv_w[:], a["conv_w"].rearrange("(c p) t -> p c t", p=P))
            load(sp, "mamba", conv_b[:], a["conv_b"])
            load(sp, "mamba", w_out[:], a["w_out"].rearrange("(k p) n -> p k n", p=P))
            load(sp, "mamba", a_log[:], bcast(a["A_log"], NH))
            load(sp, "mamba", dt_bias[:], bcast(a["dt_bias"], NH))
            load(sp, "mamba", dskip[:], bcast(a["D_skip"], DIN))
            load(sp, "ffn1", fgT[:], a["fgT"].rearrange("(k p) n -> p k n", p=P))
            load(sp, "ffn1", fuT[:], a["fuT"].rearrange("(k p) n -> p k n", p=P))
            last = len(FF_CHUNKS) - 1
            n = FF_CHUNKS[last][1]
            load(sp, "ffn1", fdT[:, 0:last, :], a["fdT"][0:P * last, :].rearrange("(k p) n -> p k n", p=P))
            load(sp, "ffn1", fdT[0:n, last, :], a["fdT"][P * last:, :])
            for dst, src in ((gate_s, "gate_s"), (up_s, "up_s")):
                load(sp, "ffn1", dst[:], a[src])
            load(sp, "ffn1", down_s[:], bcast(a["down_s"], DIM))

        def loaded(eng, key):
            eng.wait_ge(loads[key], total_loads[key])

        total_loads = {"x": 16, "tables": 16, "prep": 48, "attn": 96, "ffn0": 80, "mamba": 112, "ffn1": 112}

        ln = {k: sem(f"ln_{k}") for k in ("stat", "var", "root", "xn", "tr", "row")}

        def rounds(n):
            return n if n < 3 else n - 1 + BATCH

        def ln_stats(dve, n):
            for t in range(TILES):
                nc.vector.bn_stats(stats[:, t, :], x[:, t, :]).then_inc(ln["stat"], 1)
            for t in range(TILES):
                dve.wait_ge(ln["stat"], 2 * TILES * n + t + 1)
                nc.vector.bn_aggr(mv[:, t, :], stats[:, t, :]).then_inc(ln["stat"], 1)
            dve.wait_ge(ln["stat"], 2 * TILES * (n + 1))
            nc.vector.tensor_scalar(rvar[:], mv[:, :, 1], LN_EPS, None, ALU.add).then_inc(ln["var"], 1)
            dve.wait_ge(ln["var"], 2 * rounds(n) + 1)
            nc.vector.reciprocal(rvar[:], rvar[:]).then_inc(ln["var"], 1)

        def ln_vector(dve, n):
            dve.wait_ge(ln["root"], rounds(n) + 1)
            for t in range(TILES):
                nc.vector.tensor_scalar(xn[:, t, :], x[:, t, :], mv[:, t, 0:1], rstd[:, t:t + 1],
                                        ALU.subtract, ALU.mult).then_inc(ln["xn"], 1)
            for u in (1, 3, 5, 7):
                ln_evacuate(dve, nc.vector.tensor_copy, n, u)

        def ln_evacuate(eng, copy, n, u):
            eng.wait_ge(ln["tr"], 8 * n + u + 1)
            k, g = u % KC, u // KC
            copy(xnT[:, k, g * SEQ:(g + 1) * SEQ], bank[u][:])

        def ln_scalar(act, n):
            act.wait_ge(ln["var"], 2 * rounds(n) + 2)
            nc.scalar.activation(rstd[:], rvar[:], ACT.Sqrt).then_inc(ln["root"], 1)
            for u in (0, 2, 4, 6):
                ln_evacuate(act, nc.scalar.copy, n, u)

        def ln_tensor(pe, n):
            for u in range(8):
                k, g = u % KC, u // KC
                pe.wait_ge(ln["xn"], TILES * n + TB * (g + 1))
                for i in range(TB):
                    last = nc.tensor.transpose(bank[u][:, i * P:(i + 1) * P],
                                               xn[:, TB * g + i, k * P:(k + 1) * P], ident)
                last.then_inc(ln["tr"], 1)

        def lnr_stats(dve, b):
            hold(dve, "dve", M["used"], TOPK * TB * (b + 1) + START)
            for i in range(TB):
                nc.vector.bn_stats(stats[:, i, :], row_of_x(b * TB + i)).then_inc(ln["stat"], 1)
            hold(dve, "dve", ln["stat"], 4 * TILES + 2 * TB * b + TB)
            for i in range(TB):
                nc.vector.bn_aggr(mv[:, i, :], stats[:, i, :]).then_inc(ln["stat"], 1)
            dve.wait_ge(ln["stat"], 4 * TILES + 2 * TB * b + 2 * TB)
            nc.vector.tensor_scalar(rvar[:, 0:TB], mv[:, 0:TB, 1], LN_EPS, None, ALU.add).then_inc(ln["var"], 1)
            dve.wait_ge(ln["var"], 2 * b + 5)
            nc.vector.reciprocal(rvar[:, 0:TB], rvar[:, 0:TB]).then_inc(ln["var"], 1)

        def lnr_root(act, b):
            act.wait_ge(ln["var"], 2 * b + 6)
            nc.scalar.activation(rstd[:, 0:TB], rvar[:, 0:TB], ACT.Sqrt).then_inc(ln["root"], 1)

        def lnr_apply(dve, b):
            hold(dve, "dve", ln["root"], b + 3)
            for i in range(TB):
                nc.vector.tensor_scalar(xnr[:, i, :], row_of_x(b * TB + i), mv[:, i, 0:1], rstd[:, i:i + 1],
                                        ALU.subtract, ALU.mult).then_inc(ln["xn"], 1)

        def lnr_tensor(pe, b):
            hold(pe, "pe", ln["xn"], 2 * TILES + TB * (b + 1))
            for k in range(KC):
                for i in range(TB):
                    last = nc.tensor.transpose(bank[1 + k][:, i * P:(i + 1) * P], xnr[:, i, k * P:(k + 1) * P], ident)
                last.then_inc(ln["tr"], 1)

        def lnr_evacuate(eng, copy, b, k):
            eng.wait_ge(ln["tr"], 16 + KC * b + k + 1)
            copy(xnT[:, k, row_tokens(b)], bank[1 + k][:]).then_inc(ln["row"], 1)

        prep_w = sem("prep_w")
        prep_ev = sem("prep_ev")
        consts = sem("consts")

        def prep_tensor(pe):
            loaded(pe, "prep")
            for h in range(HEADS):
                c = (h % 8) * KVL
                nc.tensor.matmul(bank[h // 8][:, c:c + KVL], wqbT[:, h, 0:P], wkvT[:, 0, h, :],
                                 start=True, stop=True)
                last = nc.tensor.matmul(bank[2 + h // 8][0:QL2, c:c + KVL], wqbT[:, h, P:QL], wkvT[:, 0, h, :],
                                        start=True, stop=True)
            last.then_inc(prep_w, 1)
            for h in range(HEADS):
                c = (h // 2 % 2) * DIM
                r = KVL * (h % 2)
                last = nc.tensor.matmul(bank[4 + h // 4][r:r + KVL, c:c + DIM], wkvT[:, 1, h, :], w_o[:, h, :],
                                        start=True, stop=True)
            last.then_inc(prep_w, 1)

        def prep_scalar(act):
            act.wait_ge(prep_w, 1)
            for m in range(2):
                for dst, b, n in ((wqe1, 0, P), (wqe2, 2, QL2)):
                    nc.scalar.copy(dst[:, 8 * m:8 * m + 8, 0:KVL],
                                   bank[b + m][0:n, :].rearrange("p (h c) -> p h c", h=8))
            act.wait_ge(prep_w, 2)
            for m in range(4):
                nc.scalar.copy(wvo[:, 2 * m:2 * m + 2, :], bank[4 + m][:].rearrange("p (h c) -> p h c", h=2))

        A = {k: sem(f"a_{k}") for k in
             ("proj", "sq", "ms", "root", "inv", "cq", "kr", "kv", "vt", "v",
              "q", "qs", "rope", "rope_v", "rope_w", "rope_a", "qt", "qte", "s", "max", "exp", "pt", "pte", "pv", "rr", "o",
              "ot", "ote", "y", "res")}
        NU = HG * TB

        Q_STEPS = (2, 5, 8, 11)

        def att_tensor(pe):
            def project(b):
                for m in range(3):
                    for k in range(KC):
                        last = nc.tensor.matmul(bank[m][:], w_a[:, k, m * P:(m + 1) * P],
                                                xnT[:, k, row_tokens(b)], start=(k == 0), stop=(k == KC - 1))
                    last.then_inc(A["proj"], 1)

            def mean_squares(b, n):
                if n == 0:
                    pe.wait_ge(A["sq"], 3 * b + 3)
                    nc.tensor.matmul(bank[5][:], ones[:], sq[:, 0, :], start=True, stop=False)
                    nc.tensor.matmul(bank[5][:], ones[0:QL2, :], sq[0:QL2, 1, :], start=False, stop=True)\
                        .then_inc(A["ms"], 1)
                else:
                    pe.wait_ge(A["inv"], 4 * b + 1)
                    nc.tensor.matmul(bank[5][:], ones[0:KVL, :], sq[0:KVL, 2, :], start=True, stop=True)\
                        .then_inc(A["ms"], 1)

            def row_values(b):
                hold(pe, "pe", A["kv"], b + 1)
                for i in range(TB):
                    last = nc.tensor.transpose(bank[5][:, i * KVL:(i + 1) * KVL],
                                               KT[0:KVL, i * P:(i + 1) * P], ident[0:KVL, 0:KVL])
                last.then_inc(A["vt"], 1)

            def first_queries(b):
                pe.wait_ge(A["cq"], 2 * b + 2)
                for i in range(TB):
                    if i >= 2:
                        pe.wait_ge(A["qs"], TB * GROUPS * b + i - 1 + START)
                    q_product(pe, b * GROUPS, 0, i, 7 - i % 2)
                pe.wait_ge(A["kr"], b + 1)
                pe.wait_ge(A["v"], b + 1)
                for i in range(TB):
                    if i % 2:
                        hold(pe, "pe", A["rope_v"], 2 * b + i // 2 + 1)
                    else:
                        hold(pe, "pe", A["rope"], ROPES * b + i // 2 + 1)
                    if i == 3:
                        hold(pe, "pe", A["qte"], TB * GROUPS * b + 1 + START)
                    q_transpose(pe, i)

            def output(b, i):
                for half in range(2):
                    hold(pe, "pe", A["ote"], 2 * TB * b + max(0, 2 * i + half - 1) + START)
                    for c in range(4):
                        cc = 4 * half + c
                        last = nc.tensor.transpose(bank[3 + half][:, c * P:(c + 1) * P],
                                                   O[:, i, cc * P:(cc + 1) * P], ident)
                    last.then_inc(A["ot"], 1)
                pe.wait_ge(A["ote"], 2 * TB * b + 2 * i + 2 + START)
                if i >= 2:
                    pe.wait_ge(A["res"], TB * b + i - 1 + START)
                for c in range(HEADS // 2):
                    last = nc.tensor.matmul(bank[6 + i % 2][:, 0:DIM], OT[:, i % 2, c * P:(c + 1) * P],
                                            wvo[:, c, :], start=(c == 0), stop=(c == HEADS // 2 - 1))
                last.then_inc(A["y"], 1)

            def row(b, with_next):
                with pe.Fori(0, GROUPS - 1) as hg:
                    group_tensor(pe, b * GROUPS + hg, ROPES * b + 2 + TB * hg, hg, True)
                group_tensor(pe, b * GROUPS + (GROUPS - 1), None, GROUPS - 1, False)
                if with_next:
                    project(b + 1)
                pe.wait_ge(A["o"], HEADS * b + HEADS)
                output(b, 0)
                if with_next:
                    mean_squares(b + 1, 0)
                output(b, 1)
                if with_next:
                    mean_squares(b + 1, 1)
                output(b, 2)
                output(b, 3)
                if with_next:
                    row_values(b + 1)
                if with_next:
                    pe.wait_ge(A["res"], TB * b + TB + START)
                    first_queries(b + 1)

            project(0)
            mean_squares(0, 0)
            mean_squares(0, 1)
            row_values(0)
            first_queries(0)
            with pe.Fori(0, BATCH - 1) as b:
                row(b, True)
            row(BATCH - 1, False)

        ROPES = 2 + TB * (GROUPS - 1)

        def row_tokens(b):
            return slice(b * SEQ, (b + 1) * SEQ) if isinstance(b, int) else bass.ds(b * SEQ, SEQ)

        def q_product(pe, g, hg, i, at):
            w1 = wqe1[:, bass.ds(hg * HG, HG), :].rearrange("p h c -> p (h c)") if not isinstance(hg, int) \
                else wqe1[:, hg * HG:(hg + 1) * HG, :].rearrange("p h c -> p (h c)")
            w2 = wqe2[:, bass.ds(hg * HG, HG), :].rearrange("p h c -> p (h c)") if not isinstance(hg, int) \
                else wqe2[:, hg * HG:(hg + 1) * HG, :].rearrange("p h c -> p (h c)")
            nc.tensor.matmul(bank[at][:], cq1[:, i * P:(i + 1) * P], w1, start=True, stop=False)
            nc.tensor.matmul(bank[at][:], cq2[:, i * P:(i + 1) * P], w2, start=False, stop=True)\
                .then_inc(A["q"], 1)

        def q_transpose(pe, i):
            for h in range(HG):
                last = nc.tensor.transpose(bank[(NU + i) % 3][:, h * P:(h + 1) * P],
                                           qs[:, i, h * QE:(h + 1) * QE], ident)
            last.then_inc(A["qt"], 1)

        def group_tensor(pe, g, roped, hg, with_next):
            def scores(u):
                h, i = u // TB, u % TB
                if u >= 3:
                    pe.wait_ge(A["exp"], NU * g + u - 2)
                if u < TB:
                    pe.wait_ge(A["qte"], TB * g + min(TB, i + 3) + START)
                n = (i + 1) * P
                nc.tensor.matmul(bank[u % 3][:, 0:n], QT[:, h, i * P:(i + 1) * P], KT[:, 0:n],
                                 start=True, stop=False)
                nc.tensor.matmul(bank[u % 3][:, i * P:n], identb[:], futureb[:], start=False, stop=True)\
                    .then_inc(A["s"], 1)

            def transposes(u):
                i = u % TB
                pe.wait_ge(A["exp"], NU * g + u + 1)
                if u >= 2:
                    hold(pe, "pe", A["pte"], NU * g + u - 1)
                for j in range(i + 1):
                    last = nc.tensor.transpose(bank[3 + u % 2][:, j * P:(j + 1) * P],
                                               prob[:, u % 4, j * P:(j + 1) * P], ident)
                last.then_inc(A["pt"], 1)

            def values(u):
                h, i = u // TB, u % TB
                pe.wait_ge(A["pte"], NU * g + u + 1)
                if i == 0 and h >= 2:
                    hold(pe, "pe", A["o"], HG * g + h - 1)
                for j in range(i + 1):
                    last = nc.tensor.matmul(bank[5 + h % 2][:, i * KVL:(i + 1) * KVL],
                                            probT[:, u % 2, j * P:(j + 1) * P], V[:, j, :],
                                            start=(j == 0), stop=(j == i))
                last.then_inc(A["pv"], 1)

            for u in range(NU + TB):
                if u < NU:
                    scores(u)
                elif with_next:
                    if u < NU + 3:
                        hold(pe, "pe", A["exp"], NU * g + u - 2)
                    else:
                        hold(pe, "pe", A["qte"], TB * (g + 1) + 1 + START)
                    hold(pe, "pe", A["rope"], roped + u - NU + 1)
                    q_transpose(pe, u - NU)
                if with_next and u in Q_STEPS:
                    pe.wait_ge(A["qs"], TB * (g + 1) + Q_STEPS.index(u) + START)
                    q_product(pe, g + 1, hg + 1, Q_STEPS.index(u), 7)
                if 2 <= u < NU + 2:
                    transposes(u - 2)
                if 3 <= u < NU + 3:
                    values(u - 3)

        def att_scalar(act):
            def squares(b):
                for m, n, width in ((0, P, QL), (1, QL2, QL), (2, KVL, KVL)):
                    act.wait_ge(A["proj"], 3 * b + m + 1)
                    nc.scalar.activation(sq[0:n, m, :], bank[m][0:n, :], ACT.Square,
                                         scale=1.0 / math.sqrt(width)).then_inc(A["sq"], 1)

            def root(b, n):
                act.wait_ge(A["inv"], 4 * b + 2 * n + 2)
                if n == 0:
                    nc.scalar.activation(rq, rq, ACT.Sqrt, scale=ATT_SCALE * ATT_SCALE).then_inc(A["root"], 1)
                else:
                    nc.scalar.activation(rk[0:KVL, :], rk[0:KVL, :], ACT.Sqrt).then_inc(A["root"], 1)

            def values(b):
                act.wait_ge(A["vt"], b + 1)
                nc.scalar.copy(V.rearrange("p i c -> p (i c)"), bank[5][:, 0:TB * KVL]).then_inc(A["v"], 1)

            def first_queries(b):
                for i in range(TB):
                    q_copy(act, b * GROUPS, i, 7 - i % 2)
                for i in range(TB):
                    qt_copy(act, b * GROUPS, i)

            def output(b, i):
                for half in range(2):
                    act.wait_ge(A["ot"], 2 * TB * b + 2 * i + half + 1)
                    if i >= 2:
                        act.wait_ge(A["y"], TB * b + i - 1)
                    nc.scalar.copy(OT[:, i % 2, 4 * half * P:4 * (half + 1) * P], bank[3 + half][:])\
                        .then_inc(A["ote"], 1)

            def row(b, with_next):
                with act.Fori(0, GROUPS - 1) as hg:
                    group_scalar(act, b * GROUPS + hg, True)
                group_scalar(act, b * GROUPS + (GROUPS - 1), False)
                if with_next:
                    squares(b + 1)
                output(b, 0)
                output(b, 1)
                if with_next:
                    root(b + 1, 0)
                output(b, 2)
                if with_next:
                    root(b + 1, 1)
                output(b, 3)
                if with_next:
                    values(b + 1)
                if with_next:
                    first_queries(b + 1)

            squares(0)
            root(0, 0)
            root(0, 1)
            values(0)
            first_queries(0)
            with act.Fori(0, BATCH - 1) as b:
                row(b, True)
            row(BATCH - 1, False)

        def q_copy(act, g, i, at=7):
            act.wait_ge(A["q"], TB * g + i + 1)
            nc.scalar.copy(qs[:, i, :], bank[at][:]).then_inc(A["qs"], 1)

        def qt_copy(act, g, i):
            act.wait_ge(A["qt"], TB * g + i + 1)
            nc.scalar.copy(QT[:, :, i * P:(i + 1) * P], bank[(NU + i) % 3][:].rearrange("p (h c) -> p h c", h=HG))\
                .then_inc(A["qte"], 1)

        def group_scalar(act, g, with_next):
            def exps(u):
                i = u % TB
                act.wait_ge(A["max"], NU * g + u + 1)
                if u >= 4:
                    act.wait_ge(A["pt"], NU * g + u - 3)
                nc.scalar.activation(prob[:, u % 4, 0:(i + 1) * P], bank[u % 3][:, 0:(i + 1) * P], ACT.Exp,
                                     bias=negmax[:, u:u + 1], scale=1.0,
                                     accum_out=rowsum[:, u:u + 1]).then_inc(A["exp"], 1)

            for u in range(NU + TB):
                if u < NU:
                    exps(u)
                elif with_next:
                    qt_copy(act, g + 1, u - NU)
                if with_next and u in Q_STEPS:
                    q_copy(act, g + 1, Q_STEPS.index(u))

        def att_vector(dve):
            def rope_keys(b):
                dve.wait_ge(A["proj"], 3 * b + 3)
                nc.vector.tensor_tensor(krope[KVL:QE, 0, :], bank[2][KVL:QE, :], cosk[KVL:QE, :], ALU.mult)\
                    .then_inc(A["rope_a"], 1)
                nc.vector.tensor_tensor(krope[KVL:QE, 1, :], bank[1][KVL:QE, :], sink[KVL:QE, :], ALU.mult)\
                    .then_inc(A["rope_a"], 1)
                dve.wait_ge(A["rope_a"], 2 * b + 2)
                nc.vector.tensor_tensor(KT[KVL:QE, :], krope[KVL:QE, 0, :], krope[KVL:QE, 1, :], ALU.add)\
                    .then_inc(A["kr"], 1)

            def inverse(b, n):
                r = rq if n == 0 else rk[0:KVL, :]
                dve.wait_ge(A["ms"], 2 * b + n + 1)
                nc.vector.tensor_scalar(r, bank[5][:] if n == 0 else bank[5][0:KVL, :], RMS_EPS, None, ALU.add)\
                    .then_inc(A["inv"], 1)
                dve.wait_ge(A["inv"], 4 * b + 2 * n + 1)
                nc.vector.reciprocal(r, r).then_inc(A["inv"], 1)

            def latents(b, n):
                dve.wait_ge(A["root"], 2 * b + n + 1)
                if n == 0:
                    dve.wait_ge(A["sq"], 3 * b + 3)
                    nc.vector.scalar_tensor_tensor(out=cq1, in0=bank[0][:], scalar=qn1[:], in1=rq,
                                                   op0=ALU.mult, op1=ALU.mult).then_inc(A["cq"], 1)
                    nc.vector.scalar_tensor_tensor(out=cq2, in0=bank[1][0:QL2, :], scalar=qn2[:],
                                                   in1=rq[0:QL2, :], op0=ALU.mult, op1=ALU.mult)\
                        .then_inc(A["cq"], 1)
                else:
                    nc.vector.scalar_tensor_tensor(out=KT[0:KVL, :], in0=bank[2][0:KVL, :], scalar=kvn[:],
                                                   in1=rk[0:KVL, :], op0=ALU.mult, op1=ALU.mult)\
                        .then_inc(A["kv"], 1)

            def first_ropes(b):
                for i in (1, 3):
                    hold(dve, "dve", A["qs"], TB * GROUPS * b + i + 1 + START)
                    rope(nc.vector, dve, "dve", i, A["rope_w"], 6 * b + 3 * (i // 2) + 3, A["rope_v"], qtmp_v)
                    hold(dve, "dve", A["rope_v"], 2 * b + i // 2 + 1)

            def residual(b, i):
                dve.wait_ge(A["y"], TB * b + i + 1)
                xt = x[:, bass.ds(b * TB + i, 1), :].rearrange("p o c -> p (o c)") if not isinstance(b, int) \
                    else x[:, b * TB + i, :]
                nc.vector.tensor_tensor(xt, bank[6 + i % 2][:, 0:DIM], xt, ALU.add).then_inc(A["res"], 1)

            def row(b, with_next):
                with dve.Fori(0, GROUPS - 1) as hg:
                    group_vector(dve, b * GROUPS + hg, hg)
                group_vector(dve, b * GROUPS + (GROUPS - 1), GROUPS - 1)
                if with_next:
                    rope_keys(b + 1)
                residual(b, 0)
                if with_next:
                    inverse(b + 1, 0)
                residual(b, 1)
                if with_next:
                    inverse(b + 1, 1)
                    latents(b + 1, 0)
                residual(b, 2)
                if with_next:
                    latents(b + 1, 1)
                residual(b, 3)
                if with_next:
                    first_ropes(b + 1)

            rope_keys(0)
            inverse(0, 0)
            latents(0, 0)
            inverse(0, 1)
            latents(0, 1)
            first_ropes(0)
            with dve.Fori(0, BATCH - 1) as b:
                row(b, True)
            row(BATCH - 1, False)

        def group_vector(dve, g, hg):
            def maximum(u):
                i = u % TB
                dve.wait_ge(A["s"], NU * g + u + 1)
                nc.vector.tensor_reduce(negmax[:, u:u + 1], bank[u % 3][:, 0:(i + 1) * P], axis=AX.X,
                                        op=ALU.max, negate=True).then_inc(A["max"], 1)

            def head_out(h):
                hold(dve, "dve", A["exp"], NU * g + TB * (h + 1))
                nc.vector.reciprocal(rrow[:, TB * h:TB * (h + 1)], rowsum[:, TB * h:TB * (h + 1)])\
                    .then_inc(A["rr"], 1)
                dve.wait_ge(A["rr"], HG * g + h + 1)
                dve.wait_ge(A["pv"], NU * g + TB * (h + 1))
                col = (hg * HG + h) * KVL
                dst = O[:, :, bass.ds(col, KVL)] if not isinstance(col, int) else O[:, :, col:col + KVL]
                nc.vector.tensor_tensor(dst,
                                        bank[5 + h % 2][:, 0:TB * KVL].rearrange("p (i c) -> p i c", i=TB),
                                        rrow[:, TB * h:TB * (h + 1)].unsqueeze(2).to_broadcast([P, TB, KVL]),
                                        ALU.mult).then_inc(A["o"], 1)

            def evacuate(u):
                i = u % TB
                dve.wait_ge(A["pt"], NU * g + u + 1)
                if u >= 2:
                    dve.wait_ge(A["pv"], NU * g + u - 1)
                nc.vector.tensor_copy(probT[:, u % 2, 0:(i + 1) * P], bank[3 + u % 2][:, 0:(i + 1) * P])\
                    .then_inc(A["pte"], 1)

            for u in range(NU + 4):
                if u < NU:
                    maximum(u)
                if 2 <= u < NU + 2:
                    evacuate(u - 2)
                if u >= 7 and (u - 7) % TB == 0:
                    head_out((u - 7) // TB)

        def rope(api, eng, who, i, parts_done, n_parts, done, tmp):
            q = qs[:, i, :].rearrange("p (h c) -> p h c", h=HG)
            ta = tmp[:, 0, :].rearrange("p (h c) -> p h c", h=HG)
            tb = tmp[:, 1, :].rearrange("p (h c) -> p h c", h=HG)
            half = DR // 2
            c = cosq[:, i, :].unsqueeze(1).to_broadcast([P, HG, DR])
            s1 = sinq[:, i, 0:half].unsqueeze(1).to_broadcast([P, HG, half])
            s2 = sinq[:, i, half:DR].unsqueeze(1).to_broadcast([P, HG, half])
            api.tensor_tensor(ta, q[:, :, KVL:QE], c, ALU.mult).then_inc(parts_done, 1)
            api.tensor_tensor(tb[:, :, 0:half], q[:, :, KVL + half:QE], s1, ALU.mult).then_inc(parts_done, 1)
            api.tensor_tensor(tb[:, :, half:DR], q[:, :, KVL:KVL + half], s2, ALU.mult).then_inc(parts_done, 1)
            hold(eng, who, parts_done, n_parts)
            api.tensor_tensor(q[:, :, KVL:QE], ta, tb, ALU.add).then_inc(done, 1)

        def att_pool(pool):
            def turn(b, n, copied, i):
                hold(pool, "pool", A["qs"], copied + START)
                rope(nc.gpsimd, pool, "pool", i, A["rope_a2"], 3 * ROPES * b + 3 * n + 3, A["rope"], qtmp)
                hold(pool, "pool", A["rope"], ROPES * b + n + 1)

            with pool.Fori(0, BATCH) as b:
                for i in (0, 2):
                    turn(b, i // 2, TB * GROUPS * b + i + 1, i)
                with pool.Fori(0, GROUPS - 1) as hg:
                    for i in range(TB):
                        turn(b, TB * hg + 2 + i, TB * GROUPS * b + TB * hg + TB + i + 1, i)

        A["rope_a2"] = sem("a_rope_parts")

        M = {k: sem(f"m_{k}") for k in
             ("lg", "step", "sub", "exp", "mask", "count", "slots", "ends", "row", "zero", "sent", "in", "tr", "trc",
              "up", "hid", "down", "ey", "out", "used", "sup", "ssil", "shid", "sdown", "sacc", "trips", "table")}
        ZERO_PARTS = 4
        ZEROED = 1 + 16 * ZERO_PARTS
        MCREDIT = ("used", "tr", "trc", "up", "hid", "down", "ey", "shid", "sdown", "sacc")
        loaded_rows = [sem(f"m_rows{j}") for j in range(LOOP_TILES)]
        loaded_tile = [sem(f"m_tile{j}") for j in range(LOOP_TILES)]
        gathered = [sem(f"m_gath{j}") for j in range(8)]

        def route_tensor(pe):
            for t in range(TILES):
                for k in range(KC):
                    last = nc.tensor.matmul(bank[t // 8][:, (t % 8) * EXPERTS:(t % 8 + 1) * EXPERTS],
                                            xnT[:, k, t * P:(t + 1) * P], gateT[:, k, :],
                                            start=(k == 0), stop=(k == KC - 1))
            last.then_inc(M["lg"], 1)

            pe.wait_ge(M["mask"], 1)
            for m in range(2):
                half = mask[:, 8 * m:8 * m + 8, :].rearrange("p t e -> p (t e)")
                nc.tensor.matmul(bank[m][:], le, half, start=True, stop=True)
                last = nc.tensor.matmul(bank[2 + m][:], ones[:], half, start=True, stop=True)
            last.then_inc(M["count"], 1)
            pe.wait_ge(M["ends"], 1)
            nc.tensor.transpose(bank[4][0:1, 0:P], tile_exp, ident).then_inc(M["row"], 1)

        def route_vector(dve):
            steps = [0]

            def step(ins):
                steps[0] += 1
                ins.then_inc(M["step"], 1)
                dve.wait_ge(M["step"], steps[0])

            step(nc.vector.memset(lgs[:, :, EXPERTS:EXPERTS + 2], -LOW))
            dve.wait_ge(M["lg"], 1)
            for m in range(2):
                step(nc.vector.tensor_copy(lgs[:, 8 * m:8 * m + 8, 0:EXPERTS],
                                    bank[m][:].rearrange("p (t e) -> p t e", t=8)))
            for t in range(TILES):
                last = nc.vector.max(top8[:, t, :], lgs[:, t, 0:EXPERTS])
            step(last)
            nc.vector.tensor_tensor(comb, lgs[:, :, 0:EXPERTS], top8[:, :, 0:1].to_broadcast([P, TILES, EXPERTS]),
                             ALU.subtract).then_inc(M["sub"], 1)
            dve.wait_ge(M["sub"], 1)
            step(nc.vector.memset(top8[:, :, TOPK:8], -LOW))
            for t in range(TILES):
                last = nc.vector.match_replace(taken_pad[:, t, :], top8[:, t, :], lgs[:, t, :], LOW)
            step(last)
            nc.vector.tensor_scalar(mask, taken_pad[:, :, 0:EXPERTS], 0.9 * LOW, None, ALU.is_lt).then_inc(M["mask"], 1)
            dve.wait_ge(M["mask"], 1)
            dve.wait_ge(M["count"], 1)
            step(nc.vector.memset(before[:, 0, :], 0.0))
            for t in range(TILES):
                step(nc.vector.tensor_tensor(before[:, t + 1, :], before[:, t, :],
                                      bank[2 + t // 8][:, (t % 8) * EXPERTS:(t % 8 + 1) * EXPERTS], ALU.add))
            step(nc.vector.tensor_tensor(filled, before[:, TILES, :].unsqueeze(2).to_broadcast([P, EXPERTS, TOKENS // ROWS - 1]),
                                  full.unsqueeze(1).to_broadcast([P, EXPERTS, TOKENS // ROWS - 1]), ALU.is_gt))
            step(nc.vector.tensor_reduce(n_tiles, filled, axis=AX.X, op=ALU.add))
            step(nc.vector.tensor_scalar(n_tiles, n_tiles, 1.0, None, ALU.add))
            step(nc.vector.tensor_tensor_scan(tile_end, ones[:, 0:EXPERTS], n_tiles, 0.0, ALU.mult, ALU.add))
            step(nc.vector.tensor_scalar(ended, tile_end, partition, None, ALU.is_le))
            step(nc.vector.tensor_reduce(tile_exp, ended, axis=AX.X, op=ALU.add))
            nc.vector.tensor_scalar(tile_exp, tile_exp, EXPERTS - 1.0, None, ALU.min).then_inc(M["ends"], 1)
            step(nc.vector.tensor_tensor(row_base, tile_end, n_tiles, ALU.subtract))
            step(nc.vector.tensor_scalar(row_base, row_base, 1.0 * ROWS, None, ALU.mult))
            for m in range(2):
                step(nc.vector.tensor_tensor(key[:, 8 * m:8 * m + 8, :], before[:, 8 * m:8 * m + 8, :],
                                      bank[m][:].rearrange("p (t e) -> p t e", t=8), ALU.add))
            step(nc.vector.tensor_tensor(key, key, row_base.unsqueeze(1).to_broadcast([P, TILES, EXPERTS]), ALU.add))
            step(nc.vector.tensor_scalar(key, key, -1.0, FAR + 1.0, ALU.mult, ALU.add))
            step(nc.vector.tensor_tensor(key, key, mask, ALU.mult))
            for t in range(TILES):
                last = nc.vector.max(near8[:, t, :], key[:, t, :])
            step(last)
            nc.vector.tensor_scalar(slots[:], near8[:, :, 0:TOPK], -1.0, 1.0 * FAR, ALU.mult, ALU.add)\
                .then_inc(M["slots"], 1)
            marks = MAX_TILES // LOOP_TILES
            step(nc.vector.tensor_tensor(ended[0:1, 0:marks], tile_end[0:1, EXPERTS - 1:EXPERTS].to_broadcast([1, marks]),
                                  loop_marks[0:1, :], ALU.is_gt))
            step(nc.vector.tensor_reduce(tile_exp0, ended[0:1, 0:marks], axis=AX.X, op=ALU.add))
            step(nc.vector.tensor_copy(trips[0:1, 0:1], tile_exp0))
            step(nc.vector.tensor_scalar(tile_exp0, tile_exp0, -1.0, None, ALU.add))
            step(nc.vector.tensor_copy(trips[0:1, 1:2], tile_exp0))
            dve.wait_ge(M["row"], 1)
            nc.vector.tensor_copy(tile_row[:], bank[4][0:1, 0:P]).then_inc(M["trips"], 1)
            dve.wait_ge(M["trips"], 1)
            dve.wait_ge(M["exp"], 1)
            step(nc.vector.tensor_tensor(taken, mask, comb, ALU.mult))
            step(nc.vector.tensor_reduce(rsum, taken, axis=AX.X, op=ALU.add))
            step(nc.vector.reciprocal(rsum, rsum))
            step(nc.vector.tensor_tensor(comb, taken, rsum.unsqueeze(2).to_broadcast([P, TILES, EXPERTS]), ALU.mult))
            for k in range(TOPK):
                step(nc.vector.tensor_tensor(taken, key, near8[:, :, k:k + 1].to_broadcast([P, TILES, EXPERTS]),
                                      ALU.is_equal))
                step(nc.vector.tensor_tensor(taken, taken, comb, ALU.mult))
                step(nc.vector.tensor_reduce(weight[:, :, k], taken, axis=AX.X, op=ALU.add))

        def route_scalar(act):
            act.wait_ge(M["sub"], 1)
            nc.scalar.activation(comb, comb, ACT.Exp).then_inc(M["exp"], 1)

        def send_pool(pool):
            pool.wait_ge(M["slots"], 1)
            pool.wait_ge(M["zero"], ZEROED)
            for t in range(TILES):
                for k in range(TOPK):
                    nc.gpsimd.indirect_dma_start(
                        sent[:, :], bass.IndirectOffsetOnAxis(ap=slots[:, t, k:k + 1], axis=0),
                        xn[:, t, :], None).then_inc(M["sent"], 16)

        def row_of_x(t):
            return x[:, t, :] if isinstance(t, int) else x[:, bass.ds(t, 1), :].rearrange("p o c -> p (o c)")

        def row_tables(pool, b):
            hold(pool, "pool", M["used"], TOPK * TB * b + START)
            nc.gpsimd.tensor_copy(row_slots[:], slots[:, bass.ds(b * TB, TB), :] if not isinstance(b, int)
                                  else slots[:, b * TB:(b + 1) * TB, :]).then_inc(M["table"], 1)
            nc.gpsimd.tensor_copy(row_weight[:], weight[:, bass.ds(b * TB, TB), :] if not isinstance(b, int)
                                  else weight[:, b * TB:(b + 1) * TB, :]).then_inc(M["table"], 1)
            hold(pool, "pool", M["table"], 2 * b + 2)

        def return_pool(pool, b, i):
            for k in range(TOPK):
                n = i * TOPK + k
                if n >= 8:
                    hold(pool, "pool", M["used"], TOPK * TB * b + n - 7 + START)
                nc.gpsimd.indirect_dma_start(
                    gath[:, n % 8, :], None, returned[:, :],
                    bass.IndirectOffsetOnAxis(ap=row_slots[:, i, k:k + 1], axis=0)).then_inc(gathered[n % 8], 16)

        def return_vector(dve, b, i):
            for k in range(TOPK):
                n = i * TOPK + k
                if i == 0 and k == 0:
                    hold(dve, "dve", M["table"], 2 * b + 2)
                dve.wait_ge(gathered[n % 8], 16 * (TOPK * TB // 8 * b + n // 8 + 1))
                if k:
                    hold(dve, "dve", M["used"], TOPK * TB * b + n + START)
                nc.vector.scalar_tensor_tensor(out=row_of_x(b * TB + i), in0=gath[:, n % 8, :],
                                               scalar=row_weight[:, i, k:k + 1], in1=row_of_x(b * TB + i),
                                               op0=ALU.mult, op1=ALU.add).then_inc(M["used"], 1)

        LT4 = LOOP_TILES

        def steps_of(eng):
            eng.wait_ge(M["trips"], 1)
            return eng.value_load(trips[0:1, 0:1], min_val=EXPERTS // LT4, max_val=MAX_TILES // LT4)

        def last_step(eng):
            eng.wait_ge(M["trips"], 1)
            return eng.value_load(trips[0:1, 1:2], min_val=EXPERTS // LT4 - 1, max_val=MAX_TILES // LT4 - 1)

        def experts_sp(sp):
            steps = steps_of(sp)
            sp.wait_ge(M["sent"], 16 * TILES * TOPK)
            with sp.Fori(0, steps) as it:
                for j in range(LT4):
                    e = sp.value_load(tile_row[0:1, bass.ds(it * LT4 + j, 1)], min_val=0, max_val=EXPERTS - 1)
                    sp.wait_ge(M["tr"], LT4 * it + j + 1 - LT4 + START)
                    sp.dma_start(eraw[:, j, :].rearrange("p (o c) -> p o c", o=2),
                                 sent[bass.ds((it * LT4 + j) * ROWS, ROWS), :].rearrange("(o p) c -> p o c", p=P))\
                        .then_inc(loaded_rows[j], 16)
                    sp.wait_ge(M["down"], LT4 * it + j + 1 - LT4 + START)
                    sp.dma_start(w1b[:, j, :], a["w1T"][bass.ds(e, 1), :, :]
                                 .rearrange("o p n -> p (o n)")).then_inc(loaded_tile[j], 16)
                    sp.dma_start(w2b[:, j, :], a["w2T"][bass.ds(e, 1), :, :]
                                 .rearrange("o p n -> p (o n)")).then_inc(loaded_tile[j], 16)

        def experts_tensor(pe):
            last_it = last_step(pe)
            pe.wait_ge(M["sacc"], TILES + START)

            def turn(it, j):
                hold(pe, "pe", loaded_rows[j], 16 * it + 16)
                hold(pe, "pe", M["trc"], LT4 * it + j - 1 + START)
                for k in range(KC):
                    for half in range(2):
                        c = (2 * k + half) * P
                        last = nc.tensor.transpose(bank[j % 2][:, c:c + P],
                                                   eraw[:, j, half * DIM + k * P:half * DIM + (k + 1) * P], ident)
                last.then_inc(M["tr"], 1)

            def up(it, j):
                hold(pe, "pe", loaded_tile[j], 32 * it + 32)
                pe.wait_ge(M["trc"], LT4 * it + j + 1 + START)
                pe.wait_ge(M["hid"], LT4 * it + max(0, j - 1) + START)
                for c in range(2):
                    for k in range(KC):
                        last = nc.tensor.matmul(bank[2 + j % 2][0:EH, c * ROWS:(c + 1) * ROWS],
                                                w1b[:, j, k * EI + c * EH:k * EI + (c + 1) * EH],
                                                eT[:, j % 2, k * ROWS:(k + 1) * ROWS],
                                                start=(k == 0), stop=(k == KC - 1))
                last.then_inc(M["up"], 1)

            def down(it, j):
                pe.wait_ge(M["hid"], LT4 * it + j + 1 + START)
                pe.wait_ge(M["ey"], LT4 * it + max(0, j - 1) + START)
                for half in range(2):
                    for c in range(2):
                        last = nc.tensor.matmul(bank[4 + j % 2][:, half * DIM:(half + 1) * DIM],
                                                hid[0:EH, j % 2, c * ROWS + half * P:c * ROWS + (half + 1) * P],
                                                w2b[:, j, c * DIM:(c + 1) * DIM],
                                                start=(c == 0), stop=(c == 1))
                last.then_inc(M["down"], 1)

            def step(it, with_next):
                for j in range(LT4):
                    up(it, j)
                    if j + 2 < LT4:
                        turn(it, j + 2)
                    elif with_next:
                        turn(it + 1, j + 2 - LT4)
                    if j:
                        down(it, j - 1)
                down(it, LT4 - 1)

            turn(0, 0)
            turn(0, 1)
            with pe.Fori(0, last_it) as it:
                step(it, True)
            step(last_it, False)

        def experts_scalar(act):
            steps = steps_of(act)
            with act.Fori(0, steps) as it:
                def store(j):
                    act.wait_ge(M["ey"], LT4 * it + j + 1 + START)
                    act.dma_start(returned[bass.ds((it * LT4 + j) * ROWS, ROWS), :].rearrange("(o p) c -> p o c", p=P),
                                  ey[:, j % 2, :].rearrange("p (o c) -> p o c", o=2)).then_inc(stored[j % 2], 16)

                for j in range(LT4):
                    act.wait_ge(M["up"], LT4 * it + j + 1 + START)
                    act.wait_ge(M["down"], LT4 * it + max(0, j - 1) + START)
                    nc.scalar.activation(hid[0:EH, j % 2, :], bank[2 + j % 2][0:EH, :], ACT.Silu)\
                        .then_inc(M["hid"], 1)
                    if j:
                        store(j - 1)
                store(LT4 - 1)
            for p in range(2):
                hold(act, "act", stored[p], 16 * (LT4 // 2) * steps + 16)
            act.wait_ge(M["exp"], 1)
            act.sem_inc(M["out"], 1)

        stored = [sem(f"m_stored{p}") for p in range(2)]

        def experts_vector(dve):
            last_it = last_step(dve)

            def turned(it, j):
                dve.wait_ge(M["tr"], LT4 * it + j + 1 + START)
                hold(dve, "dve", M["up"], LT4 * it + j - 1 + START)
                nc.vector.tensor_copy(eT[:, j % 2, :], bank[j % 2][:]).then_inc(M["trc"], 1)

            def result(it, j):
                dve.wait_ge(M["down"], LT4 * it + j + 1 + START)
                hold(dve, "dve", stored[j % 2], 16 * (LT4 // 2) * it + 16 * (j // 2) + 16)
                nc.vector.tensor_copy(ey[:, j % 2, :], bank[4 + j % 2][:]).then_inc(M["ey"], 1)

            def step(it, with_next):
                for j in range(LT4):
                    if j + 2 < LT4:
                        turned(it, j + 2)
                    elif with_next:
                        turned(it + 1, j + 2 - LT4)
                    if j:
                        result(it, j - 1)
                result(it, LT4 - 1)

            turned(0, 0)
            turned(0, 1)
            with dve.Fori(0, last_it) as it:
                step(it, True)
            step(last_it, False)

        def shared_tensor(pe):
            with pe.Fori(0, BATCH) as g:
                pe.wait_ge(M["sacc"], TB * g + START)
                n = 0
                for c, (lo, w) in enumerate(SH_CHUNKS):
                    for half in range(2):
                        for k in range(KC):
                            last = nc.tensor.matmul(bank[3 * half + c][0:w, :],
                                                    sguT[:, k, SHI * half + lo:SHI * half + lo + w],
                                                    xnT[:, k, bass.ds(g * SEQ, SEQ)],
                                                    start=(k == 0), stop=(k == KC - 1))
                        last.then_inc(M["sup"], 1)
                pe.wait_ge(M["shid"], 3 * g + 3 + START)
                for i in range(TB):
                    if i >= 2:
                        pe.wait_ge(M["sacc"], TB * g + i - 1 + START)
                    for c, (lo, w) in enumerate(SH_CHUNKS):
                        last = nc.tensor.matmul(bank[6 + i % 2][:, 0:DIM], shid[0:w, c, i * P:(i + 1) * P],
                                                sdT[0:w, c, :], start=(c == 0), stop=(c == 2))
                    last.then_inc(M["sdown"], 1)

        def shared_scalar(act):
            with act.Fori(0, BATCH) as g:
                for c, (lo, w) in enumerate(SH_CHUNKS):
                    act.wait_ge(M["sup"], 6 * g + 2 * c + 1)
                    act.wait_ge(M["shid"], 3 * g + START)
                    nc.scalar.activation(sgl[0:w, c, :], bank[c][0:w, :], ACT.Silu).then_inc(M["ssil"], 1)

        def shared_vector(dve):
            with dve.Fori(0, BATCH) as g:
                for c, (lo, w) in enumerate(SH_CHUNKS):
                    dve.wait_ge(M["sup"], 6 * g + 2 * c + 2)
                    dve.wait_ge(M["ssil"], 3 * g + c + 1)
                    dve.wait_ge(M["sdown"], TB * g + START)
                    nc.vector.tensor_tensor(shid[0:w, c, :], bank[3 + c][0:w, :], sgl[0:w, c, :], ALU.mult)\
                        .then_inc(M["shid"], 1)
                for i in range(TB):
                    dve.wait_ge(M["sdown"], TB * g + i + 1 + START)
                    xt = x[:, bass.ds(g * TB + i, 1), :].rearrange("p o c -> p (o c)")
                    nc.vector.tensor_tensor(xt, bank[6 + i % 2][:, 0:DIM], xt, ALU.add).then_inc(M["sacc"], 1)

        S = {k: sem(f"s_{k}") for k in
             ("aneg", "pad", "xb", "br", "brc", "tap", "conv", "act", "z", "zs", "bcd", "bcde", "d1", "d2", "d3", "d4",
              "dexp", "dln", "adt", "xt", "xte", "bct", "bcte", "cum", "es", "au", "seg", "lt", "g", "gm",
              "mt", "xd1", "xd", "yo", "st0", "st", "y1", "y2", "y3", "y4", "yt", "yte", "out", "res")}
        SCREDIT = ("xb", "conv", "act", "brc", "zs", "bcde", "res", "xte", "bcte", "yte", "es", "gm", "lt", "y1", "y2",
                   "yo", "st", "mt", "y4", "seg", "cum", "out", "xt", "bct", "br", "adt", "yt", "au")
        draw, dmin, dexp, dw, dln, dpos, dsel, dtv = (dts[:, n, :] for n in range(8))

        def ssm_pool(pool):
            for c in range(CH):
                nc.gpsimd.memset(xpad[:, c, 0:TAPS - 1], 0.0).then_inc(S["pad"], 1)

            def row(b, with_next):
                hold(pool, "pool", S["res"], TB * b + START)
                hold(pool, "pool", ln["row"], KC * (b + 1))
                nc.gpsimd.tensor_copy(xb, xnT[:, :, row_tokens(b)]).then_inc(S["xb"], 1)
                if with_next:
                    row_tables(pool, b + 1)
                    return_pool(pool, b + 1, 0)

                def decays(i):
                    n = TB * b + i
                    hold(pool, "pool", S["adt"], b + 1 + START)
                    hold(pool, "pool", S["seg"], n + START)
                    nc.gpsimd.tensor_tensor(AU, le.unsqueeze(1).to_broadcast([P, NH, P]),
                                            adt3[:, i, :].unsqueeze(2).to_broadcast([P, NH, P]), ALU.mult)\
                        .then_inc(S["au"], 1)

                decays(0)
                for i in range(TB):
                    n = TB * b + i
                    hold(pool, "pool", S["xte"], n + 1 + START)
                    hold(pool, "pool", S["st"], n + START)
                    nc.gpsimd.tensor_tensor(heads(xdisc), heads(xa[:, i, :]),
                                            dtv3[:, i, :].unsqueeze(2).to_broadcast([P, NH, HD]), ALU.mult)\
                        .then_inc(S["xd1"], 1)
                    hold(pool, "pool", S["xd1"], n + 1)
                    hold(pool, "pool", S["es"], n + 1 + START)
                    nc.gpsimd.tensor_tensor(heads(xdec), heads(xdisc),
                                            es[:, i, NH:2 * NH].unsqueeze(2).to_broadcast([P, NH, HD]), ALU.mult)\
                        .then_inc(S["xd"], 1)
                    if i + 1 < TB:
                        decays(i + 1)
                        if with_next:
                            return_pool(pool, b + 1, i + 1)

            with pool.Fori(0, BATCH - 1) as b:
                row(b, True)
            row(BATCH - 1, False)

        def heads(ap):
            return ap.rearrange("p (h c) -> p h c", h=NH)

        dtv3 = dtv.rearrange("p (i h) -> p i h", i=TB)
        adt3 = dsel.rearrange("p (i h) -> p i h", i=TB)

        def ssm_tensor(pe):
            def row(b, with_next):
                hold(pe, "pe", ln["row"], KC * (b + 1))
                for c in range(CH):
                    pe.wait_ge(S["brc"], CH * b + START)
                    for k in range(KC):
                        last = nc.tensor.matmul(bank[c][:], w_in[:, k, c * P:(c + 1) * P],
                                                xnT[:, k, row_tokens(b)], start=(k == 0), stop=(k == KC - 1))
                    last.then_inc(S["br"], 1)
                pe.wait_ge(S["xb"], b + 1 + START)
                for i in range(TB):
                    n = TB * b + i
                    pe.wait_ge(S["zs"], TB * b + max(0, i - 1) + START)
                    for k in range(KC):
                        last = nc.tensor.matmul(bank[4 + i % 2][:], xb[:, k, i * P:(i + 1) * P],
                                                w_in[:, k, DIN:2 * DIN], start=(k == 0), stop=(k == KC - 1))
                    last.then_inc(S["z"], 1)
                    pe.wait_ge(S["bcde"], TB * b + max(0, i - 1) + START)
                    for k in range(KC):
                        last = nc.tensor.matmul(bank[6 + i % 2][:, 0:BCD], xb[:, k, i * P:(i + 1) * P],
                                                w_in[:, k, 2 * DIN:PROJ], start=(k == 0), stop=(k == KC - 1))
                    last.then_inc(S["bcd"], 1)
                def part1(i):
                    n = TB * b + i
                    if i == 0:
                        pe.wait_ge(S["bcde"], TB * (b + 1) + START)
                        pe.wait_ge(S["zs"], TB * (b + 1) + START)
                    hold(pe, "pe", S["act"], CH * b + CH + START)
                    hold(pe, "pe", S["yte"], n - min(i, 1) + START)
                    for c in range(CH):
                        last = nc.tensor.transpose(bank[6][:, c * P:(c + 1) * P], xact[:, c, i * P:(i + 1) * P], ident)
                    last.then_inc(S["xt"], 1)
                    hold(pe, "pe", S["gm"], n + START)
                    for m in range(2):
                        last = nc.tensor.transpose(bank[0][0:DST, m * P:(m + 1) * P],
                                                   bcd[:, i, m * DST:(m + 1) * DST], ident)
                    last.then_inc(S["bct"], 1)
                    pe.wait_ge(S["adt"], b + 1 + START)
                    pe.wait_ge(S["res"], n - min(i, 1) + START)
                    for m, w in enumerate((le, gt, ones[:])):
                        last = nc.tensor.matmul(bank[7][:, m * NH:(m + 1) * NH], w, adt3[:, i, :],
                                                start=True, stop=True)
                    last.then_inc(S["cum"], 1)
                    pe.wait_ge(S["au"], n + 1 + START)
                    pe.wait_ge(S["lt"], 2 * n + START)
                    for m in range(2):
                        last = nc.tensor.matmul(bank[1 + m][:], gt, AU[:, 4 * m:4 * m + 4, :]
                                                .rearrange("p h l -> p (h l)"), start=True, stop=True)
                    last.then_inc(S["seg"], 1)
                    pe.wait_ge(S["bcte"], n + 1 + START)
                    nc.tensor.matmul(bank[0][:, 0:P], BCT[:, 0, :], BCT[:, 1, :], start=True, stop=True)\
                        .then_inc(S["g"], 1)

                def part2(i):
                    n = TB * b + i
                    pe.wait_ge(S["st"], n + START)
                    if i:
                        nc.tensor.matmul(bank[4][:], BCT[:, 1, :], state, start=True, stop=True).then_inc(S["yo"], 1)
                    pe.wait_ge(S["xd"], n + 1)
                    nc.tensor.matmul(bank[5][0:DST, :], bcd[:, i, 0:DST], xdec, start=True, stop=True)\
                        .then_inc(S["st0"], 1)
                    pe.wait_ge(S["y2"], n + START)
                    pe.wait_ge(S["mt"], n + 1 + START)
                    for h in range(NH):
                        last = nc.tensor.matmul(bank[3][:, h * HD:(h + 1) * HD], LT[:, h * P:(h + 1) * P],
                                                xdisc[:, h * HD:(h + 1) * HD], start=True, stop=True)
                    last.then_inc(S["y1"], 1)

                def part3(i):
                    n = TB * b + i
                    hold(pe, "pe", S["y4"], n + 1 + START)
                    hold(pe, "pe", S["xte"], TB * b + min(TB, i + 2) + START)
                    hold(pe, "pe", S["yte"], n + START)
                    for c in range(CH):
                        last = nc.tensor.transpose(bank[6][:, c * P:(c + 1) * P], ya[:, c * P:(c + 1) * P], ident)
                    last.then_inc(S["yt"], 1)
                    pe.wait_ge(S["yte"], n + 1 + START)
                    pe.wait_ge(S["es"], TB * b + min(TB, i + 2) + START)
                    for c in range(CH):
                        last = nc.tensor.matmul(bank[7][:, 0:DIM], yT[:, c, :], w_out[:, c, :],
                                                start=(c == 0), stop=(c == CH - 1))
                    last.then_inc(S["out"], 1)

                part1(0)
                for i in range(TB):
                    part2(i)
                    if i + 1 < TB:
                        part1(i + 1)
                    elif with_next:
                        lnr_tensor(pe, b + 1)
                    part3(i)

            with pe.Fori(0, BATCH - 1) as b:
                row(b, True)
            row(BATCH - 1, False)

        def ssm_scalar(act):
            def row(b, with_next):
                for c in range(CH):
                    hold(act, "act", S["br"], CH * b + c + 1 + START)
                    hold(act, "act", S["conv"], CH * b + START)
                    nc.scalar.copy(xpad[:, c, TAPS - 1:SEQ + TAPS - 1], bank[c][:]).then_inc(S["brc"], 1)
                for i in range(TB):
                    act.wait_ge(S["z"], TB * b + i + 1)
                    nc.scalar.activation(zs[:, i, :], bank[4 + i % 2][:], ACT.Silu).then_inc(S["zs"], 1)
                for c in range(CH):
                    act.wait_ge(S["conv"], CH * b + c + 1 + START)
                    nc.scalar.activation(xact[:, c, :], cv[:, c, :], ACT.Silu, bias=conv_b[:, c:c + 1])\
                        .then_inc(S["act"], 1)
                act.wait_ge(S["d1"], b + 1)
                nc.scalar.activation(dexp, dmin, ACT.Exp).then_inc(S["dexp"], 1)
                act.wait_ge(S["d2"], b + 1)
                nc.scalar.activation(dln, dw, ACT.Ln).then_inc(S["dln"], 1)

                def part1(i):
                    n = TB * b + i
                    act.wait_ge(S["xt"], n + 1 + START)
                    nc.scalar.copy(xa[:, i, :], bank[6][:]).then_inc(S["xte"], 1)
                    act.wait_ge(S["bct"], n + 1 + START)
                    nc.scalar.copy(BCT.rearrange("p m l -> p (m l)"), bank[0][0:DST, 0:2 * P]).then_inc(S["bcte"], 1)
                    act.wait_ge(S["cum"], n + 1 + START)
                    nc.scalar.activation(es[:, i, :], bank[7][:, 0:3 * NH], ACT.Exp).then_inc(S["es"], 1)
                    act.wait_ge(S["seg"], n + 1 + START)
                    act.wait_ge(S["y1"], n + START)
                    for m in range(2):
                        nc.scalar.activation(LT[:, m * 4 * P:(m + 1) * 4 * P], bank[1 + m][:], ACT.Exp)\
                            .then_inc(S["lt"], 1)

                part1(0)
                for i in range(TB):
                    if i + 1 < TB:
                        part1(i + 1)
                    elif with_next:
                        lnr_root(act, b + 1)
                        lnr_evacuate(act, nc.scalar.copy, b + 1, 0)
                    act.wait_ge(S["yt"], TB * b + i + 1 + START)
                    nc.scalar.copy(yT.rearrange("p c l -> p (c l)"), bank[6][:]).then_inc(S["yte"], 1)

            with act.Fori(0, BATCH - 1) as b:
                row(b, True)
            row(BATCH - 1, False)

        def ssm_vector(dve):
            dve.wait_ge(S["aneg"], 1)
            nc.vector.tensor_scalar(a_neg[:], a_neg[:], -1.0, None, ALU.mult).then_inc(S["aneg"], 1)
            dve.wait_ge(S["aneg"], 2)
            dve.wait_ge(S["pad"], CH)
            def row(b, with_next):
                for c in range(CH):
                    dve.wait_ge(S["brc"], CH * b + c + 1 + START)
                    dve.wait_ge(S["act"], CH * b + START)
                    nc.vector.tensor_scalar(cv[:, c, :], xpad[:, c, 0:SEQ], conv_w[:, c, 0:1], None, ALU.mult)\
                        .then_inc(S["tap"], 1)

                def tap(m):
                    for c in range(CH):
                        dve.wait_ge(S["tap"], (TAPS - 1) * CH * b + CH * (m - 1) + c + 1)
                        ins = nc.vector.scalar_tensor_tensor(out=cv[:, c, :], in0=xpad[:, c, m:m + SEQ],
                                                             scalar=conv_w[:, c, m:m + 1], in1=cv[:, c, :],
                                                             op0=ALU.mult, op1=ALU.add)
                        ins.then_inc(S["tap"] if m < TAPS - 1 else S["conv"], 1)

                def take_bcd(i):
                    dve.wait_ge(S["bcd"], TB * b + i + 1)
                    nc.vector.tensor_copy(bcd[:, i, :], bank[6 + i % 2][:, 0:BCD]).then_inc(S["bcde"], 1)

                tap(1)
                take_bcd(0)
                take_bcd(1)
                tap(2)
                take_bcd(2)
                take_bcd(3)
                dve.wait_ge(S["bcde"], TB * (b + 1) + START)
                nc.vector.tensor_tensor(draw.rearrange("p (i h) -> p i h", i=TB), bcd[:, :, 2 * DST:BCD],
                                        dt_bias[:].unsqueeze(1).to_broadcast([P, TB, NH]), ALU.add)\
                    .then_inc(S["d3"], 1)
                dve.wait_ge(S["d3"], 5 * b + 1)
                nc.vector.scalar_tensor_tensor(out=dmin, in0=draw, scalar=-1.0, in1=draw,
                                               op0=ALU.mult, op1=ALU.min).then_inc(S["d1"], 1)
                nc.vector.tensor_scalar(dpos, draw, 0.0, None, ALU.max).then_inc(S["d3"], 1)
                tap(3)
                dve.wait_ge(S["dexp"], b + 1)
                nc.vector.tensor_scalar(dw, dexp, 1.0, None, ALU.add).then_inc(S["d2"], 1)
                dve.wait_ge(S["d2"], b + 1)
                nc.vector.tensor_scalar(dmin, dw, -1.0, 1e-30, ALU.add, ALU.max).then_inc(S["d4"], 1)
                dve.wait_ge(S["d4"], 4 * b + 1)
                nc.vector.reciprocal(dmin, dmin).then_inc(S["d4"], 1)
                dve.wait_ge(S["d4"], 4 * b + 2)
                nc.vector.tensor_tensor(dmin, dmin, dexp, ALU.mult).then_inc(S["d4"], 1)
                dve.wait_ge(S["dln"], b + 1)
                dve.wait_ge(S["d4"], 4 * b + 3)
                nc.vector.tensor_tensor(dmin, dmin, dln, ALU.mult).then_inc(S["d4"], 1)
                nc.vector.scalar_tensor_tensor(out=draw, in0=dw, scalar=1.0, in1=dexp,
                                               op0=ALU.is_equal, op1=ALU.mult).then_inc(S["d3"], 1)
                dve.wait_ge(S["d4"], 4 * b + 4)
                dve.wait_ge(S["d3"], 5 * b + 2)
                nc.vector.tensor_tensor(dpos, dpos, dmin, ALU.add).then_inc(S["d3"], 1)
                dve.wait_ge(S["d3"], 5 * b + 4)
                nc.vector.tensor_tensor(dtv, dpos, draw, ALU.add).then_inc(S["d3"], 1)
                dve.wait_ge(S["d3"], 5 * b + 5)
                nc.vector.tensor_tensor(adt3, dtv3, a_neg[:].unsqueeze(1).to_broadcast([P, TB, NH]), ALU.mult)\
                    .then_inc(S["adt"], 1)

                def decays(i):
                    n = TB * b + i
                    dve.wait_ge(S["g"], n + 1)
                    nc.vector.tensor_tensor(Gm, bank[0][:, 0:P], le, ALU.mult).then_inc(S["gm"], 1)
                    dve.wait_ge(S["lt"], 2 * n + 2 + START)
                    dve.wait_ge(S["gm"], n + 1 + START)
                    lt3 = LT.rearrange("p (h l) -> p h l", h=NH)
                    nc.vector.tensor_tensor(lt3, lt3, Gm.unsqueeze(1).to_broadcast([P, NH, P]), ALU.mult)\
                        .then_inc(S["mt"], 1)

                def outputs(i):
                    n = TB * b + i
                    dve.wait_ge(S["st0"], n + 1)
                    if i:
                        dve.wait_ge(S["yo"], (TB - 1) * b + i + START)
                        nc.vector.tensor_tensor(heads(state), heads(state),
                                                es[0:DST, i, 2 * NH:3 * NH].unsqueeze(2).to_broadcast([DST, NH, HD]),
                                                ALU.mult).then_inc(S["tap2"], 1)
                        dve.wait_ge(S["tap2"], (TB - 1) * b + i)
                        nc.vector.tensor_tensor(state, state, bank[5][0:DST, :], ALU.add).then_inc(S["st"], 1)
                    else:
                        nc.vector.tensor_copy(state, bank[5][0:DST, :]).then_inc(S["st"], 1)
                    dve.wait_ge(S["xte"], n + 1 + START)
                    hold(dve, "dve", S["yt"], n + START)
                    nc.vector.tensor_tensor(ya, xa[:, i, :], dskip[:], ALU.mult).then_inc(S["y3"], 1)
                    if i:
                        dve.wait_ge(S["es"], n + 1 + START)
                        nc.vector.tensor_tensor(heads(yb), heads(bank[4][:]),
                                                es[:, i, 0:NH].unsqueeze(2).to_broadcast([P, NH, HD]), ALU.mult)\
                            .then_inc(S["y3"], 1)
                        dve.wait_ge(S["y3"], YC * b + 3 * i + 0)
                        nc.vector.tensor_tensor(ya, ya, yb, ALU.add).then_inc(S["y3"], 1)
                    dve.wait_ge(S["y1"], n + 1 + START)
                    dve.wait_ge(S["y3"], YC * b + 3 * i + 1)
                    nc.vector.tensor_tensor(ya, ya, bank[3][:], ALU.add).then_inc(S["y2"], 1)
                    dve.wait_ge(S["y2"], n + 1 + START)
                    nc.vector.tensor_tensor(ya, ya, zs[:, i, :], ALU.mult).then_inc(S["y4"], 1)

                def residual(i):
                    n = TB * b + i
                    dve.wait_ge(S["out"], n + 1 + START)
                    xt = row_of_x(b * TB + i)
                    nc.vector.tensor_tensor(xt, bank[7][:, 0:DIM], xt, ALU.add).then_inc(S["res"], 1)

                if with_next:
                    return_vector(dve, b + 1, 0)
                decays(0)
                for i in range(TB):
                    if with_next and i == TB - 1:
                        lnr_apply(dve, b + 1)
                    outputs(i)
                    if i + 1 < TB:
                        decays(i + 1)
                    elif with_next:
                        lnr_evacuate(dve, nc.vector.tensor_copy, b + 1, 1)
                    if with_next and i + 1 < TB:
                        return_vector(dve, b + 1, i + 1)
                    if with_next and i == TB - 2:
                        lnr_stats(dve, b + 1)
                    residual(i)

            with dve.Fori(0, BATCH - 1) as b:
                row(b, True)
            row(BATCH - 1, False)

        YC = 1 + 3 * (TB - 1)
        S["tap2"] = sem("s_tap2")

        F = {k: sem(f"f_{k}") for k in ("gate", "up", "sil", "hid", "down", "sc", "res")}
        FCREDIT = ("hid", "down", "res", "sil")
        NF = len(FF_CHUNKS)

        def ff_tensor(pe):
            with pe.Fori(0, BATCH) as g:
                for c, (lo, w) in enumerate(FF_CHUNKS):
                    hold(pe, "pe", F["hid"], NF * g + max(0, c - 1) + START)
                    for k in range(KC):
                        last = nc.tensor.matmul(bank[c % 2][0:w, :], fgT[:, k, lo:lo + w],
                                                xnT[:, k, bass.ds(g * SEQ, SEQ)], start=(k == 0), stop=(k == KC - 1))
                    last.then_inc(F["gate"], 1)
                    for k in range(KC):
                        last = nc.tensor.matmul(bank[2 + c % 2][0:w, :], fuT[:, k, lo:lo + w],
                                                xnT[:, k, bass.ds(g * SEQ, SEQ)], start=(k == 0), stop=(k == KC - 1))
                    last.then_inc(F["up"], 1)
                for i in range(TB):
                    pe.wait_ge(F["hid"], NF * g + NF + START)
                    pe.wait_ge(F["res"], TB * g + START)
                    for c, (lo, w) in enumerate(FF_CHUNKS):
                        last = nc.tensor.matmul(bank[4 + i][:, 0:DIM], fhid[0:w, c, i * P:(i + 1) * P],
                                                fdT[0:w, c, :], start=(c == 0), stop=(c == NF - 1))
                    last.then_inc(F["down"], 1)

        def ff_scalar(act):
            with act.Fori(0, BATCH) as g:
                for c, (lo, w) in enumerate(FF_CHUNKS):
                    act.wait_ge(F["gate"], NF * g + c + 1)
                    act.wait_ge(F["hid"], NF * g + max(0, c - 1) + START)
                    nc.scalar.activation(fsl[0:w, c % 2, :], bank[c % 2][0:w, :], ACT.Silu,
                                         scale=gate_s[0:w, c:c + 1]).then_inc(F["sil"], 1)

        def ff_vector(dve):
            with dve.Fori(0, BATCH) as g:
                for c, (lo, w) in enumerate(FF_CHUNKS):
                    dve.wait_ge(F["up"], NF * g + c + 1)
                    dve.wait_ge(F["sil"], NF * g + c + 1 + START)
                    dve.wait_ge(F["down"], TB * g + START)
                    nc.vector.scalar_tensor_tensor(out=fhid[0:w, c, :], in0=bank[2 + c % 2][0:w, :],
                                                   scalar=up_s[0:w, c:c + 1], in1=fsl[0:w, c % 2, :],
                                                   op0=ALU.mult, op1=ALU.mult).then_inc(F["hid"], 1)
                for i in range(TB):
                    dve.wait_ge(F["down"], TB * g + i + 1 + START)
                    dve.wait_ge(F["res"], TB * g + max(0, i - 1) + START)
                    nc.vector.tensor_tensor(fo[:, i % 2, :], bank[4 + i][:, 0:DIM], down_s[:], ALU.mult)\
                        .then_inc(F["sc"], 1)
                    dve.wait_ge(F["sc"], TB * g + i + 1)
                    xt = x[:, bass.ds(g * TB + i, 1), :].rearrange("p o c -> p (o c)")
                    nc.vector.tensor_tensor(xt, fo[:, i % 2, :], xt, ALU.add).then_inc(F["res"], 1)

        @block.sync
        def _(sp):
            issue_loads(sp)
            assert n_load == total_loads, n_load
            sp.wait_ge(M["zero"], 1)
            per = MAX_TILES * ROWS // P // ZERO_PARTS
            for n in range(ZERO_PARTS):
                sp.dma_start(sent[n * per * P:(n + 1) * per * P, :].rearrange("(p r) c -> p r c", r=per),
                             zeros[:].unsqueeze(1).to_broadcast([P, per, DIM])).then_inc(M["zero"], 16)
            experts_sp(sp)
            for g in range(BATCH):
                sp.wait_ge(F["res"], TB * (g + 1) + START)
                sp.dma_start(out[g * SEQ:(g + 1) * SEQ, :].rearrange("(t p) c -> p t c", p=P),
                             x[:, TB * g:TB * (g + 1), :]).then_inc(loads["out"], 16)
            sp.wait_ge(loads["out"], 16 * BATCH)

        @block.gpsimd
        def _(pool):
            for s in [A[k] for k in ("res", "qs", "qte", "ote")] + [M[k] for k in MCREDIT]:
                pool.sem_inc(s, START)
            for s in [S[k] for k in SCREDIT] + [F[k] for k in FCREDIT]:
                pool.sem_inc(s, START)
            for s in stored:
                pool.sem_inc(s, 16)
            nc.gpsimd.memset(zeros[:], 0.0).then_inc(M["zero"], 1)
            nc.gpsimd.memset(ones[:], 1.0).then_inc(consts, 1)
            loaded(pool, "tables")
            nc.gpsimd.tensor_copy(identb[:], ident).then_inc(consts, 1)
            nc.gpsimd.tensor_copy(futureb[:], future).then_inc(consts, 1)
            stage_end(pool, 0)
            stage_end(pool, 1)
            stage_start(pool, 2)
            att_pool(pool)
            stage_end(pool, 2)
            stage_end(pool, 3)
            stage_start(pool, 4)
            send_pool(pool)
            pool.wait_ge(M["out"], 1)
            row_tables(pool, 0)
            for i in range(TB):
                return_pool(pool, 0, i)
            stage_end(pool, 4)
            stage_end(pool, 5)
            stage_start(pool, 6)
            ssm_pool(pool)
            stage_end(pool, 6)
            stage_end(pool, 7)
            stage_end(pool, 8)

        @block.scalar
        def _(act):
            prep_scalar(act)
            loaded(act, "attn")
            stage_end(act, 0)
            stage_start(act, 1)
            ln_scalar(act, 0)
            stage_end(act, 1)
            stage_start(act, 2)
            att_scalar(act)
            stage_end(act, 2)
            stage_start(act, 3)
            ln_scalar(act, 1)
            stage_end(act, 3)
            stage_start(act, 4)
            route_scalar(act)
            shared_scalar(act)
            experts_scalar(act)
            stage_end(act, 4)
            stage_start(act, 5)
            lnr_root(act, 0)
            lnr_evacuate(act, nc.scalar.copy, 0, 0)
            loaded(act, "mamba")
            nc.scalar.activation(a_neg[:], a_log[:], ACT.Exp).then_inc(S["aneg"], 1)
            stage_end(act, 5)
            stage_start(act, 6)
            ssm_scalar(act)
            stage_end(act, 6)
            stage_start(act, 7)
            ln_scalar(act, 3)
            loaded(act, "ffn1")
            stage_end(act, 7)
            stage_start(act, 8)
            ff_scalar(act)
            stage_end(act, 8)

        @block.vector
        def _(dve):
            loaded(dve, "x")
            ln_stats(dve, 0)
            stage_end(dve, 0)
            stage_start(dve, 1)
            ln_vector(dve, 0)
            stage_end(dve, 1)
            stage_start(dve, 2)
            att_vector(dve)
            stage_end(dve, 2)
            stage_start(dve, 3)
            ln_stats(dve, 1)
            ln_vector(dve, 1)
            stage_end(dve, 3)
            stage_start(dve, 4)
            route_vector(dve)
            shared_vector(dve)
            experts_vector(dve)
            dve.wait_ge(M["sacc"], TILES + START)
            for i in range(TB):
                return_vector(dve, 0, i)
            stage_end(dve, 4)
            stage_start(dve, 5)
            lnr_stats(dve, 0)
            lnr_apply(dve, 0)
            lnr_evacuate(dve, nc.vector.tensor_copy, 0, 1)
            stage_end(dve, 5)
            stage_start(dve, 6)
            loaded(dve, "mamba")
            ssm_vector(dve)
            stage_end(dve, 6)
            stage_start(dve, 7)
            ln_stats(dve, 3)
            ln_vector(dve, 3)
            stage_end(dve, 7)
            stage_start(dve, 8)
            loaded(dve, "ffn1")
            ff_vector(dve)
            stage_end(dve, 8)

        @block.tensor
        def _(pe):
            prep_tensor(pe)
            stage_end(pe, 0)
            stage_start(pe, 1)
            loaded(pe, "tables")
            ln_tensor(pe, 0)
            stage_end(pe, 1)
            stage_start(pe, 2)
            att_tensor(pe)
            stage_end(pe, 2)
            stage_start(pe, 3)
            ln_tensor(pe, 1)
            stage_end(pe, 3)
            stage_start(pe, 4)
            loaded(pe, "ffn0")
            route_tensor(pe)
            pe.wait_ge(M["trips"], 1)
            shared_tensor(pe)
            experts_tensor(pe)
            stage_end(pe, 4)
            stage_start(pe, 5)
            lnr_tensor(pe, 0)
            stage_end(pe, 5)
            stage_start(pe, 6)
            loaded(pe, "mamba")
            ssm_tensor(pe)
            stage_end(pe, 6)
            stage_start(pe, 7)
            ln_tensor(pe, 3)
            stage_end(pe, 7)
            stage_start(pe, 8)
            loaded(pe, "ffn1")
            ff_tensor(pe)
            stage_end(pe, 8)


def shape_tables():
    r = np.arange(P)
    ident = np.eye(P, dtype=np.float32)
    future = np.where(r[None, :] > r[:, None], -1e30, 0.0)
    le = (r[:, None] <= r[None, :]).astype(np.float32)
    gt = (r[:, None] > r[None, :]).astype(np.float32)
    f = np.float32
    pos2 = np.arange(0, DR, 2, dtype=f)
    inv = f(1.0) / np.power(f(10000.0), pos2 / f(DR)).astype(f)
    wavelen = f(2.0 * np.pi) / inv
    ramp = np.clip((f(1024) / wavelen - f(1.0)) / f(3.0), f(0), f(1)).astype(f)
    inv = (inv * (f(1.0) - ramp) + inv / f(16.0) * ramp).astype(f)
    freqs = np.outer(np.arange(SEQ, dtype=f), inv).astype(f)
    emb = np.concatenate([freqs, freqs], axis=-1)
    factor = f(0.1 * math.log(16.0) + 1.0)
    cos, sin = np.cos(emb) * factor, np.sin(emb) * factor
    sin[:, :DR // 2] *= -1
    tok = [t.reshape(TB, P, DR).transpose(1, 0, 2).reshape(P, TB * DR) for t in (cos, sin)]
    feat = [np.concatenate([np.zeros((KVL, SEQ)), t.T], axis=0) for t in (cos, sin)]
    marks = [r[:, None]] + [np.tile(ROWS * np.arange(1, TOKENS // ROWS), (P, 1)),
                            np.tile(LOOP_TILES * np.arange(MAX_TILES // LOOP_TILES), (P, 1))]
    return np.concatenate([ident, future, le, gt, *tok, *feat, *marks], axis=1).astype(f)


def lay_out(i):
    c = np.ascontiguousarray
    w_qb = i["L0_attn_w_qb"].reshape(QL, HEADS, DN + DR)
    w_kvb = i["L0_attn_w_kvb"].reshape(KVL, HEADS, 2, DN)
    w_qa, w_kva = i["L0_attn_w_qa"], i["L0_attn_w_kva"]
    kr = w_kva[:, KVL:]
    w_a = np.concatenate([w_qa, kr[:, DR // 2:], kr[:, :DR // 2], w_kva], axis=1)
    columns = lambda v: c(np.pad(v, (0, P * len(FF_CHUNKS) - INTER)).reshape(len(FF_CHUNKS), P).T)
    return {
        "x": c(i["L0_attn_x"].reshape(TOKENS, DIM)),
        "tables": shape_tables(),
        "w_qbT": c(w_qb[:, :, :DN].transpose(2, 1, 0)),
        "w_qr": c(w_qb[:, :, DN:]),
        "w_kvT": c(w_kvb.transpose(3, 2, 1, 0)),
        "w_o": c(i["L0_attn_w_o"]),
        "w_a": c(w_a.reshape(KC, P, 3 * P).transpose(1, 0, 2)),
        "q_norm": c(i["L0_attn_q_norm_w"]),
        "kv_norm": c(i["L0_attn_kv_norm_w"]),
        "gateT": c(i["L0_ffn_gate_w"].T),
        "w1T": c(i["L0_ffn_experts_w1"].transpose(0, 2, 1).reshape(EXPERTS, KC, P, EI).transpose(0, 2, 1, 3)
                 .reshape(EXPERTS, P, KC * EI)),
        "w2T": c(i["L0_ffn_experts_w2"].transpose(0, 2, 1).reshape(EXPERTS, 2, EH, DIM).transpose(0, 2, 1, 3)
                 .reshape(EXPERTS, EH, 2 * DIM)),
        "sguT": c(i["L0_ffn_shared_gate_up"].T),
        "sdT": c(i["L0_ffn_shared_down"].T),
        "w_in": c(i["L1_attn_in_proj_w"].T),
        "conv_w": c(i["L1_attn_conv_w"].reshape(DIN, TAPS)),
        "conv_b": c(i["L1_attn_conv_b"].reshape(CH, P).T),
        "w_out": c(i["L1_attn_out_proj_w"].T),
        "A_log": c(i["L1_attn_A_log"]),
        "dt_bias": c(i["L1_attn_dt_bias"]),
        "D_skip": c(i["L1_attn_D_skip"]),
        "fgT": c(i["L1_ffn_gate_w"].T),
        "fuT": c(i["L1_ffn_up_w"].T),
        "fdT": c(i["L1_ffn_down_w"].T),
        "gate_s": columns(i["L1_ffn_gate_s"]),
        "up_s": columns(i["L1_ffn_up_s"]),
        "down_s": c(i["L1_ffn_down_s"]),
    }


def kernel(**inputs):
    import concourse.bacc as bacc
    from concourse.bass_utils import run_bass_kernel_spmd

    nc = bacc.Bacc("TRN2", target_bir_lowering=False, num_devices=1)
    arrays = lay_out({k: np.asarray(v) for k, v in inputs.items()})
    args = {k: nc.dram_tensor(k + "_dram", v.shape, F32, kind="ExternalInput").ap() for k, v in arrays.items()}
    out = nc.dram_tensor("out_dram", (TOKENS, DIM), F32, kind="ExternalOutput").ap()
    build(nc, args, out)
    r = run_bass_kernel_spmd(nc, [{k + "_dram": v for k, v in arrays.items()}], core_ids=[0])
    return r.results[0]["out_dram"].reshape(BATCH, SEQ, DIM)
```
